# Optimizing a Trainium2 kernel written in Bass

```python
import numpy as np
import jax
import jax.numpy as jnp

def _softmax(x, axis=-1):
    return jax.nn.softmax(x, axis=axis)

def _gelu(x):
    return jax.nn.gelu(x, approximate=True)

def _silu(x):
    return jax.nn.silu(x)

def _sigmoid(x):
    return jax.nn.sigmoid(x)

def _layernorm(x, axis=-1, eps=1e-05):
    m = jnp.mean(x, axis=axis, keepdims=True)
    v = jnp.var(x, axis=axis, keepdims=True)
    return (x - m) / jnp.sqrt(v + eps)

def _scatter_add(tgt, idx, src, axis=0):
    return tgt.at[idx].add(src)

def _segment_sum(src, seg, n):
    return jax.ops.segment_sum(src, seg, n)
kernel_name = 'mk_adaln_d2_jaxref_r8_b51517'

def setup_inputs(seed: int=0):
    np.random.seed(seed)
    _w = jnp.asarray

    def _L0_attn_setup():
        import jax, jax.numpy as jnp
        import numpy as np
        D_MODEL = 128
        N_HEADS = 16
        HEAD_DIM = D_MODEL // N_HEADS
        NEG_INF = jnp.float32(-1e+30)

        def _alibi_causal_mask(S, dtype):
            q = jnp.arange(S)[:, None]
            k = jnp.arange(S)[None, :]
            return jnp.where(k <= q, -(q - k).astype(dtype), NEG_INF)
        key = jax.random.key(seed)
        ks = jax.random.split(key, 5)
        B, S, D = (4, 256, D_MODEL)
        scale = 1.0 / np.sqrt(D)
        x = jax.random.normal(ks[0], (B, S, D), dtype=jnp.float32)
        w_qkv = jax.random.normal(ks[1], (3 * D, D), dtype=jnp.float32) * scale
        b_qkv = jnp.zeros((3 * D,), dtype=jnp.float32)
        w_out = jax.random.normal(ks[2], (D, D), dtype=jnp.float32) * scale
        b_out = jnp.zeros((D,), dtype=jnp.float32)
        return {'x': x, 'w_qkv': w_qkv, 'b_qkv': b_qkv, 'w_out': w_out, 'b_out': b_out}
    _L0_attn_in = _L0_attn_setup()

    def _L0_ffn_setup():
        import jax, jax.numpy as jnp
        import numpy as np
        E = 8
        D = 128
        H = 256
        TOP_K = 2
        key = jax.random.key(seed)
        k_x, k_g, k_w1, k_w2 = jax.random.split(key, 4)
        B, S = (4, 256)
        inp = {'input': jax.random.normal(k_x, (B, S, D), dtype=jnp.float32), 'Wg': jax.random.normal(k_g, (D, E), dtype=jnp.float32) * 0.02, 'W1': jax.random.normal(k_w1, (E, D, H), dtype=jnp.float32) * 0.02, 'b1': jnp.zeros((E, H), dtype=jnp.float32), 'W2': jax.random.normal(k_w2, (E, H, D), dtype=jnp.float32) * 0.02, 'b2': jnp.zeros((E, D), dtype=jnp.float32)}
        return inp
    _L0_ffn_in = _L0_ffn_setup()
    _L0_c = _w((lambda *s: np.random.randn(*s).astype(np.float32) * 0.05)(4, 128))
    _L0_wmod = _w((lambda *s: np.random.randn(*s).astype(np.float32) * 0.05)(128, 6 * 128) * 128 ** (-0.5))

    def _L1_attn_setup():
        import jax, jax.numpy as jnp
        import numpy as np
        B, S, D, H = (4, 256, 128, 4)
        HD = D // H

        def _reference_tuple_inner(hidden_states, Wq, Wk, Wv, Wo, bo, betas, mem, z):
            b, s, d = hidden_states.shape
            h = betas.shape[1]
            hd = d // h

            def split(x):
                return x.reshape(b, s, h, hd).transpose(0, 2, 1, 3)
            q = split(hidden_states @ Wq.T)
            k = split(hidden_states @ Wk.T)
            v = split(hidden_states @ Wv.T)
            aw = jnp.einsum('bhqd,bhkd->bhqk', q, k)
            causal = jnp.tril(jnp.ones((s, s), bool))
            aw = jnp.where(causal, aw, jnp.finfo(aw.dtype).min)
            p = jax.nn.softmax(aw, axis=-1)
            attn = jnp.einsum('bhqk,bhkd->bhqd', p, v)
            sq = jax.nn.elu(q) + 1.0
            sk = jax.nn.elu(k) + 1.0
            A_mem = jnp.einsum('bhsd,hde->bhse', sq, mem) / (jnp.einsum('bhsd,hdo->bhso', sq, z) + 1e-06)
            g = jax.nn.sigmoid(betas)
            out = g * A_mem + (1.0 - g) * attn
            delta = jnp.einsum('bhsd,hde->bhse', sk, mem) / (jnp.einsum('bhsd,hdo->bhso', sk, z) + 1e-06)
            mem_new = mem + jnp.einsum('bhsd,bhse->hde', sk, v - delta) / b
            z_new = z + jnp.mean(jnp.sum(sk, axis=2), axis=0)[:, :, None]
            out = out.transpose(0, 2, 1, 3).reshape(b, s, d)
            out = out @ Wo.T + bo
            return (out, mem_new, z_new)
        key = jax.random.key(seed)
        ks = jax.random.split(key, 6)
        s = 0.02
        return {'hidden_states': jax.random.normal(ks[0], (B, S, D), jnp.float32), 'Wq': jax.random.normal(ks[1], (D, D), jnp.float32) * s, 'Wk': jax.random.normal(ks[2], (D, D), jnp.float32) * s, 'Wv': jax.random.normal(ks[3], (D, D), jnp.float32) * s, 'Wo': jax.random.normal(ks[4], (D, D), jnp.float32) * s, 'bo': jnp.zeros((D,), jnp.float32), 'betas': jax.random.normal(ks[5], (1, H, 1, 1), jnp.float32), 'mem': jnp.zeros((H, HD, HD), jnp.float32), 'z': jnp.zeros((H, HD, 1), jnp.float32)}
    _L1_attn_in = _L1_attn_setup()

    def _L1_ffn_setup():
        import jax, jax.numpy as jnp
        import numpy as np
        DIM = 128
        DEPTH = 6
        HEADS = 16
        DIM_HEAD = 64
        WINDOW = 32
        INNER = HEADS * DIM_HEAD
        DIM_INNER = int(DIM * 4 * 2 / 3)
        QK_SCALE = 8.0

        def shift_tokens(t):
            a, s = jnp.split(t, 2, -1)
            s = jnp.pad(s, ((0, 0), (1, 0), (0, 0)))[:, :-1]
            return jnp.concatenate([a, s], -1)

        def l2norm(t):
            return t / jnp.maximum(jnp.linalg.norm(t, axis=-1, keepdims=True), 1e-12)

        def rotate_half(x):
            x1, x2 = jnp.split(x, 2, -1)
            return jnp.concatenate([-x2, x1], -1)

        def rotary_tables(n):
            half = jnp.arange(0, DIM_HEAD, 2, dtype=jnp.float32)
            inv_freq = 1.0 / 10000.0 ** (half / DIM_HEAD)
            t = jnp.arange(n, dtype=jnp.float32)
            freqs = t[:, None] * inv_freq[None, :]
            freqs = jnp.concatenate([freqs, freqs], -1)
            base_scale = (half + 0.4 * DIM_HEAD) / (1.4 * DIM_HEAD)
            power = (t - n // 2) / (WINDOW // 2)
            scale = base_scale[None, :] ** power[:, None]
            scale = jnp.concatenate([scale, scale], -1)
            return (freqs, scale)

        def local_attention(q, k, v):
            b, h, n, d = q.shape
            w = WINDOW
            nw = n // w
            bq = q.reshape(b, h, nw, w, d)
            bk = k.reshape(b, h, nw, w, d)
            bv = v.reshape(b, h, nw, w, d)

            def look(t):
                p = jnp.pad(t, ((0, 0), (0, 0), (1, 0), (0, 0), (0, 0)))
                return jnp.concatenate([p[:, :, :nw], p[:, :, 1:]], axis=3)
            bk2, bv2 = (look(bk), look(bv))
            seq = jnp.arange(n).reshape(nw, w)
            seq_p = jnp.pad(seq, ((1, 0), (0, 0)), constant_values=-1)
            jt = jnp.concatenate([seq_p[:nw], seq_p[1:]], axis=1)
            it = seq[:, :, None]
            jb = jt[:, None, :]
            mask = (it < jb) | (it > jb + w) | (jb == -1)
            sim = jnp.einsum('bhwie,bhwje->bhwij', bq, bk2) * QK_SCALE
            sim = jnp.where(mask, -jnp.finfo(sim.dtype).max, sim)
            attn = jax.nn.softmax(sim, -1)
            out = jnp.einsum('bhwij,bhwje->bhwie', attn, bv2)
            return out.reshape(b, h, n, d)

        def attn_layer(x, Wqkv, qs, ksc, Wo):
            b, n, _ = x.shape
            qkv = x @ Wqkv
            q, k, v = jnp.split(qkv, 3, -1)
            sh = lambda t: t.reshape(b, n, HEADS, DIM_HEAD).transpose(0, 2, 1, 3)
            q, k, v = (sh(q), sh(k), sh(v))
            q = l2norm(q) * qs
            k = l2norm(k) * ksc
            freqs, scale = rotary_tables(n)
            cos, sin = (jnp.cos(freqs), jnp.sin(freqs))
            q = q * cos * scale + rotate_half(q) * sin * scale
            inv = 1.0 / scale
            k = k * cos * inv + rotate_half(k) * sin * inv
            out = local_attention(q, k, v)
            out = out.transpose(0, 2, 1, 3).reshape(b, n, INNER)
            return out @ Wo

        def ffn_layer(x, g, bln, W1, b1, W2, b2):
            mu = x.mean(-1, keepdims=True)
            var = ((x - mu) ** 2).mean(-1, keepdims=True)
            xn = (x - mu) / jnp.sqrt(var + 1e-05) * g + bln
            hg = xn @ W1 + b1
            a, gate = jnp.split(hg, 2, -1)
            return a * jax.nn.gelu(gate, approximate=False) @ W2 + b2
        key = jax.random.key(seed)
        ks = jax.random.split(key, 8)
        B, N = (2, 256)
        init = lambda k, shape: jax.random.normal(k, shape, jnp.float32) * 0.02
        return {'x': jax.random.normal(ks[0], (B, N, DIM), jnp.float32), 'Wqkv': init(ks[1], (DEPTH, DIM, 3 * INNER)), 'q_scale': jnp.ones((DEPTH, DIM_HEAD), jnp.float32), 'k_scale': jnp.ones((DEPTH, DIM_HEAD), jnp.float32), 'Wo': init(ks[2], (DEPTH, INNER, DIM)), 'ln_g': jnp.ones((DEPTH, DIM), jnp.float32), 'ln_b': jnp.zeros((DEPTH, DIM), jnp.float32), 'W1': init(ks[3], (DEPTH, DIM, 2 * DIM_INNER)), 'b1': jnp.zeros((DEPTH, 2 * DIM_INNER), jnp.float32), 'W2': init(ks[4], (DEPTH, DIM_INNER, DIM)), 'b2': jnp.zeros((DEPTH, DIM), jnp.float32)}
    _L1_ffn_in = _L1_ffn_setup()
    _L1_c = _w((lambda *s: np.random.randn(*s).astype(np.float32) * 0.05)(4, 128))
    _L1_wmod = _w((lambda *s: np.random.randn(*s).astype(np.float32) * 0.05)(128, 6 * 128) * 128 ** (-0.5))
    _d = {'L0_attn_x': _L0_attn_in['x'], 'L0_attn_w_qkv': _L0_attn_in['w_qkv'], 'L0_attn_b_qkv': _L0_attn_in['b_qkv'], 'L0_attn_w_out': _L0_attn_in['w_out'], 'L0_attn_b_out': _L0_attn_in['b_out'], 'L0_ffn_Wg': _L0_ffn_in['Wg'], 'L0_ffn_W1': _L0_ffn_in['W1'], 'L0_ffn_b1': _L0_ffn_in['b1'], 'L0_ffn_W2': _L0_ffn_in['W2'], 'L0_ffn_b2': _L0_ffn_in['b2'], 'L0_c': _L0_c, 'L0_wmod': _L0_wmod, 'L1_attn_Wq': _L1_attn_in['Wq'], 'L1_attn_Wk': _L1_attn_in['Wk'], 'L1_attn_Wv': _L1_attn_in['Wv'], 'L1_attn_Wo': _L1_attn_in['Wo'], 'L1_attn_bo': _L1_attn_in['bo'], 'L1_attn_betas': _L1_attn_in['betas'], 'L1_attn_mem': _L1_attn_in['mem'], 'L1_attn_z': _L1_attn_in['z'], 'L1_ffn_Wqkv': _L1_ffn_in['Wqkv'], 'L1_ffn_q_scale': _L1_ffn_in['q_scale'], 'L1_ffn_k_scale': _L1_ffn_in['k_scale'], 'L1_ffn_Wo': _L1_ffn_in['Wo'], 'L1_ffn_ln_g': _L1_ffn_in['ln_g'], 'L1_ffn_ln_b': _L1_ffn_in['ln_b'], 'L1_ffn_W1': _L1_ffn_in['W1'], 'L1_ffn_b1': _L1_ffn_in['b1'], 'L1_ffn_W2': _L1_ffn_in['W2'], 'L1_ffn_b2': _L1_ffn_in['b2'], 'L1_c': _L1_c, 'L1_wmod': _L1_wmod}
    _x0 = _d['L0_attn_x']
    _d['L0_attn_x'] = jax.random.normal(jax.random.fold_in(jax.random.key(seed), 1), (4, 512, 128), dtype=_x0.dtype)
    del _x0
    return _d

def reference(L0_attn_x, L0_attn_w_qkv, L0_attn_b_qkv, L0_attn_w_out, L0_attn_b_out, L0_ffn_Wg, L0_ffn_W1, L0_ffn_b1, L0_ffn_W2, L0_ffn_b2, L0_c, L0_wmod, L1_attn_Wq, L1_attn_Wk, L1_attn_Wv, L1_attn_Wo, L1_attn_bo, L1_attn_betas, L1_attn_mem, L1_attn_z, L1_ffn_Wqkv, L1_ffn_q_scale, L1_ffn_k_scale, L1_ffn_Wo, L1_ffn_ln_g, L1_ffn_ln_b, L1_ffn_W1, L1_ffn_b1, L1_ffn_W2, L1_ffn_b2, L1_c, L1_wmod):

    def _L0_attn_ref(x, w_qkv, b_qkv, w_out, b_out):
        import jax, jax.numpy as jnp
        import numpy as np
        D_MODEL = 128
        N_HEADS = 16
        HEAD_DIM = D_MODEL // N_HEADS
        NEG_INF = jnp.float32(-1e+30)

        def _alibi_causal_mask(S, dtype):
            q = jnp.arange(S)[:, None]
            k = jnp.arange(S)[None, :]
            return jnp.where(k <= q, -(q - k).astype(dtype), NEG_INF)
        B, S, D = x.shape
        H, hd = (N_HEADS, HEAD_DIM)
        qkv = x @ w_qkv.T + b_qkv
        q, k, v = jnp.split(qkv, 3, axis=-1)
        q = q.reshape(B, S, H, hd).transpose(0, 2, 1, 3)
        k = k.reshape(B, S, H, hd).transpose(0, 2, 1, 3)
        v = v.reshape(B, S, H, hd).transpose(0, 2, 1, 3)
        scores = jnp.einsum('bhqd,bhkd->bhqk', q, k) / np.sqrt(hd)
        scores = scores + _alibi_causal_mask(S, scores.dtype)
        probs = jax.nn.softmax(scores, axis=-1)
        out = jnp.einsum('bhqk,bhkd->bhqd', probs, v)
        out = out.transpose(0, 2, 1, 3).reshape(B, S, D)
        return out @ w_out.T + b_out

    def _L0_ffn_ref(input, Wg, W1, b1, W2, b2):
        import jax, jax.numpy as jnp
        import numpy as np
        E = 8
        D = 128
        H = 256
        TOP_K = 2
        logits = jnp.einsum('bsd,de->bse', input, Wg)
        probs = jax.nn.softmax(logits, axis=-1)
        top_vals, top_idx = jax.lax.top_k(probs, TOP_K)
        top_vals = top_vals / jnp.sum(top_vals, axis=-1, keepdims=True)
        onehot = jax.nn.one_hot(top_idx, E, dtype=input.dtype)
        mask = jnp.sum(onehot, axis=2)
        scores = jnp.sum(onehot * top_vals[..., None], axis=2)
        xm = input[None] * jnp.moveaxis(mask, -1, 0)[..., None]
        h = jnp.einsum('ebsd,edh->ebsh', xm, W1) + b1[:, None, None, :]
        h = jax.nn.relu(h)
        y = jnp.einsum('ebsh,ehd->ebsd', h, W2) + b2[:, None, None, :]
        out = jnp.sum(y * jnp.moveaxis(scores, -1, 0)[..., None], axis=0)
        return out

    def _L1_attn_ref(hidden_states, Wq, Wk, Wv, Wo, bo, betas, mem, z):
        import jax, jax.numpy as jnp
        import numpy as np
        B, S, D, H = (4, 256, 128, 4)
        HD = D // H

        def _reference_tuple_inner(hidden_states, Wq, Wk, Wv, Wo, bo, betas, mem, z):
            b, s, d = hidden_states.shape
            h = betas.shape[1]
            hd = d // h

            def split(x):
                return x.reshape(b, s, h, hd).transpose(0, 2, 1, 3)
            q = split(hidden_states @ Wq.T)
            k = split(hidden_states @ Wk.T)
            v = split(hidden_states @ Wv.T)
            aw = jnp.einsum('bhqd,bhkd->bhqk', q, k)
            causal = jnp.tril(jnp.ones((s, s), bool))
            aw = jnp.where(causal, aw, jnp.finfo(aw.dtype).min)
            p = jax.nn.softmax(aw, axis=-1)
            attn = jnp.einsum('bhqk,bhkd->bhqd', p, v)
            sq = jax.nn.elu(q) + 1.0
            sk = jax.nn.elu(k) + 1.0
            A_mem = jnp.einsum('bhsd,hde->bhse', sq, mem) / (jnp.einsum('bhsd,hdo->bhso', sq, z) + 1e-06)
            g = jax.nn.sigmoid(betas)
            out = g * A_mem + (1.0 - g) * attn
            delta = jnp.einsum('bhsd,hde->bhse', sk, mem) / (jnp.einsum('bhsd,hdo->bhso', sk, z) + 1e-06)
            mem_new = mem + jnp.einsum('bhsd,bhse->hde', sk, v - delta) / b
            z_new = z + jnp.mean(jnp.sum(sk, axis=2), axis=0)[:, :, None]
            out = out.transpose(0, 2, 1, 3).reshape(b, s, d)
            out = out @ Wo.T + bo
            return (out, mem_new, z_new)
        return _reference_tuple_inner(hidden_states, Wq, Wk, Wv, Wo, bo, betas, mem, z)[0]

    def _L1_ffn_ref(x, Wqkv, q_scale, k_scale, Wo, ln_g, ln_b, W1, b1, W2, b2):
        import jax, jax.numpy as jnp
        import numpy as np
        DIM = 128
        DEPTH = 6
        HEADS = 16
        DIM_HEAD = 64
        WINDOW = 32
        INNER = HEADS * DIM_HEAD
        DIM_INNER = int(DIM * 4 * 2 / 3)
        QK_SCALE = 8.0

        def shift_tokens(t):
            a, s = jnp.split(t, 2, -1)
            s = jnp.pad(s, ((0, 0), (1, 0), (0, 0)))[:, :-1]
            return jnp.concatenate([a, s], -1)

        def l2norm(t):
            return t / jnp.maximum(jnp.linalg.norm(t, axis=-1, keepdims=True), 1e-12)

        def rotate_half(x):
            x1, x2 = jnp.split(x, 2, -1)
            return jnp.concatenate([-x2, x1], -1)

        def rotary_tables(n):
            half = jnp.arange(0, DIM_HEAD, 2, dtype=jnp.float32)
            inv_freq = 1.0 / 10000.0 ** (half / DIM_HEAD)
            t = jnp.arange(n, dtype=jnp.float32)
            freqs = t[:, None] * inv_freq[None, :]
            freqs = jnp.concatenate([freqs, freqs], -1)
            base_scale = (half + 0.4 * DIM_HEAD) / (1.4 * DIM_HEAD)
            power = (t - n // 2) / (WINDOW // 2)
            scale = base_scale[None, :] ** power[:, None]
            scale = jnp.concatenate([scale, scale], -1)
            return (freqs, scale)

        def local_attention(q, k, v):
            b, h, n, d = q.shape
            w = WINDOW
            nw = n // w
            bq = q.reshape(b, h, nw, w, d)
            bk = k.reshape(b, h, nw, w, d)
            bv = v.reshape(b, h, nw, w, d)

            def look(t):
                p = jnp.pad(t, ((0, 0), (0, 0), (1, 0), (0, 0), (0, 0)))
                return jnp.concatenate([p[:, :, :nw], p[:, :, 1:]], axis=3)
            bk2, bv2 = (look(bk), look(bv))
            seq = jnp.arange(n).reshape(nw, w)
            seq_p = jnp.pad(seq, ((1, 0), (0, 0)), constant_values=-1)
            jt = jnp.concatenate([seq_p[:nw], seq_p[1:]], axis=1)
            it = seq[:, :, None]
            jb = jt[:, None, :]
            mask = (it < jb) | (it > jb + w) | (jb == -1)
            sim = jnp.einsum('bhwie,bhwje->bhwij', bq, bk2) * QK_SCALE
            sim = jnp.where(mask, -jnp.finfo(sim.dtype).max, sim)
            attn = jax.nn.softmax(sim, -1)
            out = jnp.einsum('bhwij,bhwje->bhwie', attn, bv2)
            return out.reshape(b, h, n, d)

        def attn_layer(x, Wqkv, qs, ksc, Wo):
            b, n, _ = x.shape
            qkv = x @ Wqkv
            q, k, v = jnp.split(qkv, 3, -1)
            sh = lambda t: t.reshape(b, n, HEADS, DIM_HEAD).transpose(0, 2, 1, 3)
            q, k, v = (sh(q), sh(k), sh(v))
            q = l2norm(q) * qs
            k = l2norm(k) * ksc
            freqs, scale = rotary_tables(n)
            cos, sin = (jnp.cos(freqs), jnp.sin(freqs))
            q = q * cos * scale + rotate_half(q) * sin * scale
            inv = 1.0 / scale
            k = k * cos * inv + rotate_half(k) * sin * inv
            out = local_attention(q, k, v)
            out = out.transpose(0, 2, 1, 3).reshape(b, n, INNER)
            return out @ Wo

        def ffn_layer(x, g, bln, W1, b1, W2, b2):
            mu = x.mean(-1, keepdims=True)
            var = ((x - mu) ** 2).mean(-1, keepdims=True)
            xn = (x - mu) / jnp.sqrt(var + 1e-05) * g + bln
            hg = xn @ W1 + b1
            a, gate = jnp.split(hg, 2, -1)
            return a * jax.nn.gelu(gate, approximate=False) @ W2 + b2
        for i in range(DEPTH):
            x = attn_layer(shift_tokens(x), Wqkv[i], q_scale[i], k_scale[i], Wo[i]) + x
            x = ffn_layer(shift_tokens(x), ln_g[i], ln_b[i], W1[i], b1[i], W2[i], b2[i]) + x
        return x
    x = L0_attn_x
    mod = (_silu(L0_c) @ L0_wmod).reshape(L0_c.shape[0], 6, 1, -1)
    sa, ca, ga, sb, cb, gb = (mod[:, 0], mod[:, 1], mod[:, 2], mod[:, 3], mod[:, 4], mod[:, 5])
    ga = (2 * (ga >= 0) - 1) * jnp.maximum(jnp.abs(ga), 0.25)
    gb = (2 * (gb >= 0) - 1) * jnp.maximum(jnp.abs(gb), 0.25)
    h = _layernorm(x, axis=-1) * (1 + ca) + sa
    x = x + ga * _L0_attn_ref(h, L0_attn_w_qkv, L0_attn_b_qkv, L0_attn_w_out, L0_attn_b_out)
    h = _layernorm(x, axis=-1) * (1 + cb) + sb
    x = x + gb * _L0_ffn_ref(h, L0_ffn_Wg, L0_ffn_W1, L0_ffn_b1, L0_ffn_W2, L0_ffn_b2)
    mod = (_silu(L1_c) @ L1_wmod).reshape(L1_c.shape[0], 6, 1, -1)
    sa, ca, ga, sb, cb, gb = (mod[:, 0], mod[:, 1], mod[:, 2], mod[:, 3], mod[:, 4], mod[:, 5])
    ga = (2 * (ga >= 0) - 1) * jnp.maximum(jnp.abs(ga), 0.25)
    gb = (2 * (gb >= 0) - 1) * jnp.maximum(jnp.abs(gb), 0.25)
    h = _layernorm(x, axis=-1) * (1 + ca) + sa
    x = x + ga * _L1_attn_ref(h, L1_attn_Wq, L1_attn_Wk, L1_attn_Wv, L1_attn_Wo, L1_attn_bo, L1_attn_betas, L1_attn_mem, L1_attn_z)
    h = _layernorm(x, axis=-1) * (1 + cb) + sb
    x = x + gb * _L1_ffn_ref(h, L1_ffn_Wqkv, L1_ffn_q_scale, L1_ffn_k_scale, L1_ffn_Wo, L1_ffn_ln_g, L1_ffn_ln_b, L1_ffn_W1, L1_ffn_b1, L1_ffn_W2, L1_ffn_b2)
    return x

_drawn_inputs = setup_inputs


def setup_inputs(seed=0):
    import zlib

    import numpy as np

    out = dict(_drawn_inputs(seed))
    spreads = {'L0_attn_b_qkv': (0.0, 0.1),
     'L0_attn_b_out': (0.0, 0.1),
     'L0_ffn_b1': (0.0, 0.1),
     'L0_ffn_b2': (0.0, 0.1),
     'L1_attn_bo': (0.0, 0.1),
     'L1_attn_mem': (0.0, 0.1),
     'L1_attn_z': (0.0, 0.1),
     'L1_ffn_q_scale': (1.0, 0.2),
     'L1_ffn_k_scale': (1.0, 0.2),
     'L1_ffn_ln_g': (1.0, 0.2),
     'L1_ffn_ln_b': (0.0, 0.1),
     'L1_ffn_b1': (0.0, 0.1),
     'L1_ffn_b2': (0.0, 0.1)}
    factors = {}
    for name, (base, spread) in spreads.items():
        noise = np.random.default_rng([zlib.crc32(name.encode()), seed]).standard_normal(out[name].shape)
        drawn = base * np.exp(spread * noise) if base else spread * noise
        out[name] = jnp.asarray(drawn.astype(out[name].dtype))
    for name, factor in factors.items():
        out[name] = (out[name] * factor).astype(out[name].dtype)
    return out
```

```python
import math
from contextlib import ExitStack

import numpy as np

import concourse.bass as bass
from concourse import mybir

F32 = mybir.dt.float32
BF16 = mybir.dt.bfloat16
ALU = mybir.AluOpType
ACT = mybir.ActivationFunctionType
AX = mybir.AxisListType

P = 128
B = 4
S = 512
T = S // P
EPS = 1e-5
BIG = -1e30

H0, D0 = 16, 8
NE, FH = 8, 256
H1, D1 = 4, 32
DEPTH, HL, DL, WIN = 6, 16, 64, 32
INNER = HL * DL
PAIRS = HL // 2
DI = int(P * 4 * 2 / 3)
CH = [(0, P), (P, P), (2 * P, DI - 2 * P)]
FFC = len(CH)
PADH = 32

NMOD = 12
SA, CA, GA, SB, CB, GB = range(6)


def shape_constants():
    f = np.float32
    p = np.arange(P)
    ident = np.eye(P, dtype=f)
    d = np.arange(S)[None, :] - (S - P + p)[:, None]
    alibi = np.where(d <= 0, d, BIG).astype(f)
    causal = np.where(d <= 0, 0.0, BIG).astype(f)
    hm0 = (p[:, None] // D0 == np.arange(H0)[None, :]).astype(f) / f(np.sqrt(D0))
    hm1 = (p[:, None] // D1 == np.arange(H1)[None, :]).astype(f)
    i = (p % WIN)[:, None]
    j = np.arange(2 * WIN)[None, :]
    ok = (i <= j) & (j <= i + WIN)
    first = ok & ~((p[:, None] < WIN) & (j < WIN))
    wmask = np.stack([np.where(ok, 0.0, BIG), np.where(first, 0.0, BIG)], 1).astype(f)
    half = np.arange(0, DL, 2, dtype=f)
    inv_freq = f(1.0) / f(10000.0) ** (half / f(DL))
    t = np.arange(S, dtype=f)
    fr = t[:, None] * inv_freq[None, :]
    fr = np.concatenate([fr, fr], -1)
    base = (half + f(0.4 * DL)) / f(1.4 * DL)
    power = (t - S // 2) / f(WIN // 2)
    sc = base[None, :] ** power[:, None]
    sc = np.concatenate([sc, sc], -1)
    sign = np.where(np.arange(DL) < DL // 2, -1.0, 1.0).astype(f)
    c, s = np.cos(fr), np.sin(fr) * sign
    inv = f(1.0) / sc
    rot = np.stack([c * sc, s * sc, c * inv, s * inv], 0)
    rot = rot.reshape(4, T, P, DL).transpose(2, 0, 1, 3).astype(f)
    rev = np.broadcast_to(np.arange(NE, 0, -1, dtype=f), (P, T, NE))
    return {
        "ident": ident, "alibi": alibi, "causal": causal, "hm0": hm0, "hm1": hm1,
        "wmask": wmask, "rot": np.ascontiguousarray(rot), "rev": np.ascontiguousarray(rev),
    }


class Chain:

    def __init__(self, eng, sem, base=0):
        self.eng, self.sem, self.base, self.n = eng, sem, base, 0

    def do(self, ins):
        self.mark(ins)
        self.settle()

    def mark(self, ins):
        ins.then_inc(self.sem, 1)
        self.n += 1

    def settle(self):
        self.eng.wait_ge(self.sem, self.base + self.n)


DVE_A, DVE_B = 40, 10




def build(nc, ins, out):
    ctx = ExitStack()
    with ctx:
        def sb(name, shape, dt=F32):
            return ctx.enter_context(nc.sbuf_tensor(name, shape, dt))

        def sem(name):
            return ctx.enter_context(nc.semaphore(name))

        ident = sb("ident", [P, P])
        identb = sb("identb", [P, P], BF16)
        alibi = sb("alibi", [P, S])
        causal = sb("causal", [P, S])
        hm = [sb("hm0", [P, H0]), sb("hm1", [P, H1])]
        wmask = sb("wmask", [P, 2, 2 * WIN])
        wmaskb = sb("wmaskb", [P, 2, 2 * WIN], BF16)
        rot = sb("rot", [P, 4, T, DL])
        rev = sb("rev", [P, T, NE])
        half_neg = sb("half_neg", [P, 32])
        wT = sb("wT", [P, 8, P])
        bqkv = sb("bqkv", [P, 3])
        bv = sb("bv", [P, P])
        bout = sb("bout", [P, 2])
        wg = sb("wg", [P, NE])
        mw1 = sb("mw1", [P, NE, FH])
        mw2 = sb("mw2", [P, NE, 2, P])
        mb1 = sb("mb1", [P, NE, 2])
        mb2 = sb("mb2", [NE, P])
        cT = sb("cT", [P, 2, B])
        cw = sb("cw", [P, 3, 2, B])
        modT = sb("modT", [P, B, NMOD])
        gsgn = sb("gsgn", [P, B, NMOD])
        gneg = sb("gneg", [P, B, NMOD])
        mcur = sb("mcur", [P, NMOD])
        memz = sb("memz", [P, P + H1])
        beta = sb("beta", [P, 3, H1])
        wqkv = sb("wqkv", [P, 3 * INNER])
        wo = sb("wo", [P, PAIRS, P])
        w1 = sb("w1", [P, 2 * DI])
        w2 = sb("w2", [P, FFC, P])
        qks = sb("qks", [P, 2, DEPTH, DL])
        lcol = sb("lcol", [P, DEPTH, 9])
        lcur = sb("lcur", [P, 9])
        rtab = sb("rtab", [P, 4, T, DL])
        XT = sb("XT", [P, B * S])
        YT = sb("YT", [P, B * S])
        xcur = sb("xcur", [P, S])
        hT = sb("hT", [P, S])
        xn = sb("xn", [P, T, P])
        stats = sb("stats", [P, T, 6])
        mv = sb("mv", [P, T, 2])
        rstd = sb("rstd", [P, T])
        tmp = sb("tmp", [P, S])

        ARENA = 30200
        arena = sb("arena", [P, ARENA])

        class Area:

            def __init__(self):
                self.at = 0

            def take(self, *shape, part=P):
                n = int(np.prod(shape))
                v = arena[0:part, self.at:self.at + n]
                self.at += n
                assert self.at <= ARENA, self.at
                if len(shape) == 2:
                    v = v.rearrange("p (a b) -> p a b", b=shape[1])
                if len(shape) == 3:
                    v = v.rearrange("p (a b c) -> p a b c", b=shape[1], c=shape[2])
                return v

        a = Area()
        xtok = a.take(T, P)
        Qm = a.take(2, S)
        qTs = a.take(S)
        kTs = a.take(S)
        Vh = a.take(T, H0, PADH)
        Ssb = a.take(2, S)
        Pr = a.take(4, S)
        PTh = a.take(2, T, S)
        nmax = a.take(H0 * T)
        rsum = a.take(H0, T)
        rinv = a.take(H0, T)
        OTs = a.take(S)
        Otok = a.take(T, P)
        Am = a.take(T, P)
        den = a.take(T, H1)
        oTs = a.take(S)
        sqT = a.take(S)
        eq_ = a.take(S)
        hes = a.take(2, 2, S)
        hsc = a.take(2, 2, S)
        setup = Area()
        setup.at = a.at - 8 * S
        wnat = setup.take(8, P)
        wmod = setup.take(2, 6 * P)
        rt = a.take(12, T * NE)
        rs4 = a.take(6, T)
        sT = a.take(S)

        a = Area()
        xsA = a.take(S)
        xsF = a.take(S)
        ra = a.take(2, INNER)
        rb = a.take(2, INNER)
        sq = a.take(2, S)
        ss = a.take(2, HL)
        rr = a.take(2, HL)
        Vt = a.take(2, INNER)
        Vp = a.take(2, INNER)
        qT = a.take(PAIRS, P)
        kT = a.take(PAIRS, WIN + S)
        Tm = a.take(HL, 2 * WIN)
        Ex = a.take(HL, 2 * WIN)
        mx = a.take(HL)
        sm = a.take(HL)
        ri = a.take(HL)
        Bd = a.take(HL, WIN + P)
        PT = a.take(HL, P)
        PTp = a.take(HL, WIN)
        oT = a.take(PAIRS, S)
        ge = a.take(FFC, S)
        fa = a.take(FFC, S)

        pj = ctx.enter_context(nc.psum_tensor("pj", [P, 2, S], F32))
        tr = ctx.enter_context(nc.psum_tensor("tr", [P, 2, S], F32))
        sc = ctx.enter_context(nc.psum_tensor("sc", [P, 2, S], F32))
        oo = ctx.enter_context(nc.psum_tensor("oo", [P, 2, S], F32))
        SBANK = [pj[:, 0], pj[:, 1], sc[:, 0]]
        TBANK = [tr[:, 0], tr[:, 1], sc[:, 1]]

        ld_const = sem("ld_const")
        ld_x = sem("ld_x")
        ld_qkv, ld_wo, ld_ff = sem("ld_qkv"), sem("ld_wo"), sem("ld_ff")
        ld_vp = sem("ld_vp")
        st_out = sem("st_out")
        dve_c, act_c, pool_c = sem("dve_c"), sem("act_c"), sem("pool_c")
        zeroed, passed = sem("zeroed"), sem("passed")
        set_tr = sem("set_tr")
        set_ev = sem("set_ev")
        silu_e, silu_d = sem("silu_e"), sem("silu_d")
        sig_e = sem("sig_e")
        x_tr, x_in = sem("x_tr"), sem("x_in")
        mod_cur = sem("mod_cur")
        ln_in, ln_var, ln_rstd, ln_norm, ln_back, ln_out = (
            sem("ln_in"), sem("ln_var"), sem("ln_rstd"), sem("ln_norm"), sem("ln_back"), sem("ln_out"))
        qk_mm, qk_ev, v_mm, v_ev = sem("qk_mm"), sem("qk_ev"), sem("v_mm"), sem("v_ev")
        q_masked = sem("q_masked")
        scores, biased, probs, p_tr, pe_dve, pe_act, pv_done = (
            sem("scores"), sem("biased"), sem("probs"), sem("p_tr"), sem("pe_dve"), sem("pe_act"),
            sem("pv_done"))
        o_copied, o_tr, o_tok = sem("o_copied"), sem("o_tr"), sem("o_tok")
        of_tr, of_ev, prj, x_add = sem("of_tr"), sem("of_ev"), sem("prj"), sem("x_add")
        elu_m, elu_e, elu_s, mem_mm, mixed = (
            sem("elu_m"), sem("elu_e"), sem("elu_s"), sem("mem_mm"), sem("mixed"))
        lg_mm, lg_sub, lg_exp, routed, s_tr, s_ev = (
            sem("lg_mm"), sem("lg_sub"), sem("lg_exp"), sem("routed"), sem("s_tr"), sem("s_ev"))
        m_h, m_relu, m_bc, m_sc, m_y = (
            sem("m_h"), sem("m_relu"), sem("m_bc"), sem("m_sc"), sem("m_y"))
        y_in = sem("y_in")
        xs_a, tabs = sem("xs_a"), sem("tabs")
        pj_mm, sq_ev, rot_ev, ss_ok, qk_rdy, v_cp = (
            sem("pj_mm"), sem("sq_ev"), sem("rot_ev"), sem("ss_ok"), sem("qk_rdy"), sem("v_cp"))
        qk_tr, qk_cp, sc_mm, t_sub, e_exp, bd_dve, bd_pool, ptp_ok, ri_ok = (
            sem("qk_tr"), sem("qk_cp"), sem("sc_mm"), sem("t_sub"), sem("e_exp"), sem("bd_dve"),
            sem("bd_pool"), sem("ptp_ok"), sem("ri_ok"))
        pt_tr, pt_cp, o_mm, o_cp, wo_mm, y_att, xs_f = (
            sem("pt_tr"), sem("pt_cp"), sem("o_mm"), sem("o_cp"), sem("wo_mm"), sem("y_att"), sem("xs_f"))
        w1_mm, gelu_ev, ff_ev, w2_mm, y_ff = (
            sem("w1_mm"), sem("gelu_ev"), sem("ff_ev"), sem("w2_mm"), sem("y_ff"))
        lnb_in, lnb_var, lnb_rstd, lnb_norm, lnb_back, lnb_out = (
            sem("lnb_in"), sem("lnb_var"), sem("lnb_rstd"), sem("lnb_norm"), sem("lnb_back"), sem("lnb_out"))
        x_fin, f_tr, f_cp = sem("x_fin"), sem("f_tr"), sem("f_cp")
        LNA = (ln_in, ln_var, ln_rstd, ln_norm, ln_back, ln_out)
        LNB = (lnb_in, lnb_var, lnb_rstd, lnb_norm, lnb_back, lnb_out)

        def apart(eng):
            eng.sem_inc(passed, 1)

        block = ctx.enter_context(nc.Block())
        N_CONST = []

        @block.sync
        def _(sp):
            def load(dst, src):
                sp.dma_start(dst, src, allow_slow_non_contiguous=True).then_inc(ld_const, 16)
                N_CONST.append(1)

            for name, dst in (("ident", ident), ("alibi", alibi), ("causal", causal), ("hm0", hm[0]),
                              ("hm1", hm[1]), ("wmask", wmask), ("rot", rot), ("rev", rev)):
                src = ins[name]
                load(dst[tuple(slice(None) for _ in src.shape)], src)
            load(wnat[:, 0:3, :], ins["L0_attn_w_qkv"].rearrange("(a n) k -> n a k", a=3))
            for k, n in enumerate(("L0_attn_w_out", "L1_attn_Wq", "L1_attn_Wk", "L1_attn_Wv", "L1_attn_Wo")):
                load(wnat[:, 3 + k, :], ins[n])
            load(bqkv[:, :], ins["L0_attn_b_qkv"].rearrange("(a n) -> n a", a=3))
            load(bv[:, :], ins["L0_attn_b_qkv"][2 * P:3 * P].partition_broadcast(P))
            load(bout[:, 0:1], ins["L0_attn_b_out"].unsqueeze(1))
            load(bout[:, 1:2], ins["L1_attn_bo"].unsqueeze(1))
            load(wg[:, :], ins["L0_ffn_Wg"])
            load(mw1[:, :, :], ins["L0_ffn_W1"].rearrange("e k h -> k e h"))
            load(mw2[:, :, :, :], ins["L0_ffn_W2"].rearrange("e (c k) n -> k e c n", c=2))
            for c in range(2):
                load(mb1[:, :, c], ins["L0_ffn_b1"][:, c * P:(c + 1) * P].rearrange("e k -> k e"))
            load(mb2[:, :], ins["L0_ffn_b2"])
            for k in range(2):
                load(cT[:, k, :], ins[f"L{k}_c"].rearrange("b k -> k b"))
                load(wmod[:, k, :], ins[f"L{k}_wmod"])
            load(beta[:, 0, :], ins["L1_attn_betas"].rearrange("a h b c -> (a h b c)").partition_broadcast(P))
            sp.wait_ge(zeroed, 2)
            for h in range(H1):
                load(memz[h * D1:(h + 1) * D1, h * D1:(h + 1) * D1], ins["L1_attn_mem"][h])
                load(memz[h * D1:(h + 1) * D1, P + h:P + h + 1], ins["L1_attn_z"][h])
            load(qks[:, 0, :, :], ins["L1_ffn_q_scale"].partition_broadcast(P))
            load(qks[:, 1, :, :], ins["L1_ffn_k_scale"].partition_broadcast(P))
            for k, n in enumerate(("L1_ffn_ln_g", "L1_ffn_ln_b", "L1_ffn_b2")):
                load(lcol[:, :, k], ins[n].rearrange("l k -> k l"))
            for k, (o, n) in enumerate(CH):
                for part in range(2):
                    load(lcol[0:n, :, 3 + 3 * part + k],
                         ins["L1_ffn_b1"][:, part * DI + o:part * DI + o + n].rearrange("l k -> k l"))
            x_v = ins["L0_attn_x"].rearrange("b (t p) k -> b p t k", p=P)
            with sp.Fori(0, B) as b:
                sp.wait_ge(x_tr, b)
                sp.dma_start(xtok, x_v[bass.ds(b, 1)].rearrange("a p t k -> (a p) t k")).then_inc(ld_x, 16)
            w_v = ins["L1_ffn_Wo"].rearrange("l (p k) n -> l k p n", k=P)

            def layer_weights(l):
                sp.wait_ge(pj_mm, l * (6 * T * B))
                sp.dma_start(wqkv[:, :], ins["L1_ffn_Wqkv"][bass.ds(l, 1)].rearrange("a k n -> (a k) n")
                             ).then_inc(ld_qkv, 16)
                sp.wait_ge(wo_mm, l * B)
                sp.dma_start(wo[:, :, :], w_v[bass.ds(l, 1)].rearrange("a k p n -> (a k) p n")
                             ).then_inc(ld_wo, 16)
                sp.wait_ge(w2_mm, l * B)
                sp.dma_start(w1[:, :], ins["L1_ffn_W1"][bass.ds(l, 1)].rearrange("a k n -> (a k) n")
                             ).then_inc(ld_ff, 16)
                for k, (o, n) in enumerate(CH):
                    sp.dma_start(w2[0:n, k, :],
                                 ins["L1_ffn_W2"][bass.ds(l, 1), o:o + n, :].rearrange("a k n -> (a k) n")
                                 ).then_inc(ld_ff, 16)

            def move_ends(l):
                with sp.Fori(0, B) as b:
                    for t in range(T - 1):
                        g = l * (B * T) + b * T + t
                        sp.wait_ge(v_cp, g * 2 + 2)
                        sp.wait_ge(o_mm, g)
                        sp.wait_ge(ld_vp, (l * (B * (T - 1)) + b * (T - 1) + t) * 16)
                        sp.dma_start(Vp[0:WIN, (t + 1) % 2, :], Vt[P - WIN:P, t % 2, :]).then_inc(ld_vp, 16)

            layer_weights(0)
            with sp.Fori(0, DEPTH - 1) as l:
                move_ends(l)
                layer_weights(l + 1)
            move_ends(DEPTH - 1)
            out_v = out.rearrange("b (t p) k -> b p t k", p=P)
            with sp.Fori(0, B) as b:
                sp.wait_ge(f_cp, b + 1)
                sp.dma_start(out_v[bass.ds(b, 1)].rearrange("a p t k -> (a p) t k"), xn[:, :, :]
                             ).then_inc(st_out, 16)
            sp.wait_ge(st_out, 16 * B)

        n_const = 16 * len(N_CONST)

        @block.tensor
        def _(pe):
            def mm(o, l, r, start=True, stop=True, **k):
                return nc.tensor.matmul(o, l, r, start=start, stop=stop, **k)

            def tp(o, i):
                return nc.tensor.transpose(o, i, ident[0:i.shape[0], 0:i.shape[0]])

            def layer_norm(sems, k, src):
                for t in range(T):
                    last = tp(tr[:, 0, t * P:(t + 1) * P], src[:, t * P:(t + 1) * P])
                last.then_inc(sems[0], 1)
                pe.wait_ge(sems[3], k + 1)
                for t in range(T):
                    last = tp(tr[:, 1, t * P:(t + 1) * P], xn[:, t, :])
                last.then_inc(sems[4], 1)

            pe.wait_ge(ld_const, n_const)
            for g in range(2):
                for k in range(4):
                    last = tp(tr[:, g, k * P:(k + 1) * P], wnat[:, 4 * g + k, :])
                last.then_inc(set_tr, 1)
            pe.wait_ge(silu_d, 1)
            for k in range(2):
                for j in range(6):
                    last = mm(pj[:, 0, (6 * k + j) * B:(6 * k + j + 1) * B],
                              wmod[:, k, j * P:(j + 1) * P], cw[:, 2, k, :])
            last.then_inc(set_tr, 1)
            pe.wait_ge(set_ev, 3)

            def attention(b, k):
                nh, wk = (H0, H1)[k], 4 * k
                hb = b * (H0 + H1) + k * H0
                sbs = hb * T
                gb = b * 5 + k * 4
                ab = b * 2 + k
                pe.wait_ge(ln_out, b * 3 + 2 * k + 1)
                for j in range(2):
                    mm(pj[:, j], wT[:, wk + j, :], hT[:, :]).then_inc(qk_mm, 1)
                for t in range(T):
                    last = mm(sc[:, 0, t * P:(t + 1) * P], hT[:, t * P:(t + 1) * P], wT[:, wk + 2, :])
                last.then_inc(v_mm, 1)
                pe.wait_ge(qk_ev, ab * 2 + 2)
                pe.wait_ge(v_ev, ab + 1)
                if k == 1:
                    pe.wait_ge(elu_s, b + 1)
                    for t in range(T):
                        last = mm(oo[:, t // 2, (t % 2) * (P + H1):(t % 2 + 1) * (P + H1)],
                                  sqT[:, t * P:(t + 1) * P], memz[:, :])
                    last.then_inc(mem_mm, 1)
                    pe.wait_ge(mixed, b * 2 + 1)

                def group_out(g):
                    pe.wait_ge(o_copied, gb + g + 1)
                    for t in range(T):
                        last = tp(oo[:, g % 2, t * P:(t + 1) * P], OTs[:, t * P:(t + 1) * P])
                    last.then_inc(o_tr, 1)

                for h in range(nh + 1):
                    if h < nh:
                        pe.wait_ge(q_masked, hb + h + 1)
                    for i in range(T):
                        if h < nh:
                            n = T * h + i
                            if n >= 3:
                                pe.wait_ge(biased, sbs + n - 2)
                            mm(SBANK[n % 3][:, 0:(i + 1) * P], Qm[:, h % 2, i * P:(i + 1) * P],
                               kTs[:, 0:(i + 1) * P]).then_inc(scores, 1)
                        if h >= 1:
                            n = T * (h - 1) + i
                            pe.wait_ge(probs, sbs + n + 1)
                            if n >= 3:
                                hh, ii = divmod(n - 3, T)
                                pe.wait_ge((pe_act, pe_dve)[ii % 2], (hb + hh) * 2 + ii // 2 + 1)
                            for j in range(i + 1):
                                last = tp(TBANK[n % 3][:, j * P:(j + 1) * P],
                                          Pr[:, n % 4, j * P:(j + 1) * P])
                            last.then_inc(p_tr, 1)
                    if h >= 1:
                        hh = h - 1
                        g = hh // 4
                        pe.wait_ge(pe_act, (hb + hh) * 2 + 2)
                        pe.wait_ge(pe_dve, (hb + hh) * 2 + 2)
                        if hh % 4 == 0 and g >= 2:
                            pe.wait_ge(o_tok, gb + g - 1)
                        q = 32 * (hh % 4)
                        for j in range(T):
                            last = mm(oo[q:q + 32, g % 2, j * P:S], Vh[:, j, hh, :], PTh[:, hh % 2, j, j * P:S],
                                      start=(j == 0), stop=(j == T - 1))
                        last.then_inc(pv_done, 1)
                        if hh % 4 == 0 and g >= 1:
                            group_out(g - 1)
                group_out(nh // 4 - 1)
                pe.wait_ge(o_tok if k == 0 else mixed, gb + 4 if k == 0 else b * 2 + 2)
                for t in range(T):
                    last = tp(tr[:, 0, t * P:(t + 1) * P], Otok[:, t, :])
                last.then_inc(of_tr, 1)
                pe.wait_ge(of_ev, ab + 1)
                mm(pj[:, 0], wT[:, 4 * k + 3, :], oTs[:, :]).then_inc(prj, 1)
                pe.wait_ge(x_add, b * 3 + 2 * k + 1)

            def experts(b):
                pe.wait_ge(ln_out, b * 3 + 2)
                for t in range(T):
                    last = mm(tr[:, 0, t * NE:(t + 1) * NE], hT[:, t * P:(t + 1) * P], wg[:, :])
                last.then_inc(lg_mm, 1)

                def up(e):
                    for c in range(2):
                        if e >= 1:
                            pe.wait_ge(m_relu, (b * NE + e) * 2 - 1 + c)
                        mm(pj[:, c], mw1[:, e, c * P:(c + 1) * P], hT[:, :]).then_inc(m_h, 1)

                def spread(e):
                    if e >= 2:
                        pe.wait_ge(m_sc, b * NE + e - 1)
                    for t in range(T):
                        w = rt[:, 11, t * NE + e:t * NE + e + 1].broadcast_to([P, P])
                        last = tp(tr[:, e % 2, t * P:(t + 1) * P], w)
                    last.then_inc(m_bc, 1)

                def down(e):
                    pe.wait_ge(m_sc, b * NE + e + 1)
                    for c in range(2):
                        last = mm(oo[:, 0], mw2[:, e, c, :], hsc[:, e % 2, c, :], start=False,
                                  stop=(e == NE - 1 and c == 1))
                    last.then_inc(m_y, 1)

                up(0)
                pe.wait_ge(routed, b + 1)
                for t in range(T):
                    last = tp(sc[0:NE, 0, t * P:(t + 1) * P], rt[:, 11, t * NE:(t + 1) * NE])
                last.then_inc(s_tr, 1)
                spread(0)
                pe.wait_ge(s_ev, b + 1)
                mm(oo[:, 0], mb2[:, :], sT[0:NE, :], stop=False)
                for e in range(1, NE):
                    up(e)
                    spread(e)
                    down(e - 1)
                down(NE - 1)
                pe.wait_ge(x_add, b * 3 + 2)

            with pe.Fori(0, B) as b:
                pe.wait_ge(ld_x, b * 16 + 16)
                for t in range(T):
                    last = tp(tr[:, 0, t * P:(t + 1) * P], xtok[:, t, :])
                last.then_inc(x_tr, 1)
                pe.wait_ge(x_in, b + 1)
                layer_norm(LNA, b * 4, xcur)
                attention(b, 0)
                layer_norm(LNA, b * 4 + 1, xcur)
                experts(b)
                layer_norm(LNA, b * 4 + 2, xcur)
                attention(b, 1)
                layer_norm(LNA, b * 4 + 3, xcur)
                pe.wait_ge(y_in, b + 1)

            def project(g, t, c):
                if c >= 4:
                    pe.wait_ge(rot_ev, g * 4 + c - 3)
                elif c >= 2:
                    pe.wait_ge(v_cp, g * 2 + c - 1)
                else:
                    pe.wait_ge(rot_ev, g * 4)
                col = [4, 5, 0, 1, 2, 3][c] * S
                mm(pj[:, c % 2], xsA[:, t * P:(t + 1) * P], wqkv[:, col:col + S]).then_inc(pj_mm, 1)

            def turn(g):
                for j in range(4):
                    pe.wait_ge(qk_rdy, g * 2 + j // 2 + 1)
                    if j >= 2:
                        pe.wait_ge(qk_cp, g * 4 + j - 1)
                    for u in range(4):
                        pr = 4 * (j % 2) + u
                        last = tp(tr[:, j % 2, u * P:(u + 1) * P], ra[:, j // 2, pr * P:(pr + 1) * P])
                    last.then_inc(qk_tr, 1)

            def window_scores(g, t):
                pe.wait_ge(qk_cp, g * 4 + 4)
                for u in range(2):
                    mm(sc[:, u].rearrange("p (a b) -> p a b", b=2 * WIN), identb[:, :],
                       wmaskb[:, 1 if t == 0 else 0, :].unsqueeze(1).broadcast_to([P, PAIRS, 2 * WIN]),
                       stop=False, skip_group_check=True)
                for pr in range(PAIRS):
                    for u in range(2):
                        d = slice(u * DL, (u + 1) * DL)
                        for w in range(P // WIN):
                            last = mm(sc[w * WIN:(w + 1) * WIN, u, pr * 2 * WIN:(pr + 1) * 2 * WIN],
                                      qT[d, pr, w * WIN:(w + 1) * WIN],
                                      kT[d, pr, t * P + w * WIN:t * P + (w + 2) * WIN],
                                      start=False, stop=True, skip_group_check=True)
                last.then_inc(sc_mm, 1)

            def turn_probs(g, t):
                pe.wait_ge(bd_dve, g + 1)
                pe.wait_ge(bd_pool, g + 1)
                for j in range(4):
                    if j >= 2:
                        pe.wait_ge(pt_cp, g * 4 + j - 1)
                    for u in range(4):
                        last = tp(tr[:, j % 2, u * P:(u + 1) * P], Bd[:, 4 * j + u, WIN:WIN + P])
                    last.then_inc(pt_tr, 1)

            def values(n, g, t):
                if t > 0:
                    pe.wait_ge(ptp_ok, n * (T - 1) + t)
                    pe.wait_ge(ld_vp, (n * (T - 1) + t) * 16)
                pe.wait_ge(pt_cp, g * 4 + 4)
                pe.wait_ge(o_cp, g)
                for pr in range(PAIRS):
                    for u in range(2):
                        j, f = u * PAIRS + pr, (2 * pr + u) * DL
                        d = slice(u * DL, (u + 1) * DL)
                        c = (pr % 4) * P
                        last = mm(oo[d, pr // 4, c:c + P], Vt[:, t % 2, f:f + DL], PT[:, j, :],
                                  start=True, stop=(t == 0), skip_group_check=True)
                        if t > 0:
                            last = mm(oo[d, pr // 4, c:c + WIN], Vp[:, t % 2, f:f + DL], PTp[:, j, :],
                                      start=False, stop=True, skip_group_check=True)
                last.then_inc(o_mm, 1)

            with pe.Fori(0, DEPTH) as l:
                with pe.Fori(0, B) as b:
                    n = l * B + b
                    pe.wait_ge(ld_qkv, l * 16 + 16)
                    pe.wait_ge(xs_a, n + 1)
                    for c in range(6):
                        project(n * T, 0, c)
                    turn(n * T)
                    for t in range(T):
                        g = n * T + t
                        window_scores(g, t)
                        if t + 1 < T:
                            for c in range(6):
                                project(g + 1, t + 1, c)
                        turn_probs(g, t)
                        values(n, g, t)
                        if t + 1 < T:
                            turn(g + 1)
                    pe.wait_ge(o_cp, n * T + T)
                    pe.wait_ge(ld_wo, l * 16 + 16)
                    for p_ in range(PAIRS):
                        last = mm(sc[:, 0], wo[:, p_, :], oT[:, p_, :], start=(p_ == 0), stop=(p_ == PAIRS - 1))
                    last.then_inc(wo_mm, 1)
                    pe.wait_ge(xs_f, n + 1)
                    layer_norm(LNB, n, xsF)
                    pe.wait_ge(lnb_out, n + 1)
                    pe.wait_ge(ld_ff, l * 64 + 64)
                    for k, (o, m) in enumerate(CH):
                        ps = (pj, oo, sc)[k]
                        mm(ps[0:m, 0], w1[:, DI + o:DI + o + m], hT[:, :])
                        mm(ps[0:m, 1], w1[:, o:o + m], hT[:, :]).then_inc(w1_mm, 1)
                    for k, (o, m) in enumerate(CH):
                        pe.wait_ge(ff_ev, n * FFC + k + 1)
                        last = mm(tr[:, 0], w2[0:m, k, :], fa[0:m, k, :], start=(k == 0), stop=(k == FFC - 1))
                    last.then_inc(w2_mm, 1)
                    pe.wait_ge(y_ff, n + 1)

            with pe.Fori(0, B) as b:
                pe.wait_ge(x_fin, b + 1)
                for t in range(T):
                    last = tp(tr[:, 0, t * P:(t + 1) * P], xcur[:, t * P:(t + 1) * P])
                last.then_inc(f_tr, 1)
                pe.wait_ge(f_cp, b + 1)

        @block.vector
        def _(ve):
            v = nc.vector

            def layer_norm(ch, sems, k):
                ve.wait_ge(sems[0], k + 1)
                for t in range(T):
                    ins_ = v.bn_stats(stats[:, t, :], tr[:, 0, t * P:(t + 1) * P])
                ch.do(ins_)
                apart(ve)
                for t in range(T):
                    ins_ = v.bn_aggr(mv[:, t, :], stats[:, t, :])
                ch.do(ins_)
                v.tensor_scalar(rstd[:, :], mv[:, :, 1], EPS, None, ALU.add).then_inc(sems[1], 1)
                ve.wait_ge(sems[2], k + 1)
                for t in range(T):
                    ins_ = v.tensor_scalar(xn[:, t, :], tr[:, 0, t * P:(t + 1) * P], mv[:, t, 0:1],
                                           rstd[:, t:t + 1], ALU.subtract, ALU.mult)
                ins_.then_inc(sems[3], 1)

            ch = Chain(ve, dve_c)
            ve.wait_ge(ld_const, n_const)
            v.tensor_copy(identb[:, :], ident[:, :])
            ch.do(v.tensor_copy(wmaskb[:, :, :], wmask[:, :, :]))
            ve.wait_ge(silu_e, 2)
            ch.do(v.tensor_scalar(cw[:, 1], cw[:, 0], 1.0, None, ALU.add))
            ch.do(v.reciprocal(cw[:, 0], cw[:, 1]))
            v.tensor_tensor(cw[:, 2], cw[:, 0], cT[:, :, :], ALU.mult).then_inc(silu_d, 1)
            ch.do(v.tensor_scalar(beta[:, 2, :], beta[:, 1, :], 1.0, None, ALU.add))
            ch.do(v.reciprocal(beta[:, 1, :], beta[:, 2, :]))
            ch.do(v.tensor_scalar(beta[:, 2, :], beta[:, 1, :], -1.0, 1.0, ALU.mult, ALU.add))
            for g in range(2):
                ve.wait_ge(set_tr, g + 1)
                v.tensor_copy(wT[:, 4 * g:4 * g + 4, :], tr[:, g].rearrange("p (a b) -> p a b", b=P)
                              ).then_inc(set_ev, 1)
            ve.wait_ge(set_tr, 3)
            v.tensor_copy(modT[:, :, :], pj[:, 0, 0:NMOD * B].rearrange("p (j b) -> p b j", b=B)
                          ).then_inc(set_ev, 1)
            ve.wait_ge(set_ev, 3)
            for j in (CA, CB, 6 + CA, 6 + CB):
                v.tensor_scalar(modT[:, :, j], modT[:, :, j], 1.0, None, ALU.add)
            for j in (GA, GB, 6 + GA, 6 + GB):
                ins_ = v.tensor_scalar(gsgn[:, :, j], modT[:, :, j], 0.0, 2.0, ALU.is_ge, ALU.mult)
            ch.do(ins_)
            for j in (GA, GB, 6 + GA, 6 + GB):
                ins_ = v.tensor_scalar(gneg[:, :, j], modT[:, :, j], -1.0, 0.25, ALU.mult, ALU.max)
            ch.do(ins_)
            for j in (GA, GB, 6 + GA, 6 + GB):
                ins_ = v.tensor_tensor(modT[:, :, j], modT[:, :, j], gneg[:, :, j], ALU.max)
            ch.do(ins_)
            for j in (GA, GB, 6 + GA, 6 + GB):
                ins_ = v.scalar_tensor_tensor(out=modT[:, :, j], in0=gsgn[:, :, j], scalar=-1.0,
                                              in1=modT[:, :, j], op0=ALU.add, op1=ALU.mult)
            ch.do(ins_)
            dve_setup = ch.n

            def attention(b, k, ch):
                nh, d = (H0, H1)[k], (D0, D1)[k]
                hb = b * (H0 + H1) + k * H0
                sbs = hb * T
                gb = b * 5 + k * 4
                ab = b * 2 + k
                bias = (alibi, causal)[k]
                ve.wait_ge(v_mm, ab + 1)
                src = sc[:, 0].rearrange("p (t h d) -> p t h d", t=T, d=d)
                if k == 0:
                    ch.do(v.memset(Vh[:, :, :, :], 0.0))
                    for t in range(T):
                        ins_ = v.tensor_tensor(Vh[:, t, :, 0:d], src[:, t],
                                               bv[:, :].rearrange("p (h d) -> p h d", d=d), ALU.add)
                else:
                    ins_ = v.tensor_copy(Vh[:, :, 0:nh, :], src)
                ins_.then_inc(v_ev, 1)
                if k == 1:
                    ve.wait_ge(qk_ev, ab * 2 + 1)
                    v.tensor_scalar(eq_, qTs, 0.0, None, ALU.min).then_inc(elu_m, 1)
                    ve.wait_ge(elu_e, b + 1)
                    v.scalar_tensor_tensor(out=sqT, in0=qTs, scalar=0.0, in1=eq_, op0=ALU.max,
                                           op1=ALU.add).then_inc(elu_s, 1)
                    ve.wait_ge(mem_mm, b + 1)
                    for t in range(T):
                        z = (t % 2) * (P + H1) + P
                        ins_ = v.tensor_scalar(den[:, t, :], oo[:, t // 2, z:z + H1], 1e-6, None, ALU.add)
                    ch.do(ins_)
                    ch.do(v.reciprocal(den, den))
                    ch.do(v.tensor_tensor(den, den, beta[:, 1, :].unsqueeze(1).broadcast_to([P, T, H1]),
                                          ALU.mult))
                    for t in range(T):
                        z = (t % 2) * (P + H1)
                        ins_ = v.tensor_tensor(
                            Am[:, t, :].rearrange("p (h d) -> p h d", d=D1),
                            oo[:, t // 2, z:z + P].rearrange("p (h d) -> p h d", d=D1),
                            den[:, t, :].unsqueeze(2).broadcast_to([P, H1, D1]), ALU.mult)
                    ins_.then_inc(mixed, 1)

                def group_out(g):
                    ve.wait_ge(o_tr, gb + g + 1)
                    ch.do(v.reciprocal(rinv[:, 4 * g:4 * g + 4, :], rsum[:, 4 * g:4 * g + 4, :]))
                    o = Otok.rearrange("p t (h d) -> p t h d", d=d)[:, :, 4 * g:4 * g + 4, :]
                    i_ = oo[:, g % 2].rearrange("p (t h d) -> p t h d", t=T, d=PADH)[:, :, :, 0:d]
                    for t in range(T):
                        last = v.tensor_tensor(o[:, t], i_[:, t], rinv[:, 4 * g:4 * g + 4, t].unsqueeze(2)
                                               .broadcast_to([P, 4, d]), ALU.mult)
                    last.then_inc(o_tok, 1)

                for h in range(nh + 1):
                    for i in range(T):
                        if h < nh:
                            n = T * h + i
                            ve.wait_ge(scores, sbs + n + 1)
                            if n >= 2:
                                ve.wait_ge(probs, sbs + n - 1)
                            apart(ve)
                            w = (i + 1) * P
                            v.tensor_tensor_reduce(out=Ssb[:, n % 2, 0:w], in0=SBANK[n % 3][:, 0:w],
                                                   in1=bias[:, S - w:S], scale=-1.0, scalar=3e38,
                                                   op0=ALU.add, op1=ALU.min,
                                                   accum_out=nmax[:, n:n + 1]).then_inc(biased, 1)
                        if h >= 1 and i % 2 == 1:
                            n = T * (h - 1) + i
                            ve.wait_ge(p_tr, sbs + n + 1)
                            if h >= 3:
                                ve.wait_ge(pv_done, hb + h - 2)
                            w = (i + 1) * P
                            v.tensor_copy(PTh[:, (h - 1) % 2, 0:i + 1, i * P:(i + 1) * P],
                                          TBANK[n % 3][:, 0:w].rearrange("p (a b) -> p a b", b=P)
                                          ).then_inc(pe_dve, 1)
                    if h >= 6 and (h - 2) % 4 == 0:
                        group_out((h - 2) // 4 - 1)
                group_out(nh // 4 - 1)
                if k == 1:
                    ve.wait_ge(o_tok, gb + 1)
                    for t in range(T):
                        ins_ = v.tensor_tensor(Otok[:, t, :].rearrange("p (h d) -> p h d", d=D1),
                                               Otok[:, t, :].rearrange("p (h d) -> p h d", d=D1),
                                               beta[:, 2, :].unsqueeze(2).broadcast_to([P, H1, D1]), ALU.mult)
                    ch.do(ins_)
                    v.tensor_tensor(Otok, Otok, Am, ALU.add).then_inc(mixed, 1)
                ve.wait_ge(prj, ab + 1)
                g_ = 6 * k + GA
                ch.do(v.tensor_scalar(tmp[:, :], pj[:, 0], bout[:, k:k + 1], mcur[:, g_:g_ + 1],
                                      ALU.add, ALU.mult))
                v.tensor_tensor(xcur[:, :], xcur[:, :], tmp[:, :], ALU.add).then_inc(x_add, 1)

            def experts(b, ch):
                R = [rt[:, k].rearrange("p (t e) -> p t e", e=NE) for k in range(12)]

                def wide(k):
                    return rs4[:, k].unsqueeze(2).broadcast_to([P, T, NE])

                ve.wait_ge(lg_mm, b + 1)
                lg = tr[:, 0, 0:T * NE].rearrange("p (t e) -> p t e", e=NE)
                ch.do(v.tensor_reduce(rs4[:, 0], lg, AX.X, ALU.max))
                v.tensor_tensor(R[0], lg, wide(0), ALU.subtract).then_inc(lg_sub, 1)
                ve.wait_ge(lg_exp, b + 1)
                ch.do(v.tensor_reduce(rs4[:, 1], R[1], AX.X, ALU.add))
                ch.do(v.reciprocal(rs4[:, 2], rs4[:, 1]))
                ch.do(v.tensor_tensor(R[2], R[1], wide(2), ALU.mult))

                def pick(src, m, eq, key, first, s):
                    ch.do(v.tensor_reduce(rs4[:, m], R[src], AX.X, ALU.max))
                    ch.do(v.tensor_tensor(R[eq], R[src], wide(m), ALU.is_equal))
                    ch.do(v.tensor_tensor(R[key], R[eq], rev[:, :, :], ALU.mult))
                    ch.do(v.tensor_reduce(rs4[:, s], R[key], AX.X, ALU.max))
                    ch.do(v.tensor_tensor(R[first], rev[:, :, :], wide(s), ALU.is_equal))

                pick(2, 3, 3, 4, 5, 0)
                ch.do(v.scalar_tensor_tensor(out=R[6], in0=R[5], scalar=-2.0, in1=R[2], op0=ALU.mult,
                                             op1=ALU.add))
                pick(6, 4, 7, 8, 9, 1)
                v.tensor_tensor(R[10], R[5], R[9], ALU.add)
                ch.do(v.tensor_tensor(rs4[:, 5], rs4[:, 3], rs4[:, 4], ALU.add))
                ch.do(v.reciprocal(rs4[:, 5], rs4[:, 5]))
                ch.do(v.tensor_tensor(R[10], R[10], R[2], ALU.mult))
                v.tensor_tensor(R[11], R[10], wide(5), ALU.mult).then_inc(routed, 1)
                ve.wait_ge(s_tr, b + 1)
                v.tensor_copy(sT[0:NE, :], sc[0:NE, 0, :]).then_inc(s_ev, 1)
                for e in range(NE):
                    ve.wait_ge(m_relu, (b * NE + e) * 2 + 2)
                    ve.wait_ge(m_bc, b * NE + e + 1)
                    if e >= 2:
                        ve.wait_ge(m_y, b * NE + e - 1)
                    v.tensor_tensor(hsc[:, e % 2], hes[:, e % 2],
                                    tr[:, e % 2].unsqueeze(1).broadcast_to([P, 2, S]),
                                    ALU.mult).then_inc(m_sc, 1)
                ve.wait_ge(m_y, b * NE + NE)
                ch.do(v.tensor_scalar(tmp[:, :], oo[:, 0], mcur[:, GB:GB + 1], None, ALU.mult))
                v.tensor_tensor(xcur[:, :], xcur[:, :], tmp[:, :], ALU.add).then_inc(x_add, 1)

            with ve.Fori(0, B) as b:
                ch = Chain(ve, dve_c, b * DVE_A + dve_setup)
                ve.wait_ge(y_in, b)
                v.tensor_copy(mcur[:, :].unsqueeze(1), modT[:, bass.ds(b, 1), :]).then_inc(mod_cur, 1)
                ve.wait_ge(mod_cur, b + 1)
                ve.wait_ge(x_tr, b + 1)
                v.tensor_copy(xcur[:, :], tr[:, 0]).then_inc(x_in, 1)
                layer_norm(ch, LNA, b * 4)
                attention(b, 0, ch)
                layer_norm(ch, LNA, b * 4 + 1)
                experts(b, ch)
                layer_norm(ch, LNA, b * 4 + 2)
                attention(b, 1, ch)
                layer_norm(ch, LNA, b * 4 + 3)
                ve.wait_ge(x_add, b * 3 + 3)
                ch.do(v.tensor_copy(XT[:, bass.ds(b * S, S)], xcur[:, :]))
                assert ch.n == DVE_A, ("DVE_A", ch.n)

            def rotate(g, t, c):
                k, hf = c // 2, c % 2
                ve.wait_ge(sq_ev, g * 4 + c + 1)
                src = pj[:, c % 2].rearrange("p (h u d) -> p h u d", u=2, d=DL // 2)
                tc_ = rtab[:, 2 * k, t, :].rearrange("p (u d) -> p u d", u=2)
                ts_ = rtab[:, 2 * k + 1, t, :].rearrange("p (u d) -> p u d", u=2)
                wide = [P, PAIRS, 2, DL // 2]
                co = slice(hf * S, (hf + 1) * S)
                v.tensor_tensor(ra[:, k, co].rearrange("p (h u d) -> p h u d", u=2, d=DL // 2), src,
                                tc_.unsqueeze(1).broadcast_to(wide), ALU.mult)
                v.tensor_tensor(rb[:, k, co].rearrange("p (h u d) -> p h u d", u=2, d=DL // 2),
                                src[:, :, ::-1, :], ts_.unsqueeze(1).broadcast_to(wide), ALU.mult
                                ).then_inc(rot_ev, 1)
                v.tensor_reduce(ss[:, k, hf * PAIRS:(hf + 1) * PAIRS],
                                sq[:, c % 2].rearrange("p (h d) -> p h d", d=DL), AX.X, ALU.add
                                ).then_inc(ss_ok, 1)

            def soft1(g, ch):
                ve.wait_ge(sc_mm, g + 1)
                s_v = sc[:, :, :].rearrange("p u (a b) -> p (u a) b", b=2 * WIN)
                ch.do(v.tensor_reduce(mx, s_v, AX.X, ALU.max))
                v.tensor_tensor(Tm, s_v, mx.unsqueeze(2).broadcast_to([P, HL, 2 * WIN]),
                                ALU.subtract).then_inc(t_sub, 1)

            with ve.Fori(0, DEPTH) as l:
                base = dve_setup + B * DVE_A
                ve.wait_ge(y_ff, l * B)
                v.tensor_copy(lcur[:, :].unsqueeze(1), lcol[:, bass.ds(l, 1), :])
                for k in range(2):
                    qv = qks[:, k, bass.ds(l, 1), :]
                    v.tensor_tensor(rtab[:, 2 * k], rot[:, 2 * k], qv.broadcast_to([P, T, DL]), ALU.mult)
                    for u in range(2):
                        h_ = slice(u * DL // 2, (u + 1) * DL // 2)
                        o_ = slice((1 - u) * DL // 2, (2 - u) * DL // 2)
                        ins_ = v.tensor_tensor(rtab[:, 2 * k + 1, :, h_], rot[:, 2 * k + 1, :, h_],
                                               qks[:, k, bass.ds(l, 1), o_].broadcast_to([P, T, DL // 2]),
                                               ALU.mult)
                ins_.then_inc(tabs, 1)
                ve.wait_ge(tabs, l + 1)
                apart(ve)
                with ve.Fori(0, B) as b:
                    n = l * B + b
                    ch = Chain(ve, dve_c, n * DVE_B + base)
                    for c in range(4):
                        rotate(n * T, 0, c)
                    for t in range(T):
                        g = n * T + t
                        soft1(g, ch)
                        if t + 1 < T:
                            rotate(g + 1, t + 1, 0)
                            rotate(g + 1, t + 1, 1)
                        ve.wait_ge(e_exp, g + 1)
                        ch.do(v.tensor_reduce(sm, Ex, AX.X, ALU.add))
                        v.reciprocal(ri, sm).then_inc(ri_ok, 1)
                        ve.wait_ge(ri_ok, g + 1)
                        ve.wait_ge(pt_tr, g * 4)
                        for w in range(2):
                            q = slice(w * WIN, (w + 1) * WIN)
                            last = v.tensor_tensor(Bd[q, :, w * WIN:(w + 2) * WIN], Ex[q],
                                                   ri[q].unsqueeze(2).broadcast_to([WIN, HL, 2 * WIN]),
                                                   ALU.mult)
                        last.then_inc(bd_dve, 1)
                        if t > 0:
                            ve.wait_ge(bd_dve, g + 1)
                            ve.wait_ge(o_mm, g)
                            v.transpose(PTp[0:WIN], Bd[0:WIN, :, 0:WIN]).then_inc(ptp_ok, 1)
                        if t + 1 < T:
                            rotate(g + 1, t + 1, 2)
                            rotate(g + 1, t + 1, 3)
                    y = YT[:, bass.ds(b * S, S)]
                    ve.wait_ge(wo_mm, n + 1)
                    v.tensor_tensor(y, sc[:, 0], y, ALU.add).then_inc(y_att, 1)
                    layer_norm(ch, LNB, n)
                    for k, (o, m) in enumerate(CH):
                        ps = (pj, oo, sc)[k]
                        ve.wait_ge(gelu_ev, n * FFC + k + 1)
                        v.scalar_tensor_tensor(out=fa[0:m, k, :], in0=ps[0:m, 1], scalar=lcur[0:m, 3 + k:4 + k],
                                               in1=ge[0:m, k, :], op0=ALU.add, op1=ALU.mult
                                               ).then_inc(ff_ev, 1)
                    ve.wait_ge(w2_mm, n + 1)
                    v.scalar_tensor_tensor(out=y, in0=tr[:, 0], scalar=lcur[:, 2:3], in1=y,
                                           op0=ALU.add, op1=ALU.add).then_inc(y_ff, 1)
                    assert ch.n == DVE_B, ("DVE_B", ch.n)

            with ve.Fori(0, B) as b:
                ch = Chain(ve, dve_c, b * 2 + base + DEPTH * B * DVE_B)
                ve.wait_ge(y_ff, DEPTH * B)
                ve.wait_ge(f_tr, b)
                ch.do(v.tensor_copy(mcur[:, :].unsqueeze(1), modT[:, bass.ds(b, 1), :]))
                ch.do(v.tensor_scalar(tmp[:, :], YT[:, bass.ds(b * S, S)], mcur[:, 6 + GB:7 + GB], None,
                                      ALU.mult))
                v.tensor_tensor(xcur[:, :], XT[:, bass.ds(b * S, S)], tmp[:, :], ALU.add).then_inc(x_fin, 1)
                ve.wait_ge(f_tr, b + 1)
                ve.wait_ge(st_out, b * 16)
                v.tensor_copy(xn[:, :, :], tr[:, 0].rearrange("p (a b) -> p a b", b=P)).then_inc(f_cp, 1)

        @block.scalar
        def _(ac):
            def act(o, i, f, **k):
                return nc.scalar.activation(o, i, f, **k)

            ac.wait_ge(ld_const, n_const)
            act(cw[:, 0], cT[:, :, :], ACT.Exp, scale=-1.0).then_inc(silu_e, 1)
            act(beta[:, 1, :], beta[:, 0, :], ACT.Exp, scale=-1.0).then_inc(silu_e, 1)

            def ln_finish(sems, k, scale, bias, dst):
                ac.wait_ge(sems[4], k + 1)
                act(dst, tr[:, 1], ACT.Identity, scale=scale, bias=bias).then_inc(sems[5], 1)

            def attention(b, k):
                nh = (H0, H1)[k]
                hb = b * (H0 + H1) + k * H0
                sbs = hb * T
                gb = b * 5 + k * 4
                ab = b * 2 + k
                for j in range(2):
                    ac.wait_ge(qk_mm, ab * 2 + j + 1)
                    dst = (qTs, kTs)[j]
                    if k == 0:
                        act(dst, pj[:, j], ACT.Identity, bias=bqkv[:, j:j + 1]).then_inc(qk_ev, 1)
                    else:
                        act(dst, pj[:, j], ACT.Copy).then_inc(qk_ev, 1)
                if k == 1:
                    ac.wait_ge(elu_m, b + 1)
                    act(eq_, eq_, ACT.Exp).then_inc(elu_e, 1)

                def group_out(g):
                    ac.wait_ge(pv_done, hb + 4 * g + 4)
                    if g >= 1:
                        ac.wait_ge(o_tr, gb + g)
                    act(OTs, oo[:, g % 2], ACT.Copy).then_inc(o_copied, 1)

                for h in range(nh + 1):
                    for i in range(T):
                        if h < nh:
                            n = T * h + i
                            w = (i + 1) * P
                            ac.wait_ge(biased, sbs + n + 1)
                        if h >= 1 and i % 2 == 0:
                            m = T * (h - 1) + i
                            ac.wait_ge(p_tr, sbs + m + 1)
                            if h >= 3:
                                ac.wait_ge(pv_done, hb + h - 2)
                            ww = (i + 1) * P
                            act(PTh[:, (h - 1) % 2, 0:i + 1, i * P:(i + 1) * P],
                                TBANK[m % 3][:, 0:ww].rearrange("p (a b) -> p a b", b=P), ACT.Copy
                                ).then_inc(pe_act, 1)
                        if h < nh:
                            if n >= 4:
                                ac.wait_ge(p_tr, sbs + n - 3)
                            act(Pr[:, n % 4, 0:w], Ssb[:, n % 2, 0:w], ACT.Exp, scale=-1.0,
                                bias=nmax[:, n:n + 1], accum_out=rsum[:, h, i:i + 1]).then_inc(probs, 1)
                    if h >= 4 and h % 4 == 1:
                        group_out(h // 4 - 1)
                group_out(nh // 4 - 1)
                ac.wait_ge(of_tr, ab + 1)
                act(oTs, tr[:, 0], ACT.Copy).then_inc(of_ev, 1)

            with ac.Fori(0, B) as b:
                ac.wait_ge(mod_cur, b + 1)
                ln_finish(LNA, b * 4, mcur[:, CA:CA + 1], mcur[:, SA:SA + 1], hT[:, :])
                attention(b, 0)
                ln_finish(LNA, b * 4 + 1, mcur[:, CB:CB + 1], mcur[:, SB:SB + 1], hT[:, :])
                ac.wait_ge(lg_sub, b + 1)
                act(rt[:, 1], rt[:, 0], ACT.Exp).then_inc(lg_exp, 1)
                for e in range(NE):
                    for c in range(2):
                        ac.wait_ge(m_h, (b * NE + e) * 2 + c + 1)
                        if e >= 2 and c == 0:
                            ac.wait_ge(m_sc, b * NE + e - 1)
                        act(hes[:, e % 2, c, :], pj[:, c], ACT.Relu, bias=mb1[:, e, c:c + 1]
                            ).then_inc(m_relu, 1)
                ln_finish(LNA, b * 4 + 2, mcur[:, 6 + CA:7 + CA], mcur[:, 6 + SA:7 + SA], hT[:, :])
                attention(b, 1)
                ac.wait_ge(ln_back, b * 4 + 4)
                apart(ac)
                act(YT[:, bass.ds(b * S, S)], tr[:, 1], ACT.Identity, scale=mcur[:, 6 + CB:7 + CB],
                    bias=mcur[:, 6 + SB:7 + SB]).then_inc(y_in, 1)

            hp = P // 2
            ac.wait_ge(zeroed, 8)
            ac.wait_ge(y_in, B)

            def shifted(dst, y):
                act(dst[0:hp, :], y[0:hp, :], ACT.Copy)
                return act(dst[hp:P, 1:S], y[hp:P, 0:S - 1], ACT.Copy)

            def square(g, c):
                ac.wait_ge(pj_mm, g * 6 + c + 3)
                act(sq[:, c % 2], pj[:, c % 2], ACT.Square).then_inc(sq_ev, 1)

            def copy_v(g, t, c):
                ac.wait_ge(pj_mm, g * 6 + c + 1)
                act(Vt[:, t % 2, c * S:(c + 1) * S], pj[:, c], ACT.Copy).then_inc(v_cp, 1)

            def take_qk(g, t):
                for j in range(4):
                    ac.wait_ge(qk_tr, g * 4 + j + 1)
                    src = tr[:, j % 2].rearrange("p (a b) -> p a b", b=P)
                    pr = slice(4 * (j % 2), 4 * (j % 2) + 4)
                    if j < 2:
                        dst = qT[:, pr, :]
                    else:
                        dst = kT[:, pr, WIN + t * P:WIN + (t + 1) * P]
                    act(dst, src, ACT.Copy).then_inc(qk_cp, 1)

            with ac.Fori(0, DEPTH) as l:
                with ac.Fori(0, B) as b:
                    n = l * B + b
                    y = YT[:, bass.ds(b * S, S)]
                    ac.wait_ge(y_ff, n)
                    ac.wait_ge(pj_mm, n * (6 * T))
                    apart(ac)
                    shifted(xsA, y).then_inc(xs_a, 1)
                    for c in range(2):
                        copy_v(n * T, 0, c)
                    for c in range(4):
                        if c >= 2:
                            ac.wait_ge(ss_ok, n * T * 4 + c - 1)
                        square(n * T, c)
                    take_qk(n * T, 0)
                    for t in range(T):
                        g = n * T + t
                        if t + 1 < T:
                            if t >= 1:
                                ac.wait_ge(o_mm, g)
                                ac.wait_ge(ld_vp, (n * (T - 1) + t) * 16)
                            for c in range(2):
                                copy_v(g + 1, t + 1, c)
                            ac.wait_ge(ss_ok, g * 4 + 3)
                            square(g + 1, 0)
                        ac.wait_ge(t_sub, g + 1)
                        ac.wait_ge(bd_pool, g)
                        act(Ex, Tm, ACT.Exp, scale=8.0).then_inc(e_exp, 1)
                        if t + 1 < T:
                            for c in range(1, 4):
                                ac.wait_ge(ss_ok, g * 4 + 3 + c)
                                square(g + 1, c)
                        for j in range(4):
                            ac.wait_ge(pt_tr, g * 4 + j + 1)
                            if j == 0:
                                ac.wait_ge(o_mm, g)
                            act(PT[:, 4 * j:4 * j + 4, :], tr[:, j % 2].rearrange("p (a b) -> p a b", b=P),
                                ACT.Copy).then_inc(pt_cp, 1)
                        ac.wait_ge(o_mm, g + 1)
                        act(oT[:, :, t * P:(t + 1) * P], oo[:, :, :].rearrange("p u (a b) -> p (u a) b", b=P),
                            ACT.Copy).then_inc(o_cp, 1)
                        if t + 1 < T:
                            take_qk(g + 1, t + 1)
                    ac.wait_ge(y_att, n + 1)
                    apart(ac)
                    shifted(xsF, y).then_inc(xs_f, 1)
                    ln_finish(LNB, n, lcur[:, 0:1], lcur[:, 1:2], hT[:, :])
                    for k, (o, m) in enumerate(CH):
                        ps = (pj, oo, sc)[k]
                        ac.wait_ge(w1_mm, n * FFC + k + 1)
                        act(ge[0:m, k, :], ps[0:m, 0], ACT.Gelu, bias=lcur[0:m, 6 + k:7 + k]
                            ).then_inc(gelu_ev, 1)

        @block.gpsimd
        def _(gp):
            p_ = nc.gpsimd
            ch = Chain(gp, pool_c)
            p_.memset(memz[:, :], 0.0).then_inc(zeroed, 1)
            p_.memset(lcol[:, :, :], 0.0).then_inc(zeroed, 1)
            ch.do(p_.memset(half_neg[:, :], -0.5))
            gp.wait_ge(ld_const, n_const)

            def power(sems, k):
                gp.wait_ge(sems[1], k + 1)
                p_.tensor_tensor(rstd[:, :], rstd[:, :], half_neg[:, 0:T], ALU.pow).then_inc(sems[2], 1)

            def attention(b, k):
                nh = (H0, H1)[k]
                hb = b * (H0 + H1) + k * H0
                ab = b * 2 + k
                gp.wait_ge(qk_ev, ab * 2 + 1)
                for h in range(nh):
                    if h >= 2:
                        gp.wait_ge(scores, (hb + h - 1) * T)
                    apart(gp)
                    p_.tensor_scalar(Qm[:, h % 2, :], qTs, hm[k][:, h:h + 1], 1.0, ALU.mult, ALU.mult
                                     ).then_inc(q_masked, 1)

            with gp.Fori(0, B) as b:
                power(LNA, b * 4)
                attention(b, 0)
                power(LNA, b * 4 + 1)
                power(LNA, b * 4 + 2)
                attention(b, 1)
                power(LNA, b * 4 + 3)

            gp.wait_ge(y_in, B)
            for area in (Bd, kT[:, :, 0:WIN], Vp, PTp, xsA[:, 0:1], xsF[:, 0:1]):
                p_.memset(area, 0.0).then_inc(zeroed, 1)

            def normed(g, k):
                gp.wait_ge(ss_ok, g * 4 + 2 * k + 2)
                gp.wait_ge(rot_ev, g * 4 + 2 * k + 2)
                apart(gp)
                ch.do(p_.tensor_scalar(rr[:, k, :], ss[:, k, :], 1e-24, 1.0, ALU.max, ALU.mult))
                p_.tensor_tensor(rr[:, k, :], rr[:, k, :], half_neg[:, 0:HL], ALU.pow)
                ch.do(p_.tensor_tensor(ra[:, k, :], ra[:, k, :], rb[:, k, :], ALU.add))
                r3 = ra[:, k, :].rearrange("p (h d) -> p h d", d=DL)
                p_.tensor_tensor(r3, r3, rr[:, k, :].unsqueeze(2).broadcast_to([P, HL, DL]), ALU.mult
                                 ).then_inc(qk_rdy, 1)

            with gp.Fori(0, DEPTH * B) as n:
                ch = Chain(gp, pool_c, n * (T * 5) + 1)
                normed(n * T, 0)
                normed(n * T, 1)
                for t in range(T):
                    g = n * T + t
                    if t + 1 < T:
                        normed(g + 1, 0)
                    gp.wait_ge(ri_ok, g + 1)
                    gp.wait_ge(pt_tr, g * 4)
                    gp.wait_ge(qk_rdy, g * 2 + (3 if t + 1 < T else 2))
                    for w in range(2, 4):
                        q = slice(w * WIN, (w + 1) * WIN)
                        last = p_.tensor_tensor(Bd[q, :, w * WIN:(w + 2) * WIN], Ex[q],
                                                ri[q].unsqueeze(2).broadcast_to([WIN, HL, 2 * WIN]), ALU.mult)
                        if w == 2:
                            ch.do(last)
                    last.then_inc(bd_pool, 1)
                    gp.wait_ge(bd_pool, g + 1)
                    if t + 1 < T:
                        normed(g + 1, 1)
                power(LNB, n)


_INS = ['L0_attn_x', 'L0_attn_w_qkv', 'L0_attn_b_qkv', 'L0_attn_w_out', 'L0_attn_b_out', 'L0_ffn_Wg',
        'L0_ffn_W1', 'L0_ffn_b1', 'L0_ffn_W2', 'L0_ffn_b2', 'L0_c', 'L0_wmod', 'L1_attn_Wq', 'L1_attn_Wk',
        'L1_attn_Wv', 'L1_attn_Wo', 'L1_attn_bo', 'L1_attn_betas', 'L1_attn_mem', 'L1_attn_z',
        'L1_ffn_Wqkv', 'L1_ffn_q_scale', 'L1_ffn_k_scale', 'L1_ffn_Wo', 'L1_ffn_ln_g', 'L1_ffn_ln_b',
        'L1_ffn_W1', 'L1_ffn_b1', 'L1_ffn_W2', 'L1_ffn_b2', 'L1_c', 'L1_wmod']


def kernel(**inputs):
    import concourse.bacc as _bacc
    from concourse.bass_utils import run_bass_kernel_spmd as _run

    nc = _bacc.Bacc("TRN2", target_bir_lowering=False, num_devices=1)
    arrays, aps = {}, {}
    for name, a in [(n, inputs[n]) for n in _INS] + list(shape_constants().items()):
        a = np.ascontiguousarray(a)
        arrays[f"in_{name}"] = a
        aps[name] = nc.dram_tensor(f"in_{name}", a.shape, mybir.dt.from_np(a.dtype), kind="ExternalInput").ap()
    out = nc.dram_tensor("out_x", (B, S, P), F32, kind="ExternalOutput").ap()
    build(nc, aps, out)
    r = _run(nc, [arrays], core_ids=[0])
    return r.results[0]["out_x"]
```

```python
import math
from contextlib import ExitStack

import numpy as np

import concourse.bass as bass
from concourse import mybir

F32 = mybir.dt.float32
BF16 = mybir.dt.bfloat16
ALU = mybir.AluOpType
ACT = mybir.ActivationFunctionType
AX = mybir.AxisListType

P = 128
B = 4
S = 512
T = S // P
EPS = 1e-5
BIG = -1e30

H0, D0 = 16, 8
NE, FH = 8, 256
H1, D1 = 4, 32
DEPTH, HL, DL, WIN = 6, 16, 64, 32
INNER = HL * DL
PAIRS = HL // 2
DI = int(P * 4 * 2 / 3)
CH = [(0, P), (P, P), (2 * P, DI - 2 * P)]
FFC = len(CH)
PADH = 32

NMOD = 12
SA, CA, GA, SB, CB, GB = range(6)


def shape_constants():
    f = np.float32
    p = np.arange(P)
    ident = np.eye(P, dtype=f)
    d = np.arange(S)[None, :] - (S - P + p)[:, None]
    alibi = np.where(d <= 0, d, BIG).astype(f)
    causal = np.where(d <= 0, 0.0, BIG).astype(f)
    hm0 = (p[:, None] // D0 == np.arange(H0)[None, :]).astype(f) / f(np.sqrt(D0))
    hm1 = (p[:, None] // D1 == np.arange(H1)[None, :]).astype(f)
    i = (p % WIN)[:, None]
    j = np.arange(2 * WIN)[None, :]
    ok = (i <= j) & (j <= i + WIN)
    first = ok & ~((p[:, None] < WIN) & (j < WIN))
    wmask = np.stack([np.where(ok, 0.0, BIG), np.where(first, 0.0, BIG)], 1).astype(f)
    half = np.arange(0, DL, 2, dtype=f)
    inv_freq = f(1.0) / f(10000.0) ** (half / f(DL))
    t = np.arange(S, dtype=f)
    fr = t[:, None] * inv_freq[None, :]
    fr = np.concatenate([fr, fr], -1)
    base = (half + f(0.4 * DL)) / f(1.4 * DL)
    power = (t - S // 2) / f(WIN // 2)
    sc = base[None, :] ** power[:, None]
    sc = np.concatenate([sc, sc], -1)
    sign = np.where(np.arange(DL) < DL // 2, -1.0, 1.0).astype(f)
    c, s = np.cos(fr), np.sin(fr) * sign
    inv = f(1.0) / sc
    rot = np.stack([c * sc, s * sc, c * inv, s * inv], 0)
    rot = rot.reshape(4, T, P, DL).transpose(2, 0, 1, 3).astype(f)
    rev = np.broadcast_to(np.arange(NE, 0, -1, dtype=f), (P, T, NE))
    return {
        "ident": ident, "alibi": alibi, "causal": causal, "hm0": hm0, "hm1": hm1,
        "wmask": wmask, "rot": np.ascontiguousarray(rot), "rev": np.ascontiguousarray(rev),
    }


class Chain:

    def __init__(self, eng, sem, base=0):
        self.eng, self.sem, self.base, self.n = eng, sem, base, 0

    def do(self, ins):
        self.mark(ins)
        self.settle()

    def mark(self, ins):
        ins.then_inc(self.sem, 1)
        self.n += 1

    def settle(self):
        self.eng.wait_ge(self.sem, self.base + self.n)


DVE_A = 32




def build(nc, ins, out):
    ctx = ExitStack()
    with ctx:
        def sb(name, shape, dt=F32):
            return ctx.enter_context(nc.sbuf_tensor(name, shape, dt))

        def sem(name):
            return ctx.enter_context(nc.semaphore(name))

        ident = sb("ident", [P, P])
        identb = sb("identb", [P, P], BF16)
        alibi = sb("alibi", [P, S])
        causal = sb("causal", [P, S])
        hm = [sb("hm0", [P, H0]), sb("hm1", [P, H1])]
        wmask = sb("wmask", [P, 2, 2 * WIN])
        wmaskb = sb("wmaskb", [P, 2, 2 * WIN], BF16)
        rot = sb("rot", [P, 4, T, DL])
        rev = sb("rev", [P, T, NE])
        half_neg = sb("half_neg", [P, 32])
        wT = sb("wT", [P, 8, P])
        bqkv = sb("bqkv", [P, 3])
        bv = sb("bv", [P, P])
        bout = sb("bout", [P, 2])
        wg = sb("wg", [P, NE])
        mw1 = sb("mw1", [P, NE, FH])
        mw2 = sb("mw2", [P, NE, 2, P])
        mb1 = sb("mb1", [P, NE, 2])
        mb2 = sb("mb2", [NE, P])
        cT = sb("cT", [P, 2, B])
        cw = sb("cw", [P, 3, 2, B])
        modT = sb("modT", [P, B, NMOD])
        gsgn = sb("gsgn", [P, B, NMOD])
        gneg = sb("gneg", [P, B, NMOD])
        mcur = sb("mcur", [P, NMOD])
        memz = sb("memz", [P, P + H1])
        beta = sb("beta", [P, 3, H1])
        wqkv = sb("wqkv", [P, 3 * INNER])
        wo = sb("wo", [P, PAIRS, P])
        w1 = sb("w1", [P, 2 * DI])
        w2 = sb("w2", [P, FFC, P])
        qks = sb("qks", [P, 2, DEPTH, DL])
        lcol = sb("lcol", [P, DEPTH, 9])
        lcur = sb("lcur", [P, 9])
        rtab = sb("rtab", [P, 4, T, DL])
        XT = sb("XT", [P, B * S])
        YT = sb("YT", [P, B * S])
        xcur = sb("xcur", [P, S])
        hT = sb("hT", [P, S])
        xn = sb("xn", [P, T, P])
        stats = sb("stats", [P, T, 6])
        mv = sb("mv", [P, T, 2])
        rstd = sb("rstd", [P, T])
        tmp = sb("tmp", [P, S])

        ARENA = 31700
        arena = sb("arena", [P, ARENA])

        class Area:

            def __init__(self):
                self.at = 0

            def take(self, *shape, part=P):
                n = int(np.prod(shape))
                v = arena[0:part, self.at:self.at + n]
                self.at += n
                assert self.at <= ARENA, self.at
                if len(shape) == 2:
                    v = v.rearrange("p (a b) -> p a b", b=shape[1])
                if len(shape) == 3:
                    v = v.rearrange("p (a b c) -> p a b c", b=shape[1], c=shape[2])
                return v

        a = Area()
        xtok = a.take(T, P)
        Qm = a.take(2, S)
        qTs = a.take(S)
        kTs = a.take(S)
        Vh = a.take(T, H0, PADH)
        Ssb = a.take(2, S)
        Pr = a.take(4, S)
        PTh = a.take(2, T, S)
        nmax = a.take(H0 * T)
        rsum = a.take(H0, T)
        rinv = a.take(H0, T)
        OTs = a.take(S)
        Otok = a.take(T, P)
        Am = a.take(T, P)
        den = a.take(T, H1)
        oTs = a.take(S)
        sqT = a.take(S)
        eq_ = a.take(S)
        hes = a.take(2, 2, S)
        hsc = a.take(2, 2, S)
        setup = Area()
        setup.at = a.at - 8 * S
        wnat = setup.take(8, P)
        wmod = setup.take(2, 6 * P)
        rt = a.take(12, T * NE)
        rs4 = a.take(6, T)
        sT = a.take(S)

        a = Area()
        xsA, xsF = tmp, xcur
        ra = a.take(2, INNER)
        rb = a.take(2, INNER)
        sq = a.take(2, S)
        ss = a.take(2, HL)
        rr = a.take(2, HL)
        Vt = a.take(T, INNER)
        Vp = a.take(2, INNER)
        qT = a.take(PAIRS, P)
        kT = a.take(PAIRS, WIN + S)
        Tm = a.take(HL, 2 * WIN)
        Ex = a.take(HL, 2 * WIN)
        mx = a.take(HL)
        sm = a.take(HL)
        ri = a.take(HL)
        Bd = a.take(HL, WIN + P)
        PT = a.take(HL, P)
        PTp = a.take(2, HL * WIN)
        oT = a.take(PAIRS, S)
        ge = a.take(FFC, S)
        fa = a.take(FFC, S)

        pj = ctx.enter_context(nc.psum_tensor("pj", [P, 2, S], F32))
        tr = ctx.enter_context(nc.psum_tensor("tr", [P, 2, S], F32))
        sc = ctx.enter_context(nc.psum_tensor("sc", [P, 2, S], F32))
        oo = ctx.enter_context(nc.psum_tensor("oo", [P, 2, S], F32))
        SBANK = [pj[:, 0], pj[:, 1], sc[:, 0]]
        TBANK = [tr[:, 0], tr[:, 1], sc[:, 1]]

        ld_const = sem("ld_const")
        ld_x = sem("ld_x")
        ld_qkv, ld_wo, ld_ff = sem("ld_qkv"), sem("ld_wo"), sem("ld_ff")
        ld_vp = sem("ld_vp")
        st_out = sem("st_out")
        dve_c, act_c, pool_c = sem("dve_c"), sem("act_c"), sem("pool_c")
        zeroed, passed = sem("zeroed"), sem("passed")
        set_tr = sem("set_tr")
        set_ev = sem("set_ev")
        silu_e, silu_d = sem("silu_e"), sem("silu_d")
        sig_e = sem("sig_e")
        x_tr, x_in = sem("x_tr"), sem("x_in")
        mod_cur = sem("mod_cur")
        ln_in, ln_var, ln_rstd, ln_norm, ln_back, ln_out = (
            sem("ln_in"), sem("ln_var"), sem("ln_rstd"), sem("ln_norm"), sem("ln_back"), sem("ln_out"))
        qk_mm, qk_ev, v_mm, v_ev = sem("qk_mm"), sem("qk_ev"), sem("v_mm"), sem("v_ev")
        q_masked = sem("q_masked")
        scores, biased, probs, p_tr, pe_dve, pe_act, pv_done = (
            sem("scores"), sem("biased"), sem("probs"), sem("p_tr"), sem("pe_dve"), sem("pe_act"),
            sem("pv_done"))
        o_copied, o_tr, o_tok = sem("o_copied"), sem("o_tr"), sem("o_tok")
        of_tr, of_ev, prj, x_add = sem("of_tr"), sem("of_ev"), sem("prj"), sem("x_add")
        elu_m, elu_e, elu_s, mem_mm, mixed = (
            sem("elu_m"), sem("elu_e"), sem("elu_s"), sem("mem_mm"), sem("mixed"))
        lg_mm, lg_sub, lg_exp, routed, s_tr, s_ev = (
            sem("lg_mm"), sem("lg_sub"), sem("lg_exp"), sem("routed"), sem("s_tr"), sem("s_ev"))
        m_h, m_relu, m_bc, m_sc, m_y = (
            sem("m_h"), sem("m_relu"), sem("m_bc"), sem("m_sc"), sem("m_y"))
        y_in = sem("y_in")
        xs_a, tabs = sem("xs_a"), sem("tabs")
        pj_mm, sq_ev, rot_ev, ss_ok, qk_rdy, v_cp = (
            sem("pj_mm"), sem("sq_ev"), sem("rot_ev"), sem("ss_ok"), sem("qk_rdy"), sem("v_cp"))
        qk_tr, qk_cp, sc_mm, t_sub, e_exp, bd_dve, bd_pool, ptp_ok, ri_ok = (
            sem("qk_tr"), sem("qk_cp"), sem("sc_mm"), sem("t_sub"), sem("e_exp"), sem("bd_dve"),
            sem("bd_pool"), sem("ptp_ok"), sem("ri_ok"))
        pt_tr, pt_cp, o_mm, o_cp, wo_mm, y_att, xs_f = (
            sem("pt_tr"), sem("pt_cp"), sem("o_mm"), sem("o_cp"), sem("wo_mm"), sem("y_att"), sem("xs_f"))
        w1_mm, gelu_ev, ff_ev, w2_mm, y_ff = (
            sem("w1_mm"), sem("gelu_ev"), sem("ff_ev"), sem("w2_mm"), sem("y_ff"))
        lnb_in, lnb_var, lnb_rstd, lnb_norm, lnb_back, lnb_out = (
            sem("lnb_in"), sem("lnb_var"), sem("lnb_rstd"), sem("lnb_norm"), sem("lnb_back"), sem("lnb_out"))
        lc_ok = sem("lc_ok")
        x_fin, f_tr, f_cp = sem("x_fin"), sem("f_tr"), sem("f_cp")
        ln_bn, ln_ag, lnb_bn, lnb_ag = sem("ln_bn"), sem("ln_ag"), sem("lnb_bn"), sem("lnb_ag")
        mx_ok, sm_ok, r_ok, sum_ok, bd_half = (
            sem("mx_ok"), sem("sm_ok"), sem("r_ok"), sem("sum_ok"), sem("bd_half"))
        LNA = (ln_in, ln_var, ln_rstd, ln_norm, ln_back, ln_out, ln_bn, ln_ag)
        LNB = (lnb_in, lnb_var, lnb_rstd, lnb_norm, lnb_back, lnb_out, lnb_bn, lnb_ag)
        LNA_BANKS = (tr[:, 0], tr[:, 1])
        LNB_BANKS = (pj[:, 0], pj[:, 1])

        def wait(eng, s_, v_):
            if not (isinstance(v_, int) and v_ <= 0):
                eng.wait_ge(s_, v_)

        def apart(eng):
            eng.sem_inc(passed, 1)

        block = ctx.enter_context(nc.Block())
        N_CONST = []

        @block.sync
        def _(sp):
            def load(dst, src):
                sp.dma_start(dst, src, allow_slow_non_contiguous=True).then_inc(ld_const, 16)
                N_CONST.append(1)

            for name, dst in (("ident", ident), ("alibi", alibi), ("causal", causal), ("hm0", hm[0]),
                              ("hm1", hm[1]), ("wmask", wmask), ("rot", rot), ("rev", rev)):
                src = ins[name]
                load(dst[tuple(slice(None) for _ in src.shape)], src)
            load(wnat[:, 0:3, :], ins["L0_attn_w_qkv"].rearrange("(a n) k -> n a k", a=3))
            for k, n in enumerate(("L0_attn_w_out", "L1_attn_Wq", "L1_attn_Wk", "L1_attn_Wv", "L1_attn_Wo")):
                load(wnat[:, 3 + k, :], ins[n])
            load(bqkv[:, :], ins["L0_attn_b_qkv"].rearrange("(a n) -> n a", a=3))
            load(bv[:, :], ins["L0_attn_b_qkv"][2 * P:3 * P].partition_broadcast(P))
            load(bout[:, 0:1], ins["L0_attn_b_out"].unsqueeze(1))
            load(bout[:, 1:2], ins["L1_attn_bo"].unsqueeze(1))
            load(wg[:, :], ins["L0_ffn_Wg"])
            load(mw1[:, :, :], ins["L0_ffn_W1"].rearrange("e k h -> k e h"))
            load(mw2[:, :, :, :], ins["L0_ffn_W2"].rearrange("e (c k) n -> k e c n", c=2))
            for c in range(2):
                load(mb1[:, :, c], ins["L0_ffn_b1"][:, c * P:(c + 1) * P].rearrange("e k -> k e"))
            load(mb2[:, :], ins["L0_ffn_b2"])
            for k in range(2):
                load(cT[:, k, :], ins[f"L{k}_c"].rearrange("b k -> k b"))
                load(wmod[:, k, :], ins[f"L{k}_wmod"])
            load(beta[:, 0, :], ins["L1_attn_betas"].rearrange("a h b c -> (a h b c)").partition_broadcast(P))
            sp.wait_ge(zeroed, 2)
            for h in range(H1):
                load(memz[h * D1:(h + 1) * D1, h * D1:(h + 1) * D1], ins["L1_attn_mem"][h])
                load(memz[h * D1:(h + 1) * D1, P + h:P + h + 1], ins["L1_attn_z"][h])
            load(qks[:, 0, :, :], ins["L1_ffn_q_scale"].partition_broadcast(P))
            load(qks[:, 1, :, :], ins["L1_ffn_k_scale"].partition_broadcast(P))
            for k, n in enumerate(("L1_ffn_ln_g", "L1_ffn_ln_b", "L1_ffn_b2")):
                load(lcol[:, :, k], ins[n].rearrange("l k -> k l"))
            for k, (o, n) in enumerate(CH):
                for part in range(2):
                    load(lcol[0:n, :, 3 + 3 * part + k],
                         ins["L1_ffn_b1"][:, part * DI + o:part * DI + o + n].rearrange("l k -> k l"))
            x_v = ins["L0_attn_x"].rearrange("b (t p) k -> b p t k", p=P)
            with sp.Fori(0, B) as b:
                sp.wait_ge(x_tr, b + 1)
                sp.dma_start(xtok, x_v[bass.ds(b, 1)].rearrange("a p t k -> (a p) t k")).then_inc(ld_x, 16)
            w_v = ins["L1_ffn_Wo"].rearrange("l (p k) n -> l k p n", k=P)

            def qkv_weights(l):
                wait(sp, pj_mm, l * (6 * T * B))
                sp.dma_start(wqkv[:, :], ins["L1_ffn_Wqkv"][bass.ds(l, 1)].rearrange("a k n -> (a k) n")
                             ).then_inc(ld_qkv, 16)

            def other_weights(l):
                wait(sp, wo_mm, l * B)
                sp.dma_start(wo[:, :, :], w_v[bass.ds(l, 1)].rearrange("a k p n -> (a k) p n")
                             ).then_inc(ld_wo, 16)
                wait(sp, w2_mm, l * B)
                sp.dma_start(w1[:, :], ins["L1_ffn_W1"][bass.ds(l, 1)].rearrange("a k n -> (a k) n")
                             ).then_inc(ld_ff, 16)
                for k, (o, n) in enumerate(CH):
                    sp.dma_start(w2[0:n, k, :],
                                 ins["L1_ffn_W2"][bass.ds(l, 1), o:o + n, :].rearrange("a k n -> (a k) n")
                                 ).then_inc(ld_ff, 16)

            def move_ends(n):
                for t in range(T - 1):
                    g = n * T + t
                    wait(sp, v_cp, g * 2 + 2)
                    wait(sp, o_mm, g)
                    wait(sp, ld_vp, (n * (T - 1) + t) * 16)
                    sp.dma_start(Vp[0:WIN, (t + 1) % 2, :], Vt[P - WIN:P, t, :]).then_inc(ld_vp, 16)

            qkv_weights(0)
            other_weights(0)
            move_ends(0)
            with sp.Fori(1, B) as b:
                move_ends(b)
            with sp.Fori(1, DEPTH) as l:
                qkv_weights(l)
                move_ends(l * B)
                other_weights(l)
                with sp.Fori(1, B) as b:
                    move_ends(l * B + b)
            out_v = out.rearrange("b (t p) k -> b p t k", p=P)
            with sp.Fori(0, B) as b:
                sp.wait_ge(f_cp, b + 1)
                sp.dma_start(out_v[bass.ds(b, 1)].rearrange("a p t k -> (a p) t k"), xn[:, :, :]
                             ).then_inc(st_out, 16)
            sp.wait_ge(st_out, 16 * B)

        n_const = 16 * len(N_CONST)
        NB = DEPTH * B
        NTILE = NB * T
        ORDER = (0, 2, 1, 3)

        class Slot:

            def __init__(self, n, t, l, b, m, lm=None, ym=None, new=True, c_=True, d_=True):
                self.args = (n, t, new, c_, d_, m, lm)
                self.l, self.b, self.ym = l, b, ym
                self.starts = new and t == 0 and isinstance(b, int)

        def run_slots(eng, slot):
            for t in range(T):
                slot(Slot(0, t, 0, 0, m=None, c_=t >= 1, d_=t >= 2))
            with eng.Fori(1, B) as b:
                for t in range(T):
                    slot(Slot(b, t, 0, b, m=b - 1, lm=0, ym=b - 1))
            with eng.Fori(1, DEPTH) as l:
                for t in range(T):
                    slot(Slot(l * B, t, l, 0, m=l * B - 1, lm=l - 1, ym=B - 1))
                with eng.Fori(1, B) as b:
                    for t in range(T):
                        slot(Slot(l * B + b, t, l, b, m=l * B + b - 1, lm=l, ym=b - 1))
            for t in range(T):
                slot(Slot(NB, t, DEPTH, 0, m=NB - 1, lm=DEPTH - 1, ym=B - 1, new=False, c_=t < 1, d_=t < 2))

        @block.tensor
        def _(pe):
            def mm(o, l, r, start=True, stop=True, **k):
                return nc.tensor.matmul(o, l, r, start=start, stop=stop, **k)

            def tp(o, i):
                return nc.tensor.transpose(o, i, ident[0:i.shape[0], 0:i.shape[0]])

            def norm_in(sems, bank, src):
                for t in range(T):
                    last = tp(bank[:, t * P:(t + 1) * P], src[:, t * P:(t + 1) * P])
                last.then_inc(sems[0], 1)

            def norm_back(sems, bank, k):
                pe.wait_ge(sems[3], k + 1)
                for t in range(T):
                    last = tp(bank[:, t * P:(t + 1) * P], xn[:, t, :])
                last.then_inc(sems[4], 1)

            def layer_norm(k, src):
                norm_in(LNA, LNA_BANKS[0], src)
                norm_back(LNA, LNA_BANKS[1], k)

            pe.wait_ge(ld_const, n_const)
            for g in range(2):
                for k in range(4):
                    last = tp(tr[:, g, k * P:(k + 1) * P], wnat[:, 4 * g + k, :])
                last.then_inc(set_tr, 1)
            pe.wait_ge(silu_d, 1)
            for k in range(2):
                for j in range(6):
                    last = mm(pj[:, 0, (6 * k + j) * B:(6 * k + j + 1) * B],
                              wmod[:, k, j * P:(j + 1) * P], cw[:, 2, k, :])
            last.then_inc(set_tr, 1)
            pe.wait_ge(set_ev, 3)

            def attention(b, k):
                nh, wk = (H0, H1)[k], 4 * k
                hb = b * (H0 + H1) + k * H0
                sbs = hb * T
                gb = b * 5 + k * 4
                ab = b * 2 + k
                pe.wait_ge(ln_out, b * 3 + 2 * k + 1)
                for j in range(2):
                    mm(pj[:, j], wT[:, wk + j, :], hT[:, :]).then_inc(qk_mm, 1)
                for t in range(T):
                    last = mm(sc[:, 0, t * P:(t + 1) * P], hT[:, t * P:(t + 1) * P], wT[:, wk + 2, :])
                last.then_inc(v_mm, 1)
                pe.wait_ge(qk_ev, ab * 2 + 2)
                pe.wait_ge(v_ev, ab + 1)
                if k == 1:
                    pe.wait_ge(elu_s, b + 1)
                    for t in range(T):
                        last = mm(oo[:, t // 2, (t % 2) * (P + H1):(t % 2 + 1) * (P + H1)],
                                  sqT[:, t * P:(t + 1) * P], memz[:, :])
                    last.then_inc(mem_mm, 1)
                    pe.wait_ge(mixed, b * 2 + 1)

                def group_out(g):
                    pe.wait_ge(o_copied, gb + g + 1)
                    for t in range(T):
                        last = tp(oo[:, g % 2, t * P:(t + 1) * P], OTs[:, t * P:(t + 1) * P])
                    last.then_inc(o_tr, 1)

                for h in range(nh + 1):
                    if h < nh:
                        pe.wait_ge(q_masked, hb + h + 1)
                    for i in range(T):
                        if h < nh:
                            n = T * h + i
                            if n >= 3:
                                pe.wait_ge(biased, sbs + n - 2)
                            mm(SBANK[n % 3][:, 0:(i + 1) * P], Qm[:, h % 2, i * P:(i + 1) * P],
                               kTs[:, 0:(i + 1) * P]).then_inc(scores, 1)
                        if h >= 1:
                            n = T * (h - 1) + i
                            pe.wait_ge(probs, sbs + n + 1)
                            if n >= 3:
                                hh, ii = divmod(n - 3, T)
                                pe.wait_ge((pe_act, pe_dve)[ii % 2], (hb + hh) * 2 + ii // 2 + 1)
                            for j in range(i + 1):
                                last = tp(TBANK[n % 3][:, j * P:(j + 1) * P],
                                          Pr[:, n % 4, j * P:(j + 1) * P])
                            last.then_inc(p_tr, 1)
                    if h >= 1:
                        hh = h - 1
                        g = hh // 4
                        pe.wait_ge(pe_act, (hb + hh) * 2 + 2)
                        pe.wait_ge(pe_dve, (hb + hh) * 2 + 2)
                        if hh % 4 == 0 and g >= 2:
                            pe.wait_ge(o_tok, gb + g - 1)
                        q = 32 * (hh % 4)
                        for j in range(T):
                            last = mm(oo[q:q + 32, g % 2, j * P:S], Vh[:, j, hh, :], PTh[:, hh % 2, j, j * P:S],
                                      start=(j == 0), stop=(j == T - 1))
                        last.then_inc(pv_done, 1)
                        if hh % 4 == 0 and g >= 1:
                            group_out(g - 1)
                group_out(nh // 4 - 1)
                pe.wait_ge(o_tok if k == 0 else mixed, gb + 4 if k == 0 else b * 2 + 2)
                for t in range(T):
                    last = tp(tr[:, 0, t * P:(t + 1) * P], Otok[:, t, :])
                last.then_inc(of_tr, 1)
                pe.wait_ge(of_ev, ab + 1)
                mm(pj[:, 0], wT[:, 4 * k + 3, :], oTs[:, :]).then_inc(prj, 1)
                pe.wait_ge(x_add, b * 3 + 2 * k + 1)

            def experts(b):
                pe.wait_ge(ln_out, b * 3 + 2)
                for t in range(T):
                    last = mm(tr[:, 0, t * NE:(t + 1) * NE], hT[:, t * P:(t + 1) * P], wg[:, :])
                last.then_inc(lg_mm, 1)

                def up(e):
                    for c in range(2):
                        if e >= 1:
                            pe.wait_ge(m_relu, (b * NE + e) * 2 - 1 + c)
                        mm(pj[:, c], mw1[:, e, c * P:(c + 1) * P], hT[:, :]).then_inc(m_h, 1)

                def spread(e):
                    if e >= 2:
                        pe.wait_ge(m_sc, b * NE + e - 1)
                    for t in range(T):
                        w = rt[:, 11, t * NE + e:t * NE + e + 1].broadcast_to([P, P])
                        last = tp(tr[:, e % 2, t * P:(t + 1) * P], w)
                    last.then_inc(m_bc, 1)

                def down(e):
                    pe.wait_ge(m_sc, b * NE + e + 1)
                    for c in range(2):
                        last = mm(oo[:, 0], mw2[:, e, c, :], hsc[:, e % 2, c, :], start=False,
                                  stop=(e == NE - 1 and c == 1))
                    last.then_inc(m_y, 1)

                up(0)
                pe.wait_ge(routed, b + 1)
                for t in range(T):
                    last = tp(sc[0:NE, 0, t * P:(t + 1) * P], rt[:, 11, t * NE:(t + 1) * NE])
                last.then_inc(s_tr, 1)
                spread(0)
                pe.wait_ge(s_ev, b + 1)
                mm(oo[:, 0], mb2[:, :], sT[0:NE, :], stop=False)
                for e in range(1, NE):
                    up(e)
                    spread(e)
                    down(e - 1)
                down(NE - 1)
                pe.wait_ge(x_add, b * 3 + 2)

            pe.sem_inc(x_tr, 1)
            with pe.Fori(0, B) as b:
                pe.wait_ge(ld_x, b * 16 + 16)
                for t in range(T):
                    last = tp(tr[:, 0, t * P:(t + 1) * P], xtok[:, t, :])
                last.then_inc(x_tr, 1)
                pe.wait_ge(x_in, b + 1)
                layer_norm(b * 4, xcur)
                attention(b, 0)
                layer_norm(b * 4 + 1, xcur)
                experts(b)
                layer_norm(b * 4 + 2, xcur)
                attention(b, 1)
                layer_norm(b * 4 + 3, xcur)
                pe.wait_ge(y_in, b + 2)

            def project(g, t, c):
                if c >= 4:
                    pe.wait_ge(rot_ev, g * 4 + c - 3)
                elif c >= 2:
                    pe.wait_ge(v_cp, g * 2 + c - 1)
                else:
                    wait(pe, rot_ev, g * 4)
                col = [4, 5, 0, 1, 2, 3][c] * S
                mm(pj[:, c % 2], xsA[:, t * P:(t + 1) * P], wqkv[:, col:col + S]).then_inc(pj_mm, 1)

            def turn(g, j):
                pe.wait_ge(qk_rdy, g * 2 + j // 2 + 1)
                if j >= 2:
                    pe.wait_ge(qk_cp, g * 4 + j - 1)
                for u in range(4):
                    pr = 4 * (j % 2) + u
                    last = tp(tr[:, j % 2, u * P:(u + 1) * P], ra[:, j // 2, pr * P:(pr + 1) * P])
                last.then_inc(qk_tr, 1)

            def window_scores(g, t, u):
                pe.wait_ge(qk_cp, g * 4 + 4)
                wait(pe, t_sub, g)
                mm(sc[:, u].rearrange("p (a b) -> p a b", b=2 * WIN), identb[:, :],
                   wmaskb[:, 1 if t == 0 else 0, :].unsqueeze(1).broadcast_to([P, PAIRS, 2 * WIN]),
                   stop=False, skip_group_check=True)
                d = slice(u * DL, (u + 1) * DL)
                for pr in range(PAIRS):
                    for w in range(P // WIN):
                        last = mm(sc[w * WIN:(w + 1) * WIN, u, pr * 2 * WIN:(pr + 1) * 2 * WIN],
                                  qT[d, pr, w * WIN:(w + 1) * WIN],
                                  kT[d, pr, t * P + w * WIN:t * P + (w + 2) * WIN],
                                  start=False, stop=True, skip_group_check=True)
                last.then_inc(sc_mm, 1)

            def turn_probs(g, j):
                pe.wait_ge(bd_dve, g + 1)
                pe.wait_ge(bd_pool, g + 1)
                if j < 2 and isinstance(g, int) and g + 1 >= NTILE:
                    pe.wait_ge(pt_cp, g * 4 + j - 1)
                elif j < 2:
                    pe.wait_ge(qk_cp, (g + 1) * 4 + 3 + j)
                else:
                    pe.wait_ge(pt_cp, g * 4 + j - 1)
                for u in range(4):
                    h = 4 * ORDER[j] + u
                    last = tp(tr[:, j % 2, u * P:(u + 1) * P], Bd[:, h, WIN:WIN + P])
                last.then_inc(pt_tr, 1)

            def values(g, n, t):
                if t > 0:
                    pe.wait_ge(ptp_ok, n * (T - 1) + t)
                    pe.wait_ge(ld_vp, (n * (T - 1) + t) * 16)
                wait(pe, o_cp, g)
                for pr in range(PAIRS):
                    if pr % 4 == 0:
                        pe.wait_ge(pt_cp, g * 4 + pr // 2 + 2)
                    for u in range(2):
                        j, f = u * PAIRS + pr, (2 * pr + u) * DL
                        d = slice(u * DL, (u + 1) * DL)
                        c = (pr % 4) * P
                        last = mm(oo[d, pr // 4, c:c + P], Vt[:, t, f:f + DL], PT[:, j, :],
                                  start=True, stop=(t == 0), skip_group_check=True)
                        if t > 0:
                            last = mm(oo[d, pr // 4, c:c + WIN], Vp[:, t % 2, f:f + DL],
                                      PTp[:, t % 2, j * WIN:(j + 1) * WIN],
                                      start=False, stop=True, skip_group_check=True)
                last.then_inc(o_mm, 1)

            def ff_up(m, k):
                o, w = CH[k]
                mm(pj[0:w, 0], w1[:, DI + o:DI + o + w], hT[:, :])
                mm(pj[0:w, 1], w1[:, o:o + w], hT[:, :]).then_inc(w1_mm, 1)

            def slot(s_):
                n, t, new, c_, d_, m, lm = s_.args
                g = n * T + t
                g1, t1 = g - 1, (t - 1) % T
                g2, t2, n2 = g - 2, (t - 2) % T, (n if t >= 2 else n - 1)
                if new:
                    if t == 0:
                        if s_.starts:
                            pe.wait_ge(ld_qkv, s_.l * 16 + 16)
                        pe.wait_ge(xs_a, n + 1)
                    if t == 3 and m is not None:
                        pe.wait_ge(lnb_out, m + 1)
                    for c in range(4):
                        project(g, t, c)
                if d_:
                    turn_probs(g2, 0)
                    turn_probs(g2, 1)
                if new:
                    project(g, t, 4)
                if c_:
                    window_scores(g1, t1, 0)
                if new:
                    project(g, t, 5)
                if d_:
                    turn_probs(g2, 2)
                    turn_probs(g2, 3)
                if c_:
                    window_scores(g1, t1, 1)
                if new:
                    for j in range(2):
                        if d_:
                            pe.wait_ge(pt_cp, g2 * 4 + 3 + j)
                        else:
                            wait(pe, qk_cp, (g * 4 - 1 + j) if g else 0)
                        turn(g, j)
                if m is not None and t >= 2:
                    pe.wait_ge(rot_ev, g * 4 + 4 if new else NTILE * 4)
                    if t == 2:
                        pe.wait_ge(xs_f, m + 1)
                        norm_in(LNB, LNB_BANKS[0], xsF)
                    else:
                        pe.wait_ge(lnb_out, m + 1)
                        pe.wait_ge(ld_ff, lm * 64 + 64)
                        ff_up(m, 0)
                if d_:
                    if m is not None and t == 2:
                        pe.wait_ge(y_att, m + 1)
                    if m is not None and t == 0:
                        pe.wait_ge(y_ff, m + 1)
                    values(g2, n2, t2)
                if m is not None and t == 2:
                    norm_back(LNB, LNB_BANKS[1], m)
                if m is not None and t == 3:
                    pe.wait_ge(ff_ev, m * FFC + 1)
                    ff_up(m, 1)
                if new:
                    turn(g, 2)
                    turn(g, 3)
                if m is not None and t == 1:
                    pe.wait_ge(o_cp, m * T + T)
                    pe.wait_ge(ld_wo, lm * 16 + 16)
                    for p_ in range(PAIRS):
                        last = mm(oo[:, 0], wo[:, p_, :], oT[:, p_, :], start=(p_ == 0), stop=(p_ == PAIRS - 1))
                    last.then_inc(wo_mm, 1)
                if m is not None and t == 3:
                    pe.wait_ge(ff_ev, m * FFC + 2)
                    ff_up(m, 2)
                    if d_:
                        pe.wait_ge(o_cp, g2 + 1)
                    for k, (o, w) in enumerate(CH):
                        pe.wait_ge(ff_ev, m * FFC + k + 1)
                        last = mm(oo[:, 0], w2[0:w, k, :], fa[0:w, k, :], start=(k == 0), stop=(k == FFC - 1))
                    last.then_inc(w2_mm, 1)

            run_slots(pe, slot)
            pe.wait_ge(y_ff, NB + 1)

            with pe.Fori(0, B) as b:
                pe.wait_ge(x_fin, b + 1)
                for t in range(T):
                    last = tp(tr[:, 0, t * P:(t + 1) * P], xcur[:, t * P:(t + 1) * P])
                last.then_inc(f_tr, 1)
                pe.wait_ge(f_cp, b + 1)

        @block.vector
        def _(ve):
            v = nc.vector

            def layer_norm(sems, bank, k):
                ve.wait_ge(sems[0], k + 1)
                for t in range(T):
                    last = v.bn_stats(stats[:, t, :], bank[:, t * P:(t + 1) * P])
                last.then_inc(sems[6], 1)
                ve.wait_ge(sems[6], k + 1)
                apart(ve)
                for t in range(T):
                    last = v.bn_aggr(mv[:, t, :], stats[:, t, :])
                last.then_inc(sems[7], 1)
                ve.wait_ge(sems[7], k + 1)
                v.tensor_scalar(rstd[:, :], mv[:, :, 1], EPS, None, ALU.add).then_inc(sems[1], 1)
                ve.wait_ge(sems[2], k + 1)
                for t in range(T):
                    last = v.tensor_scalar(xn[:, t, :], bank[:, t * P:(t + 1) * P], mv[:, t, 0:1],
                                           rstd[:, t:t + 1], ALU.subtract, ALU.mult)
                last.then_inc(sems[3], 1)

            ch = Chain(ve, dve_c)
            ve.wait_ge(ld_const, n_const)
            v.tensor_copy(identb[:, :], ident[:, :])
            ch.do(v.tensor_copy(wmaskb[:, :, :], wmask[:, :, :]))
            ve.wait_ge(silu_e, 2)
            ch.do(v.tensor_scalar(cw[:, 1], cw[:, 0], 1.0, None, ALU.add))
            ch.do(v.reciprocal(cw[:, 0], cw[:, 1]))
            v.tensor_tensor(cw[:, 2], cw[:, 0], cT[:, :, :], ALU.mult).then_inc(silu_d, 1)
            ch.do(v.tensor_scalar(beta[:, 2, :], beta[:, 1, :], 1.0, None, ALU.add))
            ch.do(v.reciprocal(beta[:, 1, :], beta[:, 2, :]))
            ch.do(v.tensor_scalar(beta[:, 2, :], beta[:, 1, :], -1.0, 1.0, ALU.mult, ALU.add))
            for g in range(2):
                ve.wait_ge(set_tr, g + 1)
                v.tensor_copy(wT[:, 4 * g:4 * g + 4, :], tr[:, g].rearrange("p (a b) -> p a b", b=P)
                              ).then_inc(set_ev, 1)
            ve.wait_ge(set_tr, 3)
            v.tensor_copy(modT[:, :, :], pj[:, 0, 0:NMOD * B].rearrange("p (j b) -> p b j", b=B)
                          ).then_inc(set_ev, 1)
            ve.wait_ge(set_ev, 3)
            for j in (CA, CB, 6 + CA, 6 + CB):
                v.tensor_scalar(modT[:, :, j], modT[:, :, j], 1.0, None, ALU.add)
            for j in (GA, GB, 6 + GA, 6 + GB):
                ins_ = v.tensor_scalar(gsgn[:, :, j], modT[:, :, j], 0.0, 2.0, ALU.is_ge, ALU.mult)
            ch.do(ins_)
            for j in (GA, GB, 6 + GA, 6 + GB):
                ins_ = v.tensor_scalar(gneg[:, :, j], modT[:, :, j], -1.0, 0.25, ALU.mult, ALU.max)
            ch.do(ins_)
            for j in (GA, GB, 6 + GA, 6 + GB):
                ins_ = v.tensor_tensor(modT[:, :, j], modT[:, :, j], gneg[:, :, j], ALU.max)
            ch.do(ins_)
            for j in (GA, GB, 6 + GA, 6 + GB):
                ins_ = v.scalar_tensor_tensor(out=modT[:, :, j], in0=gsgn[:, :, j], scalar=-1.0,
                                              in1=modT[:, :, j], op0=ALU.add, op1=ALU.mult)
            ch.do(ins_)
            dve_setup = ch.n

            def attention(b, k, ch):
                nh, d = (H0, H1)[k], (D0, D1)[k]
                hb = b * (H0 + H1) + k * H0
                sbs = hb * T
                gb = b * 5 + k * 4
                ab = b * 2 + k
                bias = (alibi, causal)[k]
                ve.wait_ge(v_mm, ab + 1)
                src = sc[:, 0].rearrange("p (t h d) -> p t h d", t=T, d=d)
                if k == 0:
                    ch.do(v.memset(Vh[:, :, :, :], 0.0))
                    for t in range(T):
                        ins_ = v.tensor_tensor(Vh[:, t, :, 0:d], src[:, t],
                                               bv[:, :].rearrange("p (h d) -> p h d", d=d), ALU.add)
                else:
                    ins_ = v.tensor_copy(Vh[:, :, 0:nh, :], src)
                ins_.then_inc(v_ev, 1)
                if k == 1:
                    ve.wait_ge(qk_ev, ab * 2 + 1)
                    v.tensor_scalar(eq_, qTs, 0.0, None, ALU.min).then_inc(elu_m, 1)
                    ve.wait_ge(elu_e, b + 1)
                    v.scalar_tensor_tensor(out=sqT, in0=qTs, scalar=0.0, in1=eq_, op0=ALU.max,
                                           op1=ALU.add).then_inc(elu_s, 1)
                    ve.wait_ge(mem_mm, b + 1)
                    for t in range(T):
                        z = (t % 2) * (P + H1) + P
                        ins_ = v.tensor_scalar(den[:, t, :], oo[:, t // 2, z:z + H1], 1e-6, None, ALU.add)
                    ch.do(ins_)
                    ch.do(v.reciprocal(den, den))
                    ch.do(v.tensor_tensor(den, den, beta[:, 1, :].unsqueeze(1).broadcast_to([P, T, H1]),
                                          ALU.mult))
                    for t in range(T):
                        z = (t % 2) * (P + H1)
                        ins_ = v.tensor_tensor(
                            Am[:, t, :].rearrange("p (h d) -> p h d", d=D1),
                            oo[:, t // 2, z:z + P].rearrange("p (h d) -> p h d", d=D1),
                            den[:, t, :].unsqueeze(2).broadcast_to([P, H1, D1]), ALU.mult)
                    ins_.then_inc(mixed, 1)

                def group_out(g):
                    ve.wait_ge(o_tr, gb + g + 1)
                    ch.do(v.reciprocal(rinv[:, 4 * g:4 * g + 4, :], rsum[:, 4 * g:4 * g + 4, :]))
                    o = Otok.rearrange("p t (h d) -> p t h d", d=d)[:, :, 4 * g:4 * g + 4, :]
                    i_ = oo[:, g % 2].rearrange("p (t h d) -> p t h d", t=T, d=PADH)[:, :, :, 0:d]
                    for t in range(T):
                        last = v.tensor_tensor(o[:, t], i_[:, t], rinv[:, 4 * g:4 * g + 4, t].unsqueeze(2)
                                               .broadcast_to([P, 4, d]), ALU.mult)
                    last.then_inc(o_tok, 1)

                for h in range(nh + 1):
                    for i in range(T):
                        if h < nh:
                            n = T * h + i
                            ve.wait_ge(scores, sbs + n + 1)
                            if n >= 2:
                                ve.wait_ge(probs, sbs + n - 1)
                            apart(ve)
                            w = (i + 1) * P
                            v.tensor_tensor_reduce(out=Ssb[:, n % 2, 0:w], in0=SBANK[n % 3][:, 0:w],
                                                   in1=bias[:, S - w:S], scale=-1.0, scalar=3e38,
                                                   op0=ALU.add, op1=ALU.min,
                                                   accum_out=nmax[:, n:n + 1]).then_inc(biased, 1)
                        if h >= 1 and i % 2 == 1:
                            n = T * (h - 1) + i
                            ve.wait_ge(p_tr, sbs + n + 1)
                            if h >= 3:
                                ve.wait_ge(pv_done, hb + h - 2)
                            w = (i + 1) * P
                            v.tensor_copy(PTh[:, (h - 1) % 2, 0:i + 1, i * P:(i + 1) * P],
                                          TBANK[n % 3][:, 0:w].rearrange("p (a b) -> p a b", b=P)
                                          ).then_inc(pe_dve, 1)
                    if h >= 6 and (h - 2) % 4 == 0:
                        group_out((h - 2) // 4 - 1)
                group_out(nh // 4 - 1)
                if k == 1:
                    ve.wait_ge(o_tok, gb + 1)
                    for t in range(T):
                        ins_ = v.tensor_tensor(Otok[:, t, :].rearrange("p (h d) -> p h d", d=D1),
                                               Otok[:, t, :].rearrange("p (h d) -> p h d", d=D1),
                                               beta[:, 2, :].unsqueeze(2).broadcast_to([P, H1, D1]), ALU.mult)
                    ch.do(ins_)
                    v.tensor_tensor(Otok, Otok, Am, ALU.add).then_inc(mixed, 1)
                ve.wait_ge(prj, ab + 1)
                g_ = 6 * k + GA
                ch.do(v.tensor_scalar(tmp[:, :], pj[:, 0], bout[:, k:k + 1], mcur[:, g_:g_ + 1],
                                      ALU.add, ALU.mult))
                v.tensor_tensor(xcur[:, :], xcur[:, :], tmp[:, :], ALU.add).then_inc(x_add, 1)

            def experts(b, ch):
                R = [rt[:, k].rearrange("p (t e) -> p t e", e=NE) for k in range(12)]

                def wide(k):
                    return rs4[:, k].unsqueeze(2).broadcast_to([P, T, NE])

                ve.wait_ge(lg_mm, b + 1)
                lg = tr[:, 0, 0:T * NE].rearrange("p (t e) -> p t e", e=NE)
                ch.do(v.tensor_reduce(rs4[:, 0], lg, AX.X, ALU.max))
                v.tensor_tensor(R[0], lg, wide(0), ALU.subtract).then_inc(lg_sub, 1)
                ve.wait_ge(lg_exp, b + 1)
                ch.do(v.tensor_reduce(rs4[:, 1], R[1], AX.X, ALU.add))
                ch.do(v.reciprocal(rs4[:, 2], rs4[:, 1]))
                ch.do(v.tensor_tensor(R[2], R[1], wide(2), ALU.mult))

                def pick(src, m, eq, key, first, s):
                    ch.do(v.tensor_reduce(rs4[:, m], R[src], AX.X, ALU.max))
                    ch.do(v.tensor_tensor(R[eq], R[src], wide(m), ALU.is_equal))
                    ch.do(v.tensor_tensor(R[key], R[eq], rev[:, :, :], ALU.mult))
                    ch.do(v.tensor_reduce(rs4[:, s], R[key], AX.X, ALU.max))
                    ch.do(v.tensor_tensor(R[first], rev[:, :, :], wide(s), ALU.is_equal))

                pick(2, 3, 3, 4, 5, 0)
                ch.do(v.scalar_tensor_tensor(out=R[6], in0=R[5], scalar=-2.0, in1=R[2], op0=ALU.mult,
                                             op1=ALU.add))
                pick(6, 4, 7, 8, 9, 1)
                v.tensor_tensor(R[10], R[5], R[9], ALU.add)
                ch.do(v.tensor_tensor(rs4[:, 5], rs4[:, 3], rs4[:, 4], ALU.add))
                ch.do(v.reciprocal(rs4[:, 5], rs4[:, 5]))
                ch.do(v.tensor_tensor(R[10], R[10], R[2], ALU.mult))
                v.tensor_tensor(R[11], R[10], wide(5), ALU.mult).then_inc(routed, 1)
                ve.wait_ge(s_tr, b + 1)
                v.tensor_copy(sT[0:NE, :], sc[0:NE, 0, :]).then_inc(s_ev, 1)
                for e in range(NE):
                    ve.wait_ge(m_relu, (b * NE + e) * 2 + 2)
                    ve.wait_ge(m_bc, b * NE + e + 1)
                    if e >= 2:
                        ve.wait_ge(m_y, b * NE + e - 1)
                    v.tensor_tensor(hsc[:, e % 2], hes[:, e % 2],
                                    tr[:, e % 2].unsqueeze(1).broadcast_to([P, 2, S]),
                                    ALU.mult).then_inc(m_sc, 1)
                ve.wait_ge(m_y, b * NE + NE)
                ch.do(v.tensor_scalar(tmp[:, :], oo[:, 0], mcur[:, GB:GB + 1], None, ALU.mult))
                v.tensor_tensor(xcur[:, :], xcur[:, :], tmp[:, :], ALU.add).then_inc(x_add, 1)

            with ve.Fori(0, B) as b:
                ch = Chain(ve, dve_c, b * DVE_A + dve_setup)
                ve.wait_ge(y_in, b + 1)
                v.tensor_copy(mcur[:, :].unsqueeze(1), modT[:, bass.ds(b, 1), :]).then_inc(mod_cur, 1)
                ve.wait_ge(mod_cur, b + 1)
                ve.wait_ge(x_tr, b + 2)
                v.tensor_copy(xcur[:, :], tr[:, 0]).then_inc(x_in, 1)
                layer_norm(LNA, LNA_BANKS[0], b * 4)
                attention(b, 0, ch)
                layer_norm(LNA, LNA_BANKS[0], b * 4 + 1)
                experts(b, ch)
                layer_norm(LNA, LNA_BANKS[0], b * 4 + 2)
                attention(b, 1, ch)
                ve.wait_ge(x_add, b * 3 + 3)
                ch.do(v.tensor_copy(XT[:, bass.ds(b * S, S)], xcur[:, :]))
                layer_norm(LNA, LNA_BANKS[0], b * 4 + 3)
                assert ch.n == DVE_A, ("DVE_A", ch.n)

            def rotate(g, t, c):
                k, hf = c // 2, c % 2
                ve.wait_ge(sq_ev, g * 4 + c + 1)
                src = pj[:, c % 2].rearrange("p (h u d) -> p h u d", u=2, d=DL // 2)
                tc_ = rtab[:, 2 * k, t, :].rearrange("p (u d) -> p u d", u=2)
                ts_ = rtab[:, 2 * k + 1, t, :].rearrange("p (u d) -> p u d", u=2)
                wide = [P, PAIRS, 2, DL // 2]
                co = slice(hf * S, (hf + 1) * S)
                v.tensor_tensor(ra[:, k, co].rearrange("p (h u d) -> p h u d", u=2, d=DL // 2), src,
                                tc_.unsqueeze(1).broadcast_to(wide), ALU.mult)
                v.tensor_tensor(rb[:, k, co].rearrange("p (h u d) -> p h u d", u=2, d=DL // 2),
                                src[:, :, ::-1, :], ts_.unsqueeze(1).broadcast_to(wide), ALU.mult
                                ).then_inc(rot_ev, 1)
                v.tensor_reduce(ss[:, k, hf * PAIRS:(hf + 1) * PAIRS],
                                sq[:, c % 2].rearrange("p (h d) -> p h d", d=DL), AX.X, ALU.add
                                ).then_inc(ss_ok, 1)

            def soft1(g):
                ve.wait_ge(sc_mm, g * 2 + 2)
                s_v = sc[:, :, :].rearrange("p u (a b) -> p (u a) b", b=2 * WIN)
                v.tensor_reduce(mx, s_v, AX.X, ALU.max).then_inc(mx_ok, 1)
                ve.wait_ge(mx_ok, g + 1)
                v.tensor_tensor(Tm, s_v, mx.unsqueeze(2).broadcast_to([P, HL, 2 * WIN]),
                                ALU.subtract).then_inc(t_sub, 1)

            def soft2(g, t):
                ve.wait_ge(e_exp, g + 1)
                v.tensor_reduce(sm, Ex, AX.X, ALU.add).then_inc(sm_ok, 1)
                ve.wait_ge(sm_ok, g + 1)
                v.reciprocal(ri, sm).then_inc(ri_ok, 1)
                ve.wait_ge(ri_ok, g + 1)
                wait(ve, pt_tr, g * 4)
                for w in range(2):
                    q = slice(w * WIN, (w + 1) * WIN)
                    last = v.tensor_tensor(Bd[q, :, w * WIN:(w + 2) * WIN], Ex[q],
                                           ri[q].unsqueeze(2).broadcast_to([WIN, HL, 2 * WIN]), ALU.mult)
                last.then_inc(bd_dve, 1)
                if t > 0:
                    ve.wait_ge(bd_dve, g + 1)
                    wait(ve, o_mm, g - 1)
                    v.transpose(PTp[0:WIN, t % 2, :].rearrange("p (a b) -> p a b", b=WIN),
                                Bd[0:WIN, :, 0:WIN]).then_inc(ptp_ok, 1)

            def tables(l):
                for k in range(2):
                    qv = qks[:, k, bass.ds(l, 1), :]
                    v.tensor_tensor(rtab[:, 2 * k], rot[:, 2 * k], qv.broadcast_to([P, T, DL]), ALU.mult)
                    for u in range(2):
                        h_ = slice(u * DL // 2, (u + 1) * DL // 2)
                        o_ = slice((1 - u) * DL // 2, (2 - u) * DL // 2)
                        last = v.tensor_tensor(rtab[:, 2 * k + 1, :, h_], rot[:, 2 * k + 1, :, h_],
                                               qks[:, k, bass.ds(l, 1), o_].broadcast_to([P, T, DL // 2]),
                                               ALU.mult)
                last.then_inc(tabs, 1)
                ve.wait_ge(tabs, l + 1)
                apart(ve)

            def ff_gate(m, k):
                w = CH[k][1]
                ve.wait_ge(gelu_ev, m * FFC + k + 1)
                v.scalar_tensor_tensor(out=fa[0:w, k, :], in0=pj[0:w, 1], scalar=lcur[0:w, 3 + k:4 + k],
                                       in1=ge[0:w, k, :], op0=ALU.add, op1=ALU.mult).then_inc(ff_ev, 1)

            def slot(s_):
                n, t, new, c_, d_, m, lm = s_.args
                g = n * T + t
                if s_.starts:
                    tables(s_.l)
                if new:
                    for c in range(4):
                        if c % 2 == 0:
                            wait(ve, qk_tr, g * 4 - 2 + c)
                        rotate(g, t, c)
                if c_:
                    soft1(g - 1)
                y = YT[:, bass.ds(s_.ym * S, S)] if m is not None else None
                if m is not None and t == 2:
                    v.tensor_copy(lcur[:, :].unsqueeze(1), lcol[:, bass.ds(lm, 1), :]).then_inc(lc_ok, 1)
                    ve.wait_ge(lc_ok, m + 1)
                    layer_norm(LNB, LNB_BANKS[0], m)
                if m is not None and t == 3:
                    ff_gate(m, 0)
                if c_:
                    soft2(g - 1, (t - 1) % T)
                if m is not None and t == 1:
                    ve.wait_ge(wo_mm, m + 1)
                    apart(ve)
                    v.tensor_tensor(y, oo[:, 0], y, ALU.add).then_inc(y_att, 1)
                if m is not None and t == 3:
                    ff_gate(m, 1)
                    ff_gate(m, 2)
                    ve.wait_ge(w2_mm, m + 1)
                    apart(ve)
                    v.scalar_tensor_tensor(out=y, in0=oo[:, 0], scalar=lcur[:, 2:3], in1=y,
                                           op0=ALU.add, op1=ALU.add).then_inc(y_ff, 1)

            ve.sem_inc(y_ff, 1)
            run_slots(ve, slot)
            ve.wait_ge(y_ff, NB + 1)

            def finish(b):
                ch = Chain(ve, dve_c, b * 2 + dve_setup + B * DVE_A)
                wait(ve, f_tr, b)
                ch.do(v.tensor_copy(mcur[:, :].unsqueeze(1), modT[:, bass.ds(b, 1), :]))
                ch.do(v.tensor_scalar(tmp[:, :], YT[:, bass.ds(b * S, S)], mcur[:, 6 + GB:7 + GB], None,
                                      ALU.mult))
                v.tensor_tensor(xcur[:, :], XT[:, bass.ds(b * S, S)], tmp[:, :], ALU.add).then_inc(x_fin, 1)
                ve.wait_ge(f_tr, b + 1)
                wait(ve, st_out, b * 16)
                v.tensor_copy(xn[:, :, :], tr[:, 0].rearrange("p (a b) -> p a b", b=P)).then_inc(f_cp, 1)

            finish(0)
            with ve.Fori(1, B) as b:
                finish(b)

        @block.scalar
        def _(ac):
            def act(o, i, f, **k):
                return nc.scalar.activation(o, i, f, **k)

            ac.wait_ge(ld_const, n_const)
            act(cw[:, 0], cT[:, :, :], ACT.Exp, scale=-1.0).then_inc(silu_e, 1)
            act(beta[:, 1, :], beta[:, 0, :], ACT.Exp, scale=-1.0).then_inc(silu_e, 1)

            def ln_finish(sems, bank, k, scale, bias, dst):
                ac.wait_ge(sems[4], k + 1)
                act(dst, bank, ACT.Identity, scale=scale, bias=bias).then_inc(sems[5], 1)

            def attention(b, k):
                nh = (H0, H1)[k]
                hb = b * (H0 + H1) + k * H0
                sbs = hb * T
                gb = b * 5 + k * 4
                ab = b * 2 + k
                for j in range(2):
                    ac.wait_ge(qk_mm, ab * 2 + j + 1)
                    dst = (qTs, kTs)[j]
                    if k == 0:
                        act(dst, pj[:, j], ACT.Identity, bias=bqkv[:, j:j + 1]).then_inc(qk_ev, 1)
                    else:
                        act(dst, pj[:, j], ACT.Copy).then_inc(qk_ev, 1)
                if k == 1:
                    ac.wait_ge(elu_m, b + 1)
                    act(eq_, eq_, ACT.Exp).then_inc(elu_e, 1)

                def group_out(g):
                    ac.wait_ge(pv_done, hb + 4 * g + 4)
                    if g >= 1:
                        ac.wait_ge(o_tr, gb + g)
                    act(OTs, oo[:, g % 2], ACT.Copy).then_inc(o_copied, 1)

                for h in range(nh + 1):
                    for i in range(T):
                        if h < nh:
                            n = T * h + i
                            w = (i + 1) * P
                            ac.wait_ge(biased, sbs + n + 1)
                        if h >= 1 and i % 2 == 0:
                            m = T * (h - 1) + i
                            ac.wait_ge(p_tr, sbs + m + 1)
                            if h >= 3:
                                ac.wait_ge(pv_done, hb + h - 2)
                            ww = (i + 1) * P
                            act(PTh[:, (h - 1) % 2, 0:i + 1, i * P:(i + 1) * P],
                                TBANK[m % 3][:, 0:ww].rearrange("p (a b) -> p a b", b=P), ACT.Copy
                                ).then_inc(pe_act, 1)
                        if h < nh:
                            if n >= 4:
                                ac.wait_ge(p_tr, sbs + n - 3)
                            act(Pr[:, n % 4, 0:w], Ssb[:, n % 2, 0:w], ACT.Exp, scale=-1.0,
                                bias=nmax[:, n:n + 1], accum_out=rsum[:, h, i:i + 1]).then_inc(probs, 1)
                    if h >= 4 and h % 4 == 1:
                        group_out(h // 4 - 1)
                group_out(nh // 4 - 1)
                ac.wait_ge(of_tr, ab + 1)
                act(oTs, tr[:, 0], ACT.Copy).then_inc(of_ev, 1)

            ac.sem_inc(y_in, 1)
            with ac.Fori(0, B) as b:
                ac.wait_ge(mod_cur, b + 1)
                ln_finish(LNA, LNA_BANKS[1], b * 4, mcur[:, CA:CA + 1], mcur[:, SA:SA + 1], hT[:, :])
                attention(b, 0)
                ln_finish(LNA, LNA_BANKS[1], b * 4 + 1, mcur[:, CB:CB + 1], mcur[:, SB:SB + 1], hT[:, :])
                ac.wait_ge(lg_sub, b + 1)
                act(rt[:, 1], rt[:, 0], ACT.Exp).then_inc(lg_exp, 1)
                for e in range(NE):
                    for c in range(2):
                        ac.wait_ge(m_h, (b * NE + e) * 2 + c + 1)
                        if e >= 2 and c == 0:
                            ac.wait_ge(m_sc, b * NE + e - 1)
                        act(hes[:, e % 2, c, :], pj[:, c], ACT.Relu, bias=mb1[:, e, c:c + 1]
                            ).then_inc(m_relu, 1)
                ln_finish(LNA, LNA_BANKS[1], b * 4 + 2, mcur[:, 6 + CA:7 + CA], mcur[:, 6 + SA:7 + SA], hT[:, :])
                attention(b, 1)
                ac.wait_ge(ln_back, b * 4 + 4)
                apart(ac)
                act(YT[:, bass.ds(b * S, S)], tr[:, 1], ACT.Identity, scale=mcur[:, 6 + CB:7 + CB],
                    bias=mcur[:, 6 + SB:7 + SB]).then_inc(y_in, 1)

            hp = P // 2
            ac.wait_ge(zeroed, 8)
            ac.wait_ge(y_in, B + 1)

            def shifted(dst, y):
                act(dst[0:hp, :], y[0:hp, :], ACT.Copy)
                return act(dst[hp:P, 1:S], y[hp:P, 0:S - 1], ACT.Copy)

            def square(g, c):
                ac.wait_ge(pj_mm, g * 6 + c + 3)
                act(sq[:, c % 2], pj[:, c % 2], ACT.Square).then_inc(sq_ev, 1)

            def copy_v(g, t, c):
                ac.wait_ge(pj_mm, g * 6 + c + 1)
                act(Vt[:, t, c * S:(c + 1) * S], pj[:, c], ACT.Copy).then_inc(v_cp, 1)

            def take_qk_part(g, t, j):
                ac.wait_ge(qk_tr, g * 4 + j + 1)
                src = tr[:, j % 2].rearrange("p (a b) -> p a b", b=P)
                pr = slice(4 * (j % 2), 4 * (j % 2) + 4)
                dst = qT[:, pr, :] if j < 2 else kT[:, pr, WIN + t * P:WIN + (t + 1) * P]
                act(dst, src, ACT.Copy).then_inc(qk_cp, 1)

            def take_probs(g, j):
                ac.wait_ge(pt_tr, g * 4 + j + 1)
                if j == 0:
                    wait(ac, o_mm, g)
                h = 4 * ORDER[j]
                act(PT[:, h:h + 4, :], tr[:, j % 2].rearrange("p (a b) -> p a b", b=P), ACT.Copy
                    ).then_inc(pt_cp, 1)

            def gelu(m, k):
                w = CH[k][1]
                ac.wait_ge(w1_mm, m * FFC + k + 1)
                act(ge[0:w, k, :], pj[0:w, 0], ACT.Gelu, bias=lcur[0:w, 6 + k:7 + k]).then_inc(gelu_ev, 1)

            def slot(s_):
                n, t, new, c_, d_, m, lm = s_.args
                g = n * T + t
                g2 = g - 2
                if m is not None and t == 2:
                    y = YT[:, bass.ds(s_.ym * S, S)]
                    ac.wait_ge(y_att, m + 1)
                    apart(ac)
                    shifted(xsF, y).then_inc(xs_f, 1)
                if new:
                    if t == 0:
                        y = YT[:, bass.ds(s_.b * S, S)]
                        if not (isinstance(s_.l, int) and s_.l == 0):
                            ac.wait_ge(y_ff, n - B + 2)
                        wait(ac, pj_mm, n * (6 * T))
                        apart(ac)
                        shifted(xsA, y).then_inc(xs_a, 1)
                    wait(ac, o_mm, g - T + 1)
                    if t < T - 1:
                        wait(ac, ld_vp, ((n - 1) * (T - 1) + t + 1) * 16)
                    for c in range(2):
                        copy_v(g, t, c)
                    for c in range(2):
                        wait(ac, ss_ok, g * 4 + c - 1)
                        square(g, c)
                if d_:
                    take_probs(g2, 0)
                    take_probs(g2, 1)
                if new:
                    for c in range(2, 4):
                        ac.wait_ge(ss_ok, g * 4 + c - 1)
                        square(g, c)
                if d_:
                    take_probs(g2, 2)
                    take_probs(g2, 3)
                if new:
                    take_qk_part(g, t, 0)
                    take_qk_part(g, t, 1)
                if c_:
                    ac.wait_ge(t_sub, g)
                    wait(ac, bd_pool, g - 1)
                    act(Ex, Tm, ACT.Exp, scale=8.0).then_inc(e_exp, 1)
                if m is not None and t == 3:
                    gelu(m, 0)
                if d_:
                    t2 = (t - 2) % T
                    ac.wait_ge(o_mm, g2 + 1)
                    if t == 2:
                        wait(ac, wo_mm, n)
                    act(oT[:, :, t2 * P:(t2 + 1) * P], oo[:, :, :].rearrange("p u (a b) -> p (u a) b", b=P),
                        ACT.Copy).then_inc(o_cp, 1)
                if m is not None and t == 2:
                    ln_finish(LNB, LNB_BANKS[1], m, lcur[:, 0:1], lcur[:, 1:2], hT[:, :])
                if m is not None and t == 3:
                    gelu(m, 1)
                if new:
                    take_qk_part(g, t, 2)
                    take_qk_part(g, t, 3)
                if m is not None and t == 3:
                    gelu(m, 2)

            run_slots(ac, slot)

        @block.gpsimd
        def _(gp):
            p_ = nc.gpsimd
            ch = Chain(gp, pool_c)
            p_.memset(memz[:, :], 0.0).then_inc(zeroed, 1)
            p_.memset(lcol[:, :, :], 0.0).then_inc(zeroed, 1)
            ch.do(p_.memset(half_neg[:, :], -0.5))
            gp.wait_ge(ld_const, n_const)

            def power(sems, k):
                gp.wait_ge(sems[1], k + 1)
                p_.tensor_tensor(rstd[:, :], rstd[:, :], half_neg[:, 0:T], ALU.pow).then_inc(sems[2], 1)

            def attention(b, k):
                nh = (H0, H1)[k]
                hb = b * (H0 + H1) + k * H0
                ab = b * 2 + k
                gp.wait_ge(qk_ev, ab * 2 + 1)
                for h in range(nh):
                    if h >= 2:
                        gp.wait_ge(scores, (hb + h - 1) * T)
                    apart(gp)
                    p_.tensor_scalar(Qm[:, h % 2, :], qTs, hm[k][:, h:h + 1], 1.0, ALU.mult, ALU.mult
                                     ).then_inc(q_masked, 1)

            with gp.Fori(0, B) as b:
                power(LNA, b * 4)
                attention(b, 0)
                power(LNA, b * 4 + 1)
                power(LNA, b * 4 + 2)
                attention(b, 1)
                power(LNA, b * 4 + 3)

            gp.wait_ge(y_in, B + 1)
            for area in (Bd, kT[:, :, 0:WIN], Vp, PTp, xsA[:, 0:1], xsF[:, 0:1]):
                p_.memset(area, 0.0).then_inc(zeroed, 1)

            def normed(g, k):
                gp.wait_ge(ss_ok, g * 4 + 2 * k + 2)
                apart(gp)
                p_.tensor_scalar(rr[:, k, :], ss[:, k, :], 1e-24, 1.0, ALU.max, ALU.mult).then_inc(r_ok, 1)
                gp.wait_ge(r_ok, g * 2 + k + 1)
                p_.tensor_tensor(rr[:, k, :], rr[:, k, :], half_neg[:, 0:HL], ALU.pow)
                p_.tensor_tensor(ra[:, k, :], ra[:, k, :], rb[:, k, :], ALU.add).then_inc(sum_ok, 1)
                gp.wait_ge(sum_ok, g * 2 + k + 1)
                r3 = ra[:, k, :].rearrange("p (h d) -> p h d", d=DL)
                p_.tensor_tensor(r3, r3, rr[:, k, :].unsqueeze(2).broadcast_to([P, HL, DL]), ALU.mult
                                 ).then_inc(qk_rdy, 1)

            def slot(s_):
                n, t, new, c_, d_, m, lm = s_.args
                g = n * T + t
                if new:
                    normed(g, 0)
                    normed(g, 1)
                if m is not None and t == 2:
                    power(LNB, m)
                if c_:
                    g1 = g - 1
                    gp.wait_ge(ri_ok, g1 + 1)
                    wait(gp, pt_tr, g1 * 4)
                    gp.wait_ge(qk_rdy, g * 2 + 2 if new else NTILE * 2)
                    if m is not None and t == 2:
                        gp.wait_ge(lnb_rstd, m + 1)
                    for w in range(2, 4):
                        q = slice(w * WIN, (w + 1) * WIN)
                        last = p_.tensor_tensor(Bd[q, :, w * WIN:(w + 2) * WIN], Ex[q],
                                                ri[q].unsqueeze(2).broadcast_to([WIN, HL, 2 * WIN]), ALU.mult)
                        if w == 2:
                            last.then_inc(bd_half, 1)
                            gp.wait_ge(bd_half, g1 + 1)
                    last.then_inc(bd_pool, 1)
                    gp.wait_ge(bd_pool, g1 + 1)
                    apart(gp)

            run_slots(gp, slot)


_INS = ['L0_attn_x', 'L0_attn_w_qkv', 'L0_attn_b_qkv', 'L0_attn_w_out', 'L0_attn_b_out', 'L0_ffn_Wg',
        'L0_ffn_W1', 'L0_ffn_b1', 'L0_ffn_W2', 'L0_ffn_b2', 'L0_c', 'L0_wmod', 'L1_attn_Wq', 'L1_attn_Wk',
        'L1_attn_Wv', 'L1_attn_Wo', 'L1_attn_bo', 'L1_attn_betas', 'L1_attn_mem', 'L1_attn_z',
        'L1_ffn_Wqkv', 'L1_ffn_q_scale', 'L1_ffn_k_scale', 'L1_ffn_Wo', 'L1_ffn_ln_g', 'L1_ffn_ln_b',
        'L1_ffn_W1', 'L1_ffn_b1', 'L1_ffn_W2', 'L1_ffn_b2', 'L1_c', 'L1_wmod']


def kernel(**inputs):
    import concourse.bacc as _bacc
    from concourse.bass_utils import run_bass_kernel_spmd as _run

    nc = _bacc.Bacc("TRN2", target_bir_lowering=False, num_devices=1)
    arrays, aps = {}, {}
    for name, a in [(n, inputs[n]) for n in _INS] + list(shape_constants().items()):
        a = np.ascontiguousarray(a)
        arrays[f"in_{name}"] = a
        aps[name] = nc.dram_tensor(f"in_{name}", a.shape, mybir.dt.from_np(a.dtype), kind="ExternalInput").ap()
    out = nc.dram_tensor("out_x", (B, S, P), F32, kind="ExternalOutput").ap()
    build(nc, aps, out)
    r = _run(nc, [arrays], core_ids=[0])
    return r.results[0]["out_x"]
```

```python
import math
from contextlib import ExitStack

import numpy as np

import concourse.bass as bass
from concourse import mybir

F32 = mybir.dt.float32
F32R = mybir.dt.float32r
BF16 = mybir.dt.bfloat16
ALU = mybir.AluOpType
ACT = mybir.ActivationFunctionType
AX = mybir.AxisListType

P = 128
B = 4
S = 512
T = S // P
EPS = 1e-5
BIG = -1e30

H0, D0 = 16, 8
NE, FH = 8, 256
H1, D1 = 4, 32
DEPTH, HL, DL, WIN = 6, 16, 64, 32
INNER = HL * DL
PAIRS = HL // 2
DI = int(P * 4 * 2 / 3)
CH = [(0, P), (P, P), (2 * P, DI - 2 * P)]
FFC = len(CH)
GW = 32
G = P // GW
PADH = 32

NMOD = 12
SA, CA, GA, SB, CB, GB = range(6)


def shape_constants():
    f = np.float32
    p = np.arange(P)
    ident = np.eye(P, dtype=f)
    d = np.arange(S)[None, :] - (S - P + p)[:, None]
    alibi = np.where(d <= 0, d, BIG).astype(f)
    causal = np.where(d <= 0, 0.0, BIG).astype(f)
    hm = (p[:, None] % GW // D0 == np.arange(GW // D0)[None, :]).astype(f)
    i = (p % WIN)[:, None]
    j = np.arange(2 * WIN)[None, :]
    ok = (i <= j) & (j <= i + WIN)
    first = ok & ~((p[:, None] < WIN) & (j < WIN))
    wmask = np.stack([np.where(ok, 0.0, BIG), np.where(first, 0.0, BIG)], 1).astype(f)
    half = np.arange(0, DL, 2, dtype=f)
    inv_freq = f(1.0) / f(10000.0) ** (half / f(DL))
    t = np.arange(S, dtype=f)
    fr = t[:, None] * inv_freq[None, :]
    fr = np.concatenate([fr, fr], -1)
    base = (half + f(0.4 * DL)) / f(1.4 * DL)
    power = (t - S // 2) / f(WIN // 2)
    sc = base[None, :] ** power[:, None]
    sc = np.concatenate([sc, sc], -1)
    sign = np.where(np.arange(DL) < DL // 2, -1.0, 1.0).astype(f)
    c, s = np.cos(fr), np.sin(fr) * sign
    inv = f(1.0) / sc
    rot = np.stack([c * sc, s * sc, c * inv, s * inv], 0)
    rot = rot.reshape(4, T, P, DL).transpose(2, 0, 1, 3).astype(f)
    rev = np.broadcast_to(np.arange(NE, 0, -1, dtype=f), (P, T, NE))
    return {
        "ident": ident, "alibi": alibi, "causal": causal, "hm": hm,
        "wmask": wmask, "rot": np.ascontiguousarray(rot), "rev": np.ascontiguousarray(rev),
    }


class Chain:

    def __init__(self, eng, sem, base=0):
        self.eng, self.sem, self.base, self.n = eng, sem, base, 0

    def do(self, ins):
        self.mark(ins)
        self.settle()

    def mark(self, ins):
        ins.then_inc(self.sem, 1)
        self.n += 1

    def settle(self):
        self.eng.wait_ge(self.sem, self.base + self.n)


DVE_A = 64


def build(nc, ins, out):
    ctx = ExitStack()
    with ctx:
        def sb(name, shape, dt=F32):
            return ctx.enter_context(nc.sbuf_tensor(name, shape, dt))

        def sem(name):
            return ctx.enter_context(nc.semaphore(name))

        ident = sb("ident", [P, P])
        identb = sb("identb", [P, P], BF16)
        alibi = sb("alibi", [P, S])
        causal = sb("causal", [P, S])
        hm = sb("hm", [P, GW // D0])
        wmask = sb("wmask", [P, 2, 2 * WIN])
        wmaskb = sb("wmaskb", [P, 2, 2 * WIN], BF16)
        rot = sb("rot", [P, 4, T, DL])
        rev = sb("rev", [P, T, NE])
        half_neg = sb("half_neg", [P, 32])
        wT = sb("wT", [P, 8, P])
        bst = sb("bst", [P, 2, 2, G])
        bv = sb("bv", [P, P])
        bout = sb("bout", [P, 2])
        wg = sb("wg", [P, NE])
        mb1 = sb("mb1", [P, NE, 2])
        mb2 = sb("mb2", [NE, P])
        cT = sb("cT", [P, 2, B])
        cw = sb("cw", [P, 3, 2, B])
        modT = sb("modT", [P, B, NMOD])
        gsgn = sb("gsgn", [P, B, NMOD])
        gneg = sb("gneg", [P, B, NMOD])
        mcur = sb("mcur", [P, 2, NMOD])
        memz = sb("memz", [P, P + H1])
        beta = sb("beta", [P, 3, H1])
        wqkv = sb("wqkv", [P, 3 * INNER])
        wo = sb("wo", [P, PAIRS, P])
        w1 = sb("w1", [P, 2 * DI])
        w2 = sb("w2", [P, FFC, P])
        qks = sb("qks", [P, 2, DEPTH, DL])
        lcol = sb("lcol", [P, DEPTH, 9])
        lcur = sb("lcur", [P, 9])
        rtab = sb("rtab", [P, 4, T, DL])
        XT = sb("XT", [P, B * S])
        YT = sb("YT", [P, B * S])
        xcur = sb("xcur", [P, 2, S])
        hT = sb("hT", [P, 2, S])
        xn = sb("xn", [P, T, P])
        stats = sb("stats", [P, T, 6])
        mv = sb("mv", [P, T, 2])
        rstd = sb("rstd", [P, T])
        tmp = sb("tmp", [P, S])

        Qst = sb("Qst", [P, G, S], F32R)
        Kst = sb("Kst", [P, G, S], F32R)
        Qm = sb("Qm", [P, 2, S], F32R)

        ARENA = 27504
        arena = sb("arena", [P, ARENA])

        class Area:

            def __init__(self):
                self.at = 0

            def take(self, *shape, part=P):
                n = int(np.prod(shape))
                v = arena[0:part, self.at:self.at + n]
                self.at += n
                assert self.at <= ARENA, self.at
                if len(shape) == 2:
                    v = v.rearrange("p (a b) -> p a b", b=shape[1])
                if len(shape) == 3:
                    v = v.rearrange("p (a b c) -> p a b c", b=shape[1], c=shape[2])
                return v

        a = Area()
        xtok = a.take(T, P)
        mw1 = a.take(NE, FH)
        mw2 = a.take(NE, 2, P)
        wst = a.take(2 * 2 * G, P).rearrange("p (k j g) r -> p k j g r", k=2, j=2)
        qTs = a.take(S)
        Vh = a.take(T, H0, PADH)
        Ssb = a.take(4, S)
        Pr = a.take(4, S)
        PTh = a.take(2, T, S)
        nmax = a.take(H0 * T)
        rsum = a.take(H0, T)
        rinv = a.take(H0, T)
        OTs = a.take(S)
        Otok = a.take(T, P)
        Am = a.take(T, P)
        den = a.take(T, H1)
        oTs = a.take(S)
        sqT = a.take(S)
        eq_ = a.take(S)
        hes = a.take(2, 2, S)
        hsc = a.take(2, 2, S)
        setup = Area()
        setup.at = a.at - 8 * S
        wnat = setup.take(8, P)
        wmod = setup.take(2, 6 * P)
        rt = a.take(12, T * NE)
        rs4 = a.take(6, T)
        sT = a.take(S)

        a = Area()
        xsA, xsF, hB = tmp, xcur[:, 0, :], hT[:, 0, :]
        ra = a.take(2, INNER)
        rb = a.take(2, INNER)
        sq = a.take(2, S)
        ss = a.take(2, HL)
        rr = a.take(2, HL)
        Vt = a.take(T, INNER)
        qT = a.take(PAIRS, P)
        kT = a.take(PAIRS, WIN + S)
        Tm = a.take(HL, 2 * WIN)
        Ex = a.take(HL, 2 * WIN)
        mx = a.take(HL)
        sm = a.take(HL)
        ri = a.take(HL)
        ET = a.take(HL, 2, WIN)
        PT = a.take(HL, P)
        PTp = a.take(HL, WIN)
        oT = a.take(PAIRS, S)
        ge = a.take(FFC, S)
        fa = a.take(FFC, S)

        pj = ctx.enter_context(nc.psum_tensor("pj", [P, 2, S], F32))
        tr = ctx.enter_context(nc.psum_tensor("tr", [P, 2, S], F32))
        sc = ctx.enter_context(nc.psum_tensor("sc", [P, 2, S], F32))
        oo = ctx.enter_context(nc.psum_tensor("oo", [P, 2, S], F32))
        STACK = [pj[:, 0], pj[:, 1], tr[:, 0], tr[:, 1]]
        SBANK = [pj[:, 0], pj[:, 1], sc[:, 0]]
        TBANK = [tr[:, 0], tr[:, 1], sc[:, 1]]

        ld_const = sem("ld_const")
        ld_late = sem("ld_late")
        ld_x = sem("ld_x")
        ld_qkv, ld_wo, ld_ff = sem("ld_qkv"), sem("ld_wo"), sem("ld_ff")
        st_out = sem("st_out")
        dve_c, pool_c = sem("dve_c"), sem("pool_c")
        zeroed, passed = sem("zeroed"), sem("passed")
        set_tr = sem("set_tr")
        set_ev = sem("set_ev")
        silu_e, silu_d = sem("silu_e"), sem("silu_d")
        x_tr, x_in = sem("x_tr"), sem("x_in")
        mod_cur = sem("mod_cur")
        ln_in, ln_var, ln_rstd, ln_norm, ln_back, ln_out = (
            sem("ln_in"), sem("ln_var"), sem("ln_rstd"), sem("ln_norm"), sem("ln_back"), sem("ln_out"))
        qk_mm, qk_ev, v_mm, v_ev = sem("qk_mm"), sem("qk_ev"), sem("v_mm"), sem("v_ev")
        q_masked = sem("q_masked")
        st_mm, st_hi, st_lo = sem("st_mm"), sem("st_hi"), sem("st_lo")
        scores, biased, probs, p_tr, pe_dve, pe_act, pv_done = (
            sem("scores"), sem("biased"), sem("probs"), sem("p_tr"), sem("pe_dve"), sem("pe_act"),
            sem("pv_done"))
        o_copied, o_tr, o_tok = sem("o_copied"), sem("o_tr"), sem("o_tok")
        of_tr, of_ev, prj, x_add = sem("of_tr"), sem("of_ev"), sem("prj"), sem("x_add")
        elu_m, elu_e, elu_s, mem_mm, mixed = (
            sem("elu_m"), sem("elu_e"), sem("elu_s"), sem("mem_mm"), sem("mixed"))
        lg_mm, lg_sub, lg_exp, routed, s_tr, s_ev = (
            sem("lg_mm"), sem("lg_sub"), sem("lg_exp"), sem("routed"), sem("s_tr"), sem("s_ev"))
        m_h, m_relu, m_bc, m_sc, m_y = (
            sem("m_h"), sem("m_relu"), sem("m_bc"), sem("m_sc"), sem("m_y"))
        y_in = sem("y_in")
        xs_a, tabs = sem("xs_a"), sem("tabs")
        pj_mm, sq_ev, rot_ev, ss_ok, qk_rdy, v_cp = (
            sem("pj_mm"), sem("sq_ev"), sem("rot_ev"), sem("ss_ok"), sem("qk_rdy"), sem("v_cp"))
        qk_tr, qk_cp, sc_mm, t_sub, e_exp, ex_norm, et_ok, ri_ok = (
            sem("qk_tr"), sem("qk_cp"), sem("sc_mm"), sem("t_sub"), sem("e_exp"), sem("ex_norm"),
            sem("et_ok"), sem("ri_ok"))
        pt_cp, o_mm, o_cp, wo_mm, y_att, xs_f = (
            sem("pt_cp"), sem("o_mm"), sem("o_cp"), sem("wo_mm"), sem("y_att"), sem("xs_f"))
        w1_mm, gelu_ev, ff_ev, w2_mm, y_ff = (
            sem("w1_mm"), sem("gelu_ev"), sem("ff_ev"), sem("w2_mm"), sem("y_ff"))
        lnb_in, lnb_var, lnb_rstd, lnb_norm, lnb_back, lnb_out = (
            sem("lnb_in"), sem("lnb_var"), sem("lnb_rstd"), sem("lnb_norm"), sem("lnb_back"), sem("lnb_out"))
        wmask_ok = sem("wmask_ok")
        lc_ok = sem("lc_ok")
        x_fin, f_tr, f_cp = sem("x_fin"), sem("f_tr"), sem("f_cp")
        ln_bn, ln_ag, lnb_bn, lnb_ag = sem("ln_bn"), sem("ln_ag"), sem("lnb_bn"), sem("lnb_ag")
        mx_ok, sm_ok, r_ok, sum_ok = sem("mx_ok"), sem("sm_ok"), sem("r_ok"), sem("sum_ok")
        pow_ok = sem("pow_ok")
        LNA = (ln_in, ln_var, ln_rstd, ln_norm, ln_back, ln_out, ln_bn, ln_ag)
        LNB = (lnb_in, lnb_var, lnb_rstd, lnb_norm, lnb_back, lnb_out, lnb_bn, lnb_ag)
        LNA_BANKS = [(tr[:, 0], tr[:, 1]) if i in (0, 7) else (sc[:, 1], oo[:, 1]) if i in (3, 4)
                     else (oo[:, 0], oo[:, 1]) for i in range(8)]
        LN_COLS = ((CA, SA), (CB, SB), (6 + CA, 6 + SA), (6 + CB, 6 + SB))
        FFB = (sc, oo, pj)
        LNB_BANKS = (oo[:, 0], oo[:, 1])

        def wait(eng, s_, v_):
            if not (isinstance(v_, int) and v_ <= 0):
                eng.wait_ge(s_, v_)

        def apart(eng):
            eng.sem_inc(passed, 1)

        block = ctx.enter_context(nc.Block())
        N_CONST = []

        @block.sync
        def _(sp):
            def load(dst, src, late=0):
                sp.dma_start(dst, src, allow_slow_non_contiguous=True).then_inc((ld_const, ld_late)[late], 16)
                N_CONST.append(late)

            load(ident[:, :], ins["ident"])
            for k in range(2):
                load(cT[:, k, :], ins[f"L{k}_c"].rearrange("b k -> k b"))
            load(beta[:, 0, :], ins["L1_attn_betas"].rearrange("a h b c -> (a h b c)").partition_broadcast(P))
            load(wnat[:, 0:3, :], ins["L0_attn_w_qkv"].rearrange("(a n) k -> n a k", a=3))
            for k, n in enumerate(("L0_attn_w_out", "L1_attn_Wq", "L1_attn_Wk", "L1_attn_Wv", "L1_attn_Wo")):
                load(wnat[:, 3 + k, :], ins[n])
            for k in range(2):
                load(wmod[:, k, :], ins[f"L{k}_wmod"])
            sp.wait_ge(zeroed, 1)
            for j in range(2):
                for c in range(3):
                    load(bst[c * GW:(c + 1) * GW, 0, j, :],
                         ins["L0_attn_b_qkv"][j * P:(j + 1) * P].rearrange("(g r) -> r g", g=G))
            load(bv[:, :], ins["L0_attn_b_qkv"][2 * P:3 * P].partition_broadcast(P))
            load(bout[:, 0:1], ins["L0_attn_b_out"].unsqueeze(1))
            load(bout[:, 1:2], ins["L1_attn_bo"].unsqueeze(1))
            load(hm[:, :], ins["hm"])
            load(alibi[:, :], ins["alibi"])
            x_v = ins["L0_attn_x"].rearrange("b (t p) k -> b p t k", p=P)

            def load_x(b):
                sp.wait_ge(x_tr, b + 1)
                sp.dma_start(xtok, x_v[bass.ds(b, 1)].rearrange("a p t k -> (a p) t k")).then_inc(ld_x, 16)

            load_x(0)
            load(wg[:, :], ins["L0_ffn_Wg"], 1)
            load(mw1, ins["L0_ffn_W1"].rearrange("e k h -> k e h"), 1)
            load(mw2, ins["L0_ffn_W2"].rearrange("e (c k) n -> k e c n", c=2), 1)
            for c in range(2):
                load(mb1[:, :, c], ins["L0_ffn_b1"][:, c * P:(c + 1) * P].rearrange("e k -> k e"), 1)
            load(mb2[:, :], ins["L0_ffn_b2"], 1)
            load(rev[:, :, :], ins["rev"], 1)
            load_x(1)
            load(causal[:, :], ins["causal"], 1)
            sp.wait_ge(zeroed, 3)
            for h in range(H1):
                load(memz[h * D1:(h + 1) * D1, h * D1:(h + 1) * D1], ins["L1_attn_mem"][h], 1)
                load(memz[h * D1:(h + 1) * D1, P + h:P + h + 1], ins["L1_attn_z"][h], 1)
            load(wmask[:, :, :], ins["wmask"], 1)
            load(rot[:, :, :, :], ins["rot"], 1)
            load(qks[:, 0, :, :], ins["L1_ffn_q_scale"].partition_broadcast(P), 1)
            load(qks[:, 1, :, :], ins["L1_ffn_k_scale"].partition_broadcast(P), 1)
            for k, n in enumerate(("L1_ffn_ln_g", "L1_ffn_ln_b", "L1_ffn_b2")):
                load(lcol[:, :, k], ins[n].rearrange("l k -> k l"), 1)
            for k, (o, n) in enumerate(CH):
                for part_ in range(2):
                    load(lcol[0:n, :, 3 + 3 * part_ + k],
                         ins["L1_ffn_b1"][:, part_ * DI + o:part_ * DI + o + n].rearrange("l k -> k l"), 1)
            with sp.Fori(2, B) as b:
                load_x(b)
            w_v = ins["L1_ffn_Wo"].rearrange("l (p k) n -> l k p n", k=P)

            def qkv_weights(l):
                wait(sp, pj_mm, l * (6 * T * B))
                sp.dma_start(wqkv[:, :], ins["L1_ffn_Wqkv"][bass.ds(l, 1)].rearrange("a k n -> (a k) n")
                             ).then_inc(ld_qkv, 16)

            def other_weights(l):
                wait(sp, wo_mm, l * (2 * B))
                sp.dma_start(wo[:, :, :], w_v[bass.ds(l, 1)].rearrange("a k p n -> (a k) p n")
                             ).then_inc(ld_wo, 16)
                wait(sp, w2_mm, l * B)
                sp.dma_start(w1[:, :], ins["L1_ffn_W1"][bass.ds(l, 1)].rearrange("a k n -> (a k) n")
                             ).then_inc(ld_ff, 16)
                for k, (o, n) in enumerate(CH):
                    sp.dma_start(w2[0:n, k, :],
                                 ins["L1_ffn_W2"][bass.ds(l, 1), o:o + n, :].rearrange("a k n -> (a k) n")
                                 ).then_inc(ld_ff, 16)

            qkv_weights(0)
            other_weights(0)
            with sp.Fori(1, DEPTH) as l:
                qkv_weights(l)
                other_weights(l)
            out_v = out.rearrange("b (t p) k -> b p t k", p=P)
            with sp.Fori(0, B) as b:
                sp.wait_ge(f_cp, b + 1)
                sp.dma_start(out_v[bass.ds(b, 1)].rearrange("a p t k -> (a p) t k"), xn[:, :, :]
                             ).then_inc(st_out, 16)
            sp.wait_ge(st_out, 16 * B)

        n_const, n_late = 16 * N_CONST.count(0), 16 * N_CONST.count(1)
        NB = DEPTH * B
        NTILE = NB * T

        def places(p, k, u_):
            hb = p * 2 * (H0 + H1) + (2 * H0 * k + (H0, H1)[k] * u_)
            return (p * 2 + u_, hb, hb * T, p * 10 + (8 + u_ if k else 4 * u_), p * 4 + 2 * k + u_,
                    1 + u_ + 4 * k)

        class Slot:

            def __init__(self, n, t, l, b, m, lm=None, ym=None, new=True, c_=True, d_=True):
                self.args = (n, t, new, c_, d_, m, lm)
                self.l, self.b, self.ym = l, b, ym
                self.starts = new and t == 0 and isinstance(b, int)

        def run_slots(eng, slot):
            for t in range(T):
                slot(Slot(0, t, 0, 0, m=None, c_=t >= 1, d_=t >= 2))
            with eng.Fori(1, B) as b:
                for t in range(T):
                    slot(Slot(b, t, 0, b, m=b - 1, lm=0, ym=b - 1))
            with eng.Fori(1, DEPTH) as l:
                for t in range(T):
                    slot(Slot(l * B, t, l, 0, m=l * B - 1, lm=l - 1, ym=B - 1))
                with eng.Fori(1, B) as b:
                    for t in range(T):
                        slot(Slot(l * B + b, t, l, b, m=l * B + b - 1, lm=l, ym=b - 1))
            for t in range(T):
                slot(Slot(NB, t, DEPTH, 0, m=NB - 1, lm=DEPTH - 1, ym=B - 1, new=False, c_=t < 1, d_=t < 2))

        @block.tensor
        def _(pe):
            def mm(o, l, r, start=True, stop=True, **k):
                return nc.tensor.matmul(o, l, r, start=start, stop=stop, **k)

            def tp(o, i):
                return nc.tensor.transpose(o, i, ident[0:i.shape[0], 0:i.shape[0]])

            def norm_in(sems, bank, src):
                for t in range(T):
                    last = tp(bank[:, t * P:(t + 1) * P], src[:, t * P:(t + 1) * P])
                last.then_inc(sems[0], 1)

            def norm_back(sems, bank, k):
                pe.wait_ge(sems[3], k + 1)
                for t in range(T):
                    last = tp(bank[:, t * P:(t + 1) * P], xn[:, t, :])
                last.then_inc(sems[4], 1)

            def ln_in_(i):
                norm_in(LNA, LNA_BANKS[i][0], xcur[:, i % 2, :])

            def ln_back_(p, i):
                norm_back(LNA, LNA_BANKS[i][1], p * 8 + i)

            pe.wait_ge(ld_const, n_const)
            for g in range(2):
                for k in range(4):
                    last = tp(tr[:, g, k * P:(k + 1) * P], wnat[:, 4 * g + k, :])
                last.then_inc(set_tr, 1)
            pe.wait_ge(silu_d, 1)
            for k in range(2):
                for j in range(6):
                    last = mm(pj[:, 0, (6 * k + j) * B:(6 * k + j + 1) * B],
                              wmod[:, k, j * P:(j + 1) * P], cw[:, 2, k, :])
            last.then_inc(set_tr, 1)
            pe.wait_ge(set_ev, 3)

            def attention(p, k, u_):
                nh, wk = (H0, H1)[k], 4 * k
                b, hb, sbs, gb, ab, li = places(p, k, u_)
                h_ = hT[:, u_, :]
                pe.wait_ge(ln_out, p * 6 + 4 * k + u_ + 1)
                if k == 1:
                    mm(sc[:, 1], wT[:, wk, :], h_).then_inc(qk_mm, 1)
                for i in range(2 * G):
                    if i >= len(STACK):
                        pe.wait_ge(st_lo, ab * 2 * G + i - 3)
                    mm(STACK[i % 4], wst[:, k, i % 2, i // 2, :], h_).then_inc(st_mm, 1)
                    if i == 3:
                        for t in range(T):
                            last = mm(sc[:, 0, t * P:(t + 1) * P], h_[:, t * P:(t + 1) * P], wT[:, wk + 2, :])
                        last.then_inc(v_mm, 1)
                pe.wait_ge(st_lo, (ab + 1) * 2 * G)
                pe.wait_ge(v_ev, ab + 1)
                if k == 1:
                    pe.wait_ge(elu_s, b + 1)
                    for t in range(T):
                        last = mm(oo[:, t // 2, (t % 2) * (P + H1):(t % 2 + 1) * (P + H1)],
                                  sqT[:, t * P:(t + 1) * P], memz[:, :])
                    last.then_inc(mem_mm, 1)
                    pe.wait_ge(mixed, b * 2 + 1)

                def group_out(g):
                    pe.wait_ge(o_copied, gb + g + 1)
                    for t in range(T):
                        last = tp(oo[:, g % 2, t * P:(t + 1) * P], OTs[:, t * P:(t + 1) * P])
                    last.then_inc(o_tr, 1)

                def weigh(h):
                    g = h // 4
                    pe.wait_ge(pe_act, (hb + h) * 2 + 2)
                    pe.wait_ge(pe_dve, (hb + h) * 2 + 2)
                    if h % 4 == 0 and g >= 2:
                        pe.wait_ge(o_tok, gb + g - 1)
                    q = 32 * (h % 4)
                    for j in range(T):
                        last = mm(oo[q:q + 32, g % 2, j * P:S], Vh[:, j, h, :], PTh[:, h % 2, j, j * P:S],
                                  start=(j == 0), stop=(j == T - 1))
                    last.then_inc(pv_done, 1)
                    if h % 4 == 0 and g >= 1:
                        group_out(g - 1)

                ln_in_(li)
                for h in range(nh + 2):
                    if h == 2:
                        ln_back_(p, li)
                    if h == 4:
                        if li < 6:
                            pe.wait_ge(ln_out, p * 6 + li + 1)
                        else:
                            pe.wait_ge(y_in, b + 1)
                    if h < nh and k == 0:
                        pe.wait_ge(q_masked, b * H0 + h + 1)
                    for i in range(T):
                        if h < nh:
                            n = T * h + i
                            if n >= 3:
                                pe.wait_ge(biased, sbs + n - 2)
                            q_ = Qm[:, h % 2] if k == 0 else Qst[:, h]
                            mm(SBANK[n % 3][:, 0:(i + 1) * P], q_[:, i * P:(i + 1) * P],
                               Kst[:, h // (nh // G), 0:(i + 1) * P]).then_inc(scores, 1)
                        if 1 <= h <= nh:
                            n = T * (h - 1) + i
                            pe.wait_ge(probs, sbs + n + 1)
                            if n >= 3:
                                hh, ii = divmod(n - 3, T)
                                pe.wait_ge((pe_act, pe_dve)[ii % 2], (hb + hh) * 2 + ii // 2 + 1)
                            for j in range(i + 1):
                                last = tp(TBANK[n % 3][:, j * P:(j + 1) * P],
                                          Pr[:, n % 4, j * P:(j + 1) * P])
                            last.then_inc(p_tr, 1)
                        if i == 2 and h >= 2:
                            weigh(h - 2)
                group_out(nh // 4 - 1)
                pe.wait_ge(o_tok if k == 0 else mixed, gb + 4 if k == 0 else b * 2 + 2)
                for t in range(T):
                    last = tp(tr[:, 0, t * P:(t + 1) * P], Otok[:, t, :])
                last.then_inc(of_tr, 1)
                pe.wait_ge(of_ev, ab + 1)
                mm(pj[:, 0], wT[:, 4 * k + 3, :], oTs[:, :]).then_inc(prj, 1)
                pe.wait_ge(x_add, p * 6 + 4 * k + u_ + 1)

            def experts(p, u_):
                b, li = p * 2 + u_, 3 + u_
                h_ = hT[:, u_, :]
                pe.wait_ge(ln_out, p * 6 + 3 + u_)
                for t in range(T):
                    last = mm(tr[:, 0, t * NE:(t + 1) * NE], h_[:, t * P:(t + 1) * P], wg[:, :])
                last.then_inc(lg_mm, 1)

                def up(e):
                    for c in range(2):
                        if e >= 1:
                            pe.wait_ge(m_relu, (b * NE + e) * 2 - 1 + c)
                        mm(pj[:, c], mw1[:, e, c * P:(c + 1) * P], h_).then_inc(m_h, 1)

                def spread(e):
                    if e >= 2:
                        pe.wait_ge(m_sc, b * NE + e - 1)
                    for t in range(T):
                        w = rt[:, 11, t * NE + e:t * NE + e + 1].broadcast_to([P, P])
                        last = tp(tr[:, e % 2, t * P:(t + 1) * P], w)
                    last.then_inc(m_bc, 1)

                def down(e):
                    pe.wait_ge(m_sc, b * NE + e + 1)
                    for c in range(2):
                        last = mm(oo[:, 0], mw2[:, e, c, :], hsc[:, e % 2, c, :], start=False,
                                  stop=(e == NE - 1 and c == 1))
                    last.then_inc(m_y, 1)

                up(0)
                pe.wait_ge(routed, b + 1)
                for t in range(T):
                    last = tp(sc[0:NE, 0, t * P:(t + 1) * P], rt[:, 11, t * NE:(t + 1) * NE])
                last.then_inc(s_tr, 1)
                spread(0)
                pe.wait_ge(s_ev, b + 1)
                mm(oo[:, 0], mb2[:, :], sT[0:NE, :], stop=False)
                for e in range(1, NE):
                    if e == 2:
                        ln_in_(li)
                    if e == 4:
                        ln_back_(p, li)
                    up(e)
                    spread(e)
                    down(e - 1)
                down(NE - 1)
                pe.wait_ge(ln_out, p * 6 + li + 1)
                pe.wait_ge(x_add, p * 6 + 3 + u_)

            pe.sem_inc(x_tr, 1)
            with pe.Fori(0, B // 2) as p:
                for u_ in range(2):
                    pe.wait_ge(ld_x, p * 32 + (u_ + 1) * 16)
                    for t in range(T):
                        last = tp(tr[:, u_, t * P:(t + 1) * P], xtok[:, t, :])
                    last.then_inc(x_tr, 1)
                pe.wait_ge(x_in, p * 2 + 2)
                ln_in_(0)
                ln_back_(p, 0)
                for k in range(2):
                    attention(p, k, 0)
                    attention(p, k, 1)
                    if k == 0:
                        pe.wait_ge(ld_late, n_late)
                        experts(p, 0)
                        experts(p, 1)
                ln_in_(7)
                ln_back_(p, 7)
                pe.wait_ge(y_in, p * 2 + 3)

            def project(g, t, c):
                if c >= 4:
                    pe.wait_ge(rot_ev, g * 4 + c - 3)
                elif c >= 2:
                    pe.wait_ge(v_cp, g * 2 + c - 1)
                else:
                    wait(pe, rot_ev, g * 4)
                col = [4, 5, 0, 1, 2, 3][c] * S
                mm(pj[:, c % 2], xsA[:, t * P:(t + 1) * P], wqkv[:, col:col + S]).then_inc(pj_mm, 1)

            def turn(g, j):
                pe.wait_ge(qk_rdy, g * 2 + j // 2 + 1)
                wait(pe, qk_cp, g * 4 + j - 1)
                for u in range(4):
                    pr = 4 * (j % 2) + u
                    last = tp(tr[:, j % 2, u * P:(u + 1) * P], ra[:, j // 2, pr * P:(pr + 1) * P])
                last.then_inc(qk_tr, 1)

            def window_scores(g, t, u):
                pe.wait_ge(qk_cp, g * 4 + 4)
                wait(pe, t_sub, g)
                mm(sc[:, u].rearrange("p (a b) -> p a b", b=2 * WIN), identb[:, :],
                   wmaskb[:, 1 if t == 0 else 0, :].unsqueeze(1).broadcast_to([P, PAIRS, 2 * WIN]),
                   stop=False, skip_group_check=True)
                d = slice(u * DL, (u + 1) * DL)
                for pr in range(PAIRS):
                    for w in range(P // WIN):
                        last = mm(sc[w * WIN:(w + 1) * WIN, u, pr * 2 * WIN:(pr + 1) * 2 * WIN],
                                  qT[d, pr, w * WIN:(w + 1) * WIN],
                                  kT[d, pr, t * P + w * WIN:t * P + (w + 2) * WIN],
                                  start=False, stop=True, skip_group_check=True)
                last.then_inc(sc_mm, 1)

            def values(g, t):
                pe.wait_ge(pt_cp, g + 1)
                wait(pe, o_cp, g)
                for pr in range(PAIRS):
                    for u in range(2):
                        j, f = u * PAIRS + pr, (2 * pr + u) * DL
                        d = slice(u * DL, (u + 1) * DL)
                        c = (pr % 4) * P
                        last = mm(oo[d, pr // 4, c:c + P], Vt[:, t, f:f + DL], PT[:, j, :],
                                  start=True, stop=(t == 0), skip_group_check=True)
                        if t > 0:
                            last = mm(oo[d, pr // 4, c:c + WIN], Vt[:, t - 1, f:f + DL], PTp[:, j, :],
                                      start=False, stop=True, skip_group_check=True)
                last.then_inc(o_mm, 1)

            def ff_up(m, k):
                o, w = CH[k]
                mm(FFB[k][0:w, 0], w1[:, DI + o:DI + o + w], hB)
                mm(FFB[k][0:w, 1], w1[:, o:o + w], hB).then_inc(w1_mm, 1)

            def slot(s_):
                n, t, new, c_, d_, m, lm = s_.args
                g = n * T + t
                if new:
                    if s_.starts:
                        pe.wait_ge(ld_qkv, s_.l * 16 + 16)
                    if t == 0:
                        pe.wait_ge(xs_a, n + 1)
                    project(g, t, 0)
                    project(g, t, 1)
                if m is not None and t == 2:
                    pe.wait_ge(xs_f, m + 1)
                    wait(pe, o_cp, g - 2)
                    norm_in(LNB, LNB_BANKS[0], xsF)
                if new:
                    project(g, t, 2)
                if c_:
                    turn(g - 1, 2)
                if new:
                    project(g, t, 3)
                if c_:
                    turn(g - 1, 3)
                if m is not None and t == 3:
                    pe.wait_ge(o_cp, g - 2 if new else NTILE)
                    ff_up(m, 1)
                if new:
                    project(g, t, 4)
                if m is not None and t == 2:
                    norm_back(LNB, LNB_BANKS[1], m)
                if c_:
                    if m is not None and t == 3:
                        pe.wait_ge(ff_ev, m * FFC + 1)
                    window_scores(g - 1, (t - 1) % T, 0)
                if new:
                    project(g, t, 5)
                if c_:
                    window_scores(g - 1, (t - 1) % T, 1)
                if m is not None and t == 2:
                    pe.wait_ge(lnb_out, m + 1)
                if m is not None and t == 3:
                    pe.wait_ge(rot_ev, g * 4 + 4 if new else NTILE * 4)
                    ff_up(m, 2)
                if d_:
                    if m is not None and t == 0:
                        pe.wait_ge(y_ff, m + 1)
                    if m is not None and t == 1:
                        pe.wait_ge(y_att, m * 2 + 1)
                    if m is not None and t == 3:
                        pe.wait_ge(ff_ev, m * FFC + 2)
                    values(g - 2, (t - 2) % T)
                if new and t < 3:
                    turn(g, 0)
                    turn(g, 1)
                if m is not None and t < 2:
                    pe.wait_ge(o_cp, m * T + T - 1 + t)
                    if t == 0:
                        pe.wait_ge(ld_wo, lm * 16 + 16)
                    half = slice(t * (S // 2), (t + 1) * (S // 2))
                    for p_ in range(PAIRS):
                        last = mm(oo[:, 0, half], wo[:, p_, :], oT[:, p_, half], start=(p_ == 0),
                                  stop=(p_ == PAIRS - 1))
                    last.then_inc(wo_mm, 1)
                if m is not None and t == 2:
                    pe.wait_ge(t_sub, g if new else NTILE)
                    pe.wait_ge(ld_ff, lm * 64 + 64)
                    ff_up(m, 0)
                if new and t == 3:
                    turn(g, 0)
                    turn(g, 1)
                if m is not None and t == 3:
                    if d_:
                        pe.wait_ge(o_cp, g - 1)
                    for k, (o, w) in enumerate(CH):
                        pe.wait_ge(ff_ev, m * FFC + max(k + 1, 2))
                        last = mm(oo[:, 0], w2[0:w, k, :], fa[0:w, k, :], start=(k == 0), stop=(k == FFC - 1))
                    last.then_inc(w2_mm, 1)

            pe.wait_ge(wmask_ok, 1)
            run_slots(pe, slot)
            pe.wait_ge(y_ff, NB + 1)

            with pe.Fori(0, B) as b:
                pe.wait_ge(x_fin, b + 1)
                for t in range(T):
                    last = tp(tr[:, 0, t * P:(t + 1) * P], xcur[:, 0, t * P:(t + 1) * P])
                last.then_inc(f_tr, 1)
                pe.wait_ge(f_cp, b + 1)

        @block.vector
        def _(ve):
            v = nc.vector

            def ln_stats(sems, bank, k):
                ve.wait_ge(sems[0], k + 1)
                for t in range(T):
                    last = v.bn_stats(stats[:, t, :], bank[:, t * P:(t + 1) * P])
                last.then_inc(sems[6], 1)
                ve.wait_ge(sems[6], k + 1)
                apart(ve)
                for t in range(T):
                    last = v.bn_aggr(mv[:, t, :], stats[:, t, :])
                last.then_inc(sems[7], 1)
                ve.wait_ge(sems[7], k + 1)
                v.tensor_scalar(rstd[:, :], mv[:, :, 1], EPS, None, ALU.add).then_inc(sems[1], 1)

            def ln_apply(sems, bank, k):
                ve.wait_ge(sems[2], k + 1)
                for t in range(T):
                    last = v.tensor_scalar(xn[:, t, :], bank[:, t * P:(t + 1) * P], mv[:, t, 0:1],
                                           rstd[:, t:t + 1], ALU.subtract, ALU.mult)
                last.then_inc(sems[3], 1)

            def ln_first(p, i):
                ln_stats(LNA, LNA_BANKS[i][0], p * 8 + i)

            def ln_second(p, i):
                ln_apply(LNA, LNA_BANKS[i][0], p * 8 + i)

            ch = Chain(ve, dve_c)
            ve.wait_ge(ld_const, n_const)
            ch.do(v.tensor_copy(identb[:, :], ident[:, :]))
            ve.wait_ge(silu_e, 2)
            ch.do(v.tensor_scalar(cw[:, 1], cw[:, 0], 1.0, None, ALU.add))
            ch.do(v.reciprocal(cw[:, 0], cw[:, 1]))
            v.tensor_tensor(cw[:, 2], cw[:, 0], cT[:, :, :], ALU.mult).then_inc(silu_d, 1)
            ch.do(v.tensor_scalar(beta[:, 2, :], beta[:, 1, :], 1.0, None, ALU.add))
            ch.do(v.reciprocal(beta[:, 1, :], beta[:, 2, :]))
            ch.do(v.tensor_scalar(beta[:, 2, :], beta[:, 1, :], -1.0, 1.0, ALU.mult, ALU.add))
            for g in range(2):
                ve.wait_ge(set_tr, g + 1)
                v.tensor_copy(wT[:, 4 * g:4 * g + 4, :], tr[:, g].rearrange("p (a b) -> p a b", b=P)
                              ).then_inc(set_ev, 1)
            ve.wait_ge(set_ev, 2)
            v.memset(wst[:, :, :, :, 3 * GW:P], 0.0)
            for k in range(2):
                for j in range(2):
                    for c in range(3):
                        v.tensor_scalar(wst[:, k, j, :, c * GW:(c + 1) * GW],
                                        wT[:, 4 * k + j, :].rearrange("p (g r) -> p g r", r=GW),
                                        1 / math.sqrt(D0) if k == 0 and j == 0 else 1.0, None, ALU.mult)
            ch.do(v.tensor_scalar(bst[:, 0, 0, :], bst[:, 0, 0, :], 1 / math.sqrt(D0), None, ALU.mult))
            ve.wait_ge(set_tr, 3)
            v.tensor_copy(modT[:, :, :], pj[:, 0, 0:NMOD * B].rearrange("p (j b) -> p b j", b=B)
                          ).then_inc(set_ev, 1)
            ve.wait_ge(set_ev, 3)
            for j in (CA, CB, 6 + CA, 6 + CB):
                v.tensor_scalar(modT[:, :, j], modT[:, :, j], 1.0, None, ALU.add)
            for j in (GA, GB, 6 + GA, 6 + GB):
                ins_ = v.tensor_scalar(gsgn[:, :, j], modT[:, :, j], 0.0, 2.0, ALU.is_ge, ALU.mult)
            ch.do(ins_)
            for j in (GA, GB, 6 + GA, 6 + GB):
                ins_ = v.tensor_scalar(gneg[:, :, j], modT[:, :, j], -1.0, 0.25, ALU.mult, ALU.max)
            ch.do(ins_)
            for j in (GA, GB, 6 + GA, 6 + GB):
                ins_ = v.tensor_tensor(modT[:, :, j], modT[:, :, j], gneg[:, :, j], ALU.max)
            ch.do(ins_)
            for j in (GA, GB, 6 + GA, 6 + GB):
                ins_ = v.scalar_tensor_tensor(out=modT[:, :, j], in0=gsgn[:, :, j], scalar=-1.0,
                                              in1=modT[:, :, j], op0=ALU.add, op1=ALU.mult)
            ch.do(ins_)
            dve_setup = ch.n

            def attention(p, k, u_, ch):
                nh, d = (H0, H1)[k], (D0, D1)[k]
                b, hb, sbs, gb, ab, li = places(p, k, u_)
                xc = xcur[:, u_, :]
                bias = (alibi, causal)[k]
                if k == 0:
                    ch.do(v.memset(Vh[:, :, :, :], 0.0))

                def low(i):
                    g_, j = i // 2, i % 2
                    q = slice((j + 1) * GW, (j + 2) * GW)
                    dst = (Qst, Kst)[j][q, g_, :]
                    ve.wait_ge(st_hi, ab * 2 * G + i + 1)
                    v.scalar_tensor_tensor(out=dst, in0=STACK[i % 4][q], scalar=bst[q, k, j, g_:g_ + 1],
                                           in1=dst, op0=ALU.add, op1=ALU.subtract).then_inc(st_lo, 1)

                for i in range(5):
                    low(i)
                ve.wait_ge(v_mm, ab + 1)
                src = sc[:, 0].rearrange("p (t h d) -> p t h d", t=T, d=d)
                if k == 0:
                    for t in range(T):
                        ins_ = v.tensor_tensor(Vh[:, t, :, 0:d], src[:, t],
                                               bv[:, :].rearrange("p (h d) -> p h d", d=d), ALU.add)
                else:
                    ins_ = v.tensor_copy(Vh[:, :, 0:nh, :], src)
                ins_.then_inc(v_ev, 1)
                for i in range(5, 2 * G):
                    low(i)
                if k == 1:
                    ve.wait_ge(qk_ev, b + 1)
                    v.tensor_scalar(eq_, qTs, 0.0, None, ALU.min).then_inc(elu_m, 1)
                    ve.wait_ge(elu_e, b + 1)
                    v.scalar_tensor_tensor(out=sqT, in0=qTs, scalar=0.0, in1=eq_, op0=ALU.max,
                                           op1=ALU.add).then_inc(elu_s, 1)
                    ve.wait_ge(mem_mm, b + 1)
                    for t in range(T):
                        z = (t % 2) * (P + H1) + P
                        ins_ = v.tensor_scalar(den[:, t, :], oo[:, t // 2, z:z + H1], 1e-6, None, ALU.add)
                    ch.do(ins_)
                    ch.do(v.reciprocal(den, den))
                    ch.do(v.tensor_tensor(den, den, beta[:, 1, :].unsqueeze(1).broadcast_to([P, T, H1]),
                                          ALU.mult))
                    for t in range(T):
                        z = (t % 2) * (P + H1)
                        ins_ = v.tensor_tensor(
                            Am[:, t, :].rearrange("p (h d) -> p h d", d=D1),
                            oo[:, t // 2, z:z + P].rearrange("p (h d) -> p h d", d=D1),
                            den[:, t, :].unsqueeze(2).broadcast_to([P, H1, D1]), ALU.mult)
                    ins_.then_inc(mixed, 1)

                def group_out(g):
                    ve.wait_ge(o_tr, gb + g + 1)
                    ch.do(v.reciprocal(rinv[:, 4 * g:4 * g + 4, :], rsum[:, 4 * g:4 * g + 4, :]))
                    o = Otok.rearrange("p t (h d) -> p t h d", d=d)[:, :, 4 * g:4 * g + 4, :]
                    i_ = oo[:, g % 2].rearrange("p (t h d) -> p t h d", t=T, d=PADH)[:, :, :, 0:d]
                    for t in range(T):
                        last = v.tensor_tensor(o[:, t], i_[:, t], rinv[:, 4 * g:4 * g + 4, t].unsqueeze(2)
                                               .broadcast_to([P, 4, d]), ALU.mult)
                    last.then_inc(o_tok, 1)

                ln_first(p, li)
                for h in range(nh + 1):
                    if h == 2:
                        ln_second(p, li)
                    for i in range(T):
                        if h < nh:
                            n = T * h + i
                            ve.wait_ge(scores, sbs + n + 1)
                            if n >= 4:
                                ve.wait_ge(probs, sbs + n - 3)
                            apart(ve)
                            w = (i + 1) * P
                            v.tensor_tensor_reduce(out=Ssb[:, n % 4, 0:w], in0=SBANK[n % 3][:, 0:w],
                                                   in1=bias[:, S - w:S], scale=-1.0, scalar=3e38,
                                                   op0=ALU.add, op1=ALU.min,
                                                   accum_out=nmax[:, n:n + 1]).then_inc(biased, 1)
                        if h >= 1 and i % 2 == 1:
                            n = T * (h - 1) + i
                            ve.wait_ge(p_tr, sbs + n + 1)
                            if h >= 3:
                                ve.wait_ge(pv_done, hb + h - 2)
                            w = (i + 1) * P
                            v.tensor_copy(PTh[:, (h - 1) % 2, 0:i + 1, i * P:(i + 1) * P],
                                          TBANK[n % 3][:, 0:w].rearrange("p (a b) -> p a b", b=P)
                                          ).then_inc(pe_dve, 1)
                    if h >= 6 and (h - 2) % 4 == 0:
                        group_out((h - 2) // 4 - 1)
                group_out(nh // 4 - 1)
                if k == 1:
                    ve.wait_ge(o_tok, gb + 1)
                    for t in range(T):
                        ins_ = v.tensor_tensor(Otok[:, t, :].rearrange("p (h d) -> p h d", d=D1),
                                               Otok[:, t, :].rearrange("p (h d) -> p h d", d=D1),
                                               beta[:, 2, :].unsqueeze(2).broadcast_to([P, H1, D1]), ALU.mult)
                    ch.do(ins_)
                    v.tensor_tensor(Otok, Otok, Am, ALU.add).then_inc(mixed, 1)
                ve.wait_ge(prj, ab + 1)
                g_ = 6 * k + GA
                ch.do(v.tensor_scalar(tmp[:, :], pj[:, 0], bout[:, k:k + 1], mcur[:, u_, g_:g_ + 1],
                                      ALU.add, ALU.mult))
                v.tensor_tensor(xc, xc, tmp[:, :], ALU.add).then_inc(x_add, 1)
                if k == 1:
                    ve.wait_ge(x_add, p * 6 + 5 + u_)
                    ch.do(v.tensor_copy(XT[:, bass.ds(b * S, S)], xc))

            def experts(p, u_, ch):
                b, li = p * 2 + u_, 3 + u_
                xc = xcur[:, u_, :]
                R = [rt[:, k].rearrange("p (t e) -> p t e", e=NE) for k in range(12)]

                def wide(k):
                    return rs4[:, k].unsqueeze(2).broadcast_to([P, T, NE])

                ve.wait_ge(lg_mm, b + 1)
                lg = tr[:, 0, 0:T * NE].rearrange("p (t e) -> p t e", e=NE)
                ch.do(v.tensor_reduce(rs4[:, 0], lg, AX.X, ALU.max))
                v.tensor_tensor(R[0], lg, wide(0), ALU.subtract).then_inc(lg_sub, 1)
                ve.wait_ge(lg_exp, b + 1)
                ch.do(v.tensor_reduce(rs4[:, 1], R[1], AX.X, ALU.add))
                ch.do(v.reciprocal(rs4[:, 2], rs4[:, 1]))
                ch.do(v.tensor_tensor(R[2], R[1], wide(2), ALU.mult))

                def pick(src, m, eq, key, first, s):
                    ch.do(v.tensor_reduce(rs4[:, m], R[src], AX.X, ALU.max))
                    ch.do(v.tensor_tensor(R[eq], R[src], wide(m), ALU.is_equal))
                    ch.do(v.tensor_tensor(R[key], R[eq], rev[:, :, :], ALU.mult))
                    ch.do(v.tensor_reduce(rs4[:, s], R[key], AX.X, ALU.max))
                    ch.do(v.tensor_tensor(R[first], rev[:, :, :], wide(s), ALU.is_equal))

                pick(2, 3, 3, 4, 5, 0)
                ch.do(v.scalar_tensor_tensor(out=R[6], in0=R[5], scalar=-2.0, in1=R[2], op0=ALU.mult,
                                             op1=ALU.add))
                pick(6, 4, 7, 8, 9, 1)
                v.tensor_tensor(R[10], R[5], R[9], ALU.add)
                ch.do(v.tensor_tensor(rs4[:, 5], rs4[:, 3], rs4[:, 4], ALU.add))
                ch.do(v.reciprocal(rs4[:, 5], rs4[:, 5]))
                ch.do(v.tensor_tensor(R[10], R[10], R[2], ALU.mult))
                v.tensor_tensor(R[11], R[10], wide(5), ALU.mult).then_inc(routed, 1)
                ve.wait_ge(s_tr, b + 1)
                v.tensor_copy(sT[0:NE, :], sc[0:NE, 0, :]).then_inc(s_ev, 1)
                for e in range(NE):
                    if e == 2:
                        ln_first(p, li)
                    if e == 3:
                        ln_second(p, li)
                    ve.wait_ge(m_relu, (b * NE + e) * 2 + 2)
                    ve.wait_ge(m_bc, b * NE + e + 1)
                    if e >= 2:
                        ve.wait_ge(m_y, b * NE + e - 1)
                    v.tensor_tensor(hsc[:, e % 2], hes[:, e % 2],
                                    tr[:, e % 2].unsqueeze(1).broadcast_to([P, 2, S]),
                                    ALU.mult).then_inc(m_sc, 1)
                ve.wait_ge(m_y, b * NE + NE)
                ch.do(v.tensor_scalar(tmp[:, :], oo[:, 0], mcur[:, u_, GB:GB + 1], None, ALU.mult))
                v.tensor_tensor(xc, xc, tmp[:, :], ALU.add).then_inc(x_add, 1)

            with ve.Fori(0, B // 2) as p:
                ch = Chain(ve, dve_c, p * DVE_A + dve_setup)
                ve.wait_ge(y_in, p * 2 + 1)
                v.tensor_copy(mcur[:, :, :], modT[:, bass.ds(p * 2, 2), :]).then_inc(mod_cur, 1)
                ve.wait_ge(mod_cur, p + 1)
                for u_ in range(2):
                    ve.wait_ge(x_tr, p * 2 + u_ + 2)
                    v.tensor_copy(xcur[:, u_, :], tr[:, u_]).then_inc(x_in, 1)
                ln_first(p, 0)
                ln_second(p, 0)
                for k in range(2):
                    attention(p, k, 0, ch)
                    attention(p, k, 1, ch)
                    if k == 0:
                        ve.wait_ge(ld_late, n_late)
                        experts(p, 0, ch)
                        experts(p, 1, ch)
                ln_first(p, 7)
                ln_second(p, 7)
                assert ch.n == DVE_A, ("DVE_A", ch.n)

            def rotate(g, t, c):
                k, hf = c // 2, c % 2
                ve.wait_ge(sq_ev, g * 4 + c + 1)
                src = pj[:, c % 2].rearrange("p (h u d) -> p h u d", u=2, d=DL // 2)
                tc_ = rtab[:, 2 * k, t, :].rearrange("p (u d) -> p u d", u=2)
                ts_ = rtab[:, 2 * k + 1, t, :].rearrange("p (u d) -> p u d", u=2)
                wide = [P, PAIRS, 2, DL // 2]
                co = slice(hf * S, (hf + 1) * S)
                v.tensor_tensor(ra[:, k, co].rearrange("p (h u d) -> p h u d", u=2, d=DL // 2), src,
                                tc_.unsqueeze(1).broadcast_to(wide), ALU.mult)
                v.tensor_tensor(rb[:, k, co].rearrange("p (h u d) -> p h u d", u=2, d=DL // 2),
                                src[:, :, ::-1, :], ts_.unsqueeze(1).broadcast_to(wide), ALU.mult
                                ).then_inc(rot_ev, 1)

            def lengths(g, c):
                k, hf = c // 2, c % 2
                v.tensor_reduce(ss[:, k, hf * PAIRS:(hf + 1) * PAIRS],
                                sq[:, c % 2].rearrange("p (h d) -> p h d", d=DL), AX.X, ALU.add
                                ).then_inc(ss_ok, 1)

            def add(g, k):
                ve.wait_ge(rot_ev, g * 4 + 2 * k + 2)
                v.tensor_tensor(ra[:, k, :], ra[:, k, :], rb[:, k, :], ALU.add).then_inc(sum_ok, 1)

            def soft1(g):
                ve.wait_ge(sc_mm, g * 2 + 2)
                s_v = sc[:, :, :].rearrange("p u (a b) -> p (u a) b", b=2 * WIN)
                v.tensor_reduce(mx, s_v, AX.X, ALU.max).then_inc(mx_ok, 1)
                ve.wait_ge(mx_ok, g + 1)
                v.tensor_tensor(Tm, s_v, mx.unsqueeze(2).broadcast_to([P, HL, 2 * WIN]),
                                ALU.subtract).then_inc(t_sub, 1)

            def soft2(g, between=None):
                ve.wait_ge(e_exp, g + 1)
                v.tensor_reduce(sm, Ex, AX.X, ALU.add).then_inc(sm_ok, 1)
                ve.wait_ge(sm_ok, g + 1)
                v.reciprocal(ri, sm).then_inc(ri_ok, 1)
                ve.wait_ge(ri_ok, g + 1)
                v.tensor_tensor(Ex, Ex, ri.unsqueeze(2).broadcast_to([P, HL, 2 * WIN]), ALU.mult
                                ).then_inc(ex_norm, 1)
                if between is not None:
                    between()
                ve.wait_ge(ex_norm, g + 1)
                wait(ve, pt_cp, g)
                v.transpose(ET.rearrange("p h u q -> p (h u) q"),
                            Ex.rearrange("p h (u j) -> p (h u) j", u=2)).then_inc(et_ok, 1)

            def tables(l):
                for k in range(2):
                    qv = qks[:, k, bass.ds(l, 1), :]
                    v.tensor_tensor(rtab[:, 2 * k], rot[:, 2 * k], qv.broadcast_to([P, T, DL]), ALU.mult)
                    for u in range(2):
                        h_ = slice(u * DL // 2, (u + 1) * DL // 2)
                        o_ = slice((1 - u) * DL // 2, (2 - u) * DL // 2)
                        last = v.tensor_tensor(rtab[:, 2 * k + 1, :, h_], rot[:, 2 * k + 1, :, h_],
                                               qks[:, k, bass.ds(l, 1), o_].broadcast_to([P, T, DL // 2]),
                                               ALU.mult)
                last.then_inc(tabs, 1)
                ve.wait_ge(tabs, l + 1)
                apart(ve)

            def ff_gate(m, k):
                w = CH[k][1]
                ve.wait_ge(gelu_ev, m * FFC + k + 1)
                v.scalar_tensor_tensor(out=fa[0:w, k, :], in0=FFB[k][0:w, 1], scalar=lcur[0:w, 3 + k:4 + k],
                                       in1=ge[0:w, k, :], op0=ALU.add, op1=ALU.mult).then_inc(ff_ev, 1)

            def slot(s_):
                n, t, new, c_, d_, m, lm = s_.args
                g = n * T + t
                y = YT[:, bass.ds(s_.ym * S, S)] if m is not None else None
                if s_.starts:
                    tables(s_.l)
                if m is not None and t == 2:
                    v.tensor_copy(lcur[:, :].unsqueeze(1), lcol[:, bass.ds(lm, 1), :]).then_inc(lc_ok, 1)
                    ve.wait_ge(lc_ok, m + 1)
                    ln_stats(LNB, LNB_BANKS[0], m)
                if new:
                    wait(ve, qk_tr, g * 4 - 2)
                    rotate(g, t, 0)
                if m is not None and t == 2:
                    ln_apply(LNB, LNB_BANKS[0], m)
                if new:
                    lengths(g, 0)
                    rotate(g, t, 1)
                    lengths(g, 1)
                    add(g, 0)
                    wait(ve, qk_tr, g * 4)
                    rotate(g, t, 2)
                    lengths(g, 2)
                if m is not None and t == 3:
                    ff_gate(m, 1)
                if new:
                    rotate(g, t, 3)
                if c_:
                    soft1(g - 1)
                if new:
                    lengths(g, 3)
                    add(g, 1)

                def add_attention():
                    half = YT[:, bass.ds(s_.ym * S + t * (S // 2), S // 2)]
                    ve.wait_ge(wo_mm, m * 2 + t + 1)
                    apart(ve)
                    v.tensor_tensor(half, oo[:, 0, t * (S // 2):(t + 1) * (S // 2)], half, ALU.add
                                    ).then_inc(y_att, 1)

                between = None
                if m is not None and t == 1:
                    between = add_attention
                if m is not None and t == 3:
                    ff_gate(m, 2)
                if c_:
                    soft2(g - 1, between)
                elif between is not None:
                    between()
                if m is not None and t == 0:
                    add_attention()
                if m is not None and t == 2:
                    ff_gate(m, 0)
                if m is not None and t == 3:
                    ve.wait_ge(w2_mm, m + 1)
                    apart(ve)
                    v.scalar_tensor_tensor(out=y, in0=oo[:, 0], scalar=lcur[:, 2:3], in1=y,
                                           op0=ALU.add, op1=ALU.add).then_inc(y_ff, 1)

            v.tensor_copy(wmaskb[:, :, :], wmask[:, :, :]).then_inc(wmask_ok, 1)
            ve.sem_inc(y_ff, 1)
            run_slots(ve, slot)
            ve.wait_ge(y_ff, NB + 1)

            def finish(b):
                ch = Chain(ve, dve_c, b * 2 + dve_setup + B // 2 * DVE_A)
                wait(ve, f_tr, b)
                ch.do(v.tensor_copy(mcur[:, 0:1, :], modT[:, bass.ds(b, 1), :]))
                ch.do(v.tensor_scalar(tmp[:, :], YT[:, bass.ds(b * S, S)], mcur[:, 0, 6 + GB:7 + GB], None,
                                      ALU.mult))
                v.tensor_tensor(xcur[:, 0, :], XT[:, bass.ds(b * S, S)], tmp[:, :], ALU.add).then_inc(x_fin, 1)
                ve.wait_ge(f_tr, b + 1)
                wait(ve, st_out, b * 16)
                v.tensor_copy(xn[:, :, :], tr[:, 0].rearrange("p (a b) -> p a b", b=P)).then_inc(f_cp, 1)

            finish(0)
            with ve.Fori(1, B) as b:
                finish(b)

        @block.scalar
        def _(ac):
            def act(o, i, f, **k):
                return nc.scalar.activation(o, i, f, **k)

            ac.wait_ge(ld_const, n_const)
            act(cw[:, 0], cT[:, :, :], ACT.Exp, scale=-1.0).then_inc(silu_e, 1)
            act(beta[:, 1, :], beta[:, 0, :], ACT.Exp, scale=-1.0).then_inc(silu_e, 1)

            def ln_finish(sems, bank, k, scale, bias, dst):
                ac.wait_ge(sems[4], k + 1)
                act(dst, bank, ACT.Identity, scale=scale, bias=bias).then_inc(sems[5], 1)

            def norm_end(p, i):
                c_, s_ = LN_COLS[i // 2]
                u_ = i % 2
                k_ = dict(scale=mcur[:, u_, c_:c_ + 1], bias=mcur[:, u_, s_:s_ + 1])
                if i < 6:
                    ln_finish(LNA, LNA_BANKS[i][1], p * 8 + i, dst=hT[:, u_, :], **k_)
                else:
                    ac.wait_ge(ln_back, p * 8 + i + 1)
                    apart(ac)
                    act(YT[:, bass.ds(p * (2 * S) + u_ * S, S)], LNA_BANKS[i][1], ACT.Identity, **k_
                        ).then_inc(y_in, 1)

            def attention(p, k, u_):
                nh = (H0, H1)[k]
                b, hb, sbs, gb, ab, li = places(p, k, u_)
                if k == 1:
                    ac.wait_ge(qk_mm, b + 1)
                    act(qTs, sc[:, 1], ACT.Copy).then_inc(qk_ev, 1)
                for i in range(2 * G):
                    g_, j = i // 2, i % 2
                    ac.wait_ge(st_mm, ab * 2 * G + i + 1)
                    act((Qst, Kst)[j][:, g_, :], STACK[i % 4], ACT.Identity, bias=bst[:, k, j, g_:g_ + 1]
                        ).then_inc(st_hi, 1)
                if k == 1:
                    ac.wait_ge(elu_m, b + 1)
                    act(eq_, eq_, ACT.Exp).then_inc(elu_e, 1)

                def group_out(g):
                    ac.wait_ge(pv_done, hb + 4 * g + 4)
                    if g >= 1:
                        ac.wait_ge(o_tr, gb + g)
                    act(OTs, oo[:, g % 2], ACT.Copy).then_inc(o_copied, 1)

                for h in range(nh + 1):
                    for i in range(T):
                        if h < nh:
                            n = T * h + i
                            w = (i + 1) * P
                            ac.wait_ge(biased, sbs + n + 1)
                        if h >= 1 and i % 2 == 0:
                            m = T * (h - 1) + i
                            ac.wait_ge(p_tr, sbs + m + 1)
                            if h >= 3:
                                ac.wait_ge(pv_done, hb + h - 2)
                            ww = (i + 1) * P
                            act(PTh[:, (h - 1) % 2, 0:i + 1, i * P:(i + 1) * P],
                                TBANK[m % 3][:, 0:ww].rearrange("p (a b) -> p a b", b=P), ACT.Copy
                                ).then_inc(pe_act, 1)
                        if h < nh:
                            if n >= 4:
                                ac.wait_ge(p_tr, sbs + n - 3)
                            act(Pr[:, n % 4, 0:w], Ssb[:, n % 4, 0:w], ACT.Exp, scale=-1.0,
                                bias=nmax[:, n:n + 1], accum_out=rsum[:, h, i:i + 1]).then_inc(probs, 1)
                    if h == 2:
                        norm_end(p, li)
                    if h >= 4 and h % 4 == 1:
                        group_out(h // 4 - 1)
                group_out(nh // 4 - 1)
                ac.wait_ge(of_tr, ab + 1)
                act(oTs, tr[:, 0], ACT.Copy).then_inc(of_ev, 1)

            ac.sem_inc(y_in, 1)
            def experts(p, u_):
                b = p * 2 + u_
                ac.wait_ge(lg_sub, b + 1)
                act(rt[:, 1], rt[:, 0], ACT.Exp).then_inc(lg_exp, 1)
                for e in range(NE):
                    if e == 5:
                        norm_end(p, 3 + u_)
                    for c in range(2):
                        ac.wait_ge(m_h, (b * NE + e) * 2 + c + 1)
                        if e >= 2 and c == 0:
                            ac.wait_ge(m_sc, b * NE + e - 1)
                        act(hes[:, e % 2, c, :], pj[:, c], ACT.Relu, bias=mb1[:, e, c:c + 1]
                            ).then_inc(m_relu, 1)

            with ac.Fori(0, B // 2) as p:
                ac.wait_ge(mod_cur, p + 1)
                norm_end(p, 0)
                for k in range(2):
                    attention(p, k, 0)
                    attention(p, k, 1)
                    if k == 0:
                        ac.wait_ge(ld_late, n_late)
                        experts(p, 0)
                        experts(p, 1)
                norm_end(p, 7)

            hp = P // 2
            ac.wait_ge(zeroed, 8)
            ac.wait_ge(y_in, B + 1)

            def shifted(dst, y):
                act(dst[0:hp, :], y[0:hp, :], ACT.Copy)
                return act(dst[hp:P, 1:S], y[hp:P, 0:S - 1], ACT.Copy)

            def square(g, c):
                ac.wait_ge(pj_mm, g * 6 + c + 3)
                act(sq[:, c % 2], pj[:, c % 2], ACT.Square).then_inc(sq_ev, 1)

            def copy_v(g, t, c):
                ac.wait_ge(pj_mm, g * 6 + c + 1)
                act(Vt[:, t, c * S:(c + 1) * S], pj[:, c], ACT.Copy).then_inc(v_cp, 1)

            def take_qk_part(g, t, j):
                ac.wait_ge(qk_tr, g * 4 + j + 1)
                src = tr[:, j % 2].rearrange("p (a b) -> p a b", b=P)
                pr = slice(4 * (j % 2), 4 * (j % 2) + 4)
                dst = qT[:, pr, :] if j < 2 else kT[:, pr, WIN + t * P:WIN + (t + 1) * P]
                act(dst, src, ACT.Copy).then_inc(qk_cp, 1)

            def place(g, t, blocks):
                for k in blocks:
                    if k == 0:
                        ac.wait_ge(et_ok, g + 1)
                        wait(ac, o_mm, g)
                    u, w = 1 - k // 4, k % 4
                    q = slice(w * WIN, (w + 1) * WIN)
                    if k == 4 and t == 0:
                        continue
                    key = q if u else slice((w - 1) % 4 * WIN, (w - 1) % 4 * WIN + WIN)
                    dst = PTp[key] if k == 4 else PT[key, :, q]
                    last = act(dst, ET[q, :, u, :], ACT.Copy)
                    if k == 7:
                        last.then_inc(pt_cp, 1)

            def gelu(m, k):
                w = CH[k][1]
                ac.wait_ge(w1_mm, m * FFC + k + 1)
                act(ge[0:w, k, :], FFB[k][0:w, 0], ACT.Gelu, bias=lcur[0:w, 6 + k:7 + k]).then_inc(gelu_ev, 1)

            def slot(s_):
                n, t, new, c_, d_, m, lm = s_.args
                g, g2, t2 = n * T + t, n * T + t - 2, (t - 2) % T
                if m is not None and t == 2:
                    y = YT[:, bass.ds(s_.ym * S, S)]
                    ac.wait_ge(y_att, m * 2 + 2)
                    apart(ac)
                    shifted(xsF, y).then_inc(xs_f, 1)
                if new:
                    if t == 0:
                        y = YT[:, bass.ds(s_.b * S, S)]
                        if not (isinstance(s_.l, int) and s_.l == 0):
                            ac.wait_ge(y_ff, n - B + 2)
                        wait(ac, pj_mm, n * (6 * T))
                        apart(ac)
                        shifted(xsA, y).then_inc(xs_a, 1)
                    wait(ac, o_mm, g - T + 2)
                    for c in range(2):
                        copy_v(g, t, c)
                if new:
                    wait(ac, ss_ok, g * 4 - 1)
                    square(g, 0)
                if c_:
                    take_qk_part(g - 1, (t - 1) % T, 2)
                if new:
                    wait(ac, ss_ok, g * 4)
                    square(g, 1)
                if c_:
                    take_qk_part(g - 1, (t - 1) % T, 3)
                if m is not None and t == 3:
                    gelu(m, 1)
                if d_:
                    place(g2, t2, range(0, 3))
                if new:
                    ac.wait_ge(ss_ok, g * 4 + 1)
                    square(g, 2)
                if m is not None and t == 2:
                    ln_finish(LNB, LNB_BANKS[1], m, lcur[:, 0:1], lcur[:, 1:2], hB)
                if d_:
                    place(g2, t2, range(3, 6))
                if new:
                    ac.wait_ge(ss_ok, g * 4 + 2)
                    square(g, 3)
                if d_:
                    place(g2, t2, range(6, 8))
                if m is not None and t == 3:
                    gelu(m, 2)
                if c_ and not (t < 2):
                    ac.wait_ge(t_sub, g)
                    act(Ex, Tm, ACT.Exp, scale=8.0).then_inc(e_exp, 1)
                if d_:
                    ac.wait_ge(o_mm, g2 + 1)
                    if t == 2:
                        wait(ac, wo_mm, n * 2)
                    act(oT[:, :, t2 * P:(t2 + 1) * P], oo[:, :, :].rearrange("p u (a b) -> p (u a) b", b=P),
                        ACT.Copy).then_inc(o_cp, 1)
                if c_ and (t < 2):
                    ac.wait_ge(t_sub, g)
                    act(Ex, Tm, ACT.Exp, scale=8.0).then_inc(e_exp, 1)
                if m is not None and t == 2:
                    gelu(m, 0)
                if new:
                    take_qk_part(g, t, 0)
                    take_qk_part(g, t, 1)

            run_slots(ac, slot)

        @block.gpsimd
        def _(gp):
            p_ = nc.gpsimd
            ch = Chain(gp, pool_c)
            p_.memset(bst[:, :, :, :], 0.0).then_inc(zeroed, 1)
            p_.memset(memz[:, :], 0.0).then_inc(zeroed, 1)
            p_.memset(lcol[:, :, :], 0.0).then_inc(zeroed, 1)
            ch.do(p_.memset(half_neg[:, :], -0.5))
            gp.wait_ge(ld_const, n_const)

            def power(sems, k):
                gp.wait_ge(sems[1], k + 1)
                p_.tensor_tensor(rstd[:, :], rstd[:, :], half_neg[:, 0:T], ALU.pow).then_inc(sems[2], 1)

            def mask_heads(p, u_):
                b, hb, sbs, gb, ab, li = places(p, 0, u_)
                for h in range(H0):
                    if h == 2:
                        power(LNA, p * 8 + li)
                    g_ = h // (H0 // G)
                    gp.wait_ge(st_lo, ab * 2 * G + 2 * g_ + 1)
                    if h >= 2:
                        gp.wait_ge(scores, (hb + h - 1) * T)
                    apart(gp)
                    p_.tensor_scalar(Qm[:, h % 2, :], Qst[:, g_, :], hm[:, h % (H0 // G):h % (H0 // G) + 1],
                                     1.0, ALU.mult, ALU.mult).then_inc(q_masked, 1)

            with gp.Fori(0, B // 2) as p:
                power(LNA, p * 8)
                mask_heads(p, 0)
                mask_heads(p, 1)
                for i in range(3, 8):
                    power(LNA, p * 8 + i)

            gp.wait_ge(y_in, B + 1)
            for area in (PT, kT[:, :, 0:WIN], PTp, xsA[:, 0:1], xsF[:, 0:1]):
                p_.memset(area, 0.0).then_inc(zeroed, 1)

            def normed(g, k):
                gp.wait_ge(ss_ok, g * 4 + 2 * k + 2)
                apart(gp)
                p_.tensor_scalar(rr[:, k, :], ss[:, k, :], 1e-24, 1.0, ALU.max, ALU.mult).then_inc(r_ok, 1)
                gp.wait_ge(r_ok, g * 2 + k + 1)
                p_.tensor_tensor(rr[:, k, :], rr[:, k, :], half_neg[:, 0:HL], ALU.pow).then_inc(pow_ok, 1)
                gp.wait_ge(sum_ok, g * 2 + k + 1)
                gp.wait_ge(pow_ok, g * 2 + k + 1)
                r3 = ra[:, k, :].rearrange("p (h d) -> p h d", d=DL)
                p_.tensor_tensor(r3, r3, rr[:, k, :].unsqueeze(2).broadcast_to([P, HL, DL]), ALU.mult
                                 ).then_inc(qk_rdy, 1)

            def slot(s_):
                n, t, new, c_, d_, m, lm = s_.args
                g = n * T + t
                if m is not None and t == 2:
                    power(LNB, m)
                if new:
                    normed(g, 0)
                    normed(g, 1)

            run_slots(gp, slot)


_INS = ['L0_attn_x', 'L0_attn_w_qkv', 'L0_attn_b_qkv', 'L0_attn_w_out', 'L0_attn_b_out', 'L0_ffn_Wg',
        'L0_ffn_W1', 'L0_ffn_b1', 'L0_ffn_W2', 'L0_ffn_b2', 'L0_c', 'L0_wmod', 'L1_attn_Wq', 'L1_attn_Wk',
        'L1_attn_Wv', 'L1_attn_Wo', 'L1_attn_bo', 'L1_attn_betas', 'L1_attn_mem', 'L1_attn_z',
        'L1_ffn_Wqkv', 'L1_ffn_q_scale', 'L1_ffn_k_scale', 'L1_ffn_Wo', 'L1_ffn_ln_g', 'L1_ffn_ln_b',
        'L1_ffn_W1', 'L1_ffn_b1', 'L1_ffn_W2', 'L1_ffn_b2', 'L1_c', 'L1_wmod']


def kernel(**inputs):
    import concourse.bacc as _bacc
    from concourse.bass_utils import run_bass_kernel_spmd as _run

    nc = _bacc.Bacc("TRN2", target_bir_lowering=False, num_devices=1)
    arrays, aps = {}, {}
    for name, a in [(n, inputs[n]) for n in _INS] + list(shape_constants().items()):
        a = np.ascontiguousarray(a)
        arrays[f"in_{name}"] = a
        aps[name] = nc.dram_tensor(f"in_{name}", a.shape, mybir.dt.from_np(a.dtype), kind="ExternalInput").ap()
    out = nc.dram_tensor("out_x", (B, S, P), F32, kind="ExternalOutput").ap()
    build(nc, aps, out)
    r = _run(nc, [arrays], core_ids=[0])
    return r.results[0]["out_x"]
```
